# Optimizing a Trainium2 kernel written in Bass

```python
import numpy as np
import jax
import jax.numpy as jnp

def _softmax(x, axis=-1):
    return jax.nn.softmax(x, axis=axis)

def _gelu(x):
    return jax.nn.gelu(x, approximate=True)

def _silu(x):
    return jax.nn.silu(x)

def _sigmoid(x):
    return jax.nn.sigmoid(x)

def _layernorm(x, axis=-1, eps=1e-05):
    m = jnp.mean(x, axis=axis, keepdims=True)
    v = jnp.var(x, axis=axis, keepdims=True)
    return (x - m) / jnp.sqrt(v + eps)

def _scatter_add(tgt, idx, src, axis=0):
    return tgt.at[idx].add(src)

def _segment_sum(src, seg, n):
    return jax.ops.segment_sum(src, seg, n)
kernel_name = 'mk_vit_tower_d1_tok_img4096_r4_a9e5e8'

def setup_inputs(seed: int=0):
    np.random.seed(seed)
    _w = jnp.asarray

    def _rec_inputs():
        import jax
        import jax.numpy as jnp
        _rk = jax.random.key(seed)
        x = -0.0043416 + 0.998921 * jax.random.normal(jax.random.fold_in(_rk, 1), (32, 64, 64, 2), jnp.float32)
        return x
    x = _rec_inputs()

    def _L0_tok_setup():
        import jax, jax.numpy as jnp
        import numpy as np
        H, N, CH = (64, 64, 1)
        key = jax.random.key(seed)
        k1, k2, k3 = jax.random.split(key, 3)
        A_abslog = jnp.log(jax.random.uniform(k1, (H, N), dtype=jnp.float32, minval=0.5, maxval=0.999))
        A_phase = jax.random.uniform(k2, (H, N), dtype=jnp.float32, minval=-np.pi, maxval=np.pi)
        C = jax.random.normal(k3, (CH, H, N, 2), dtype=jnp.float32)
        return {'A_abslog': A_abslog, 'A_phase': A_phase, 'C': C, 'L': 1024}
    _L0_tok_all = _L0_tok_setup()
    _L0_tok_in = {k: v for k, v in _L0_tok_all.items() if k in ('A_abslog', 'A_phase')}
    del _L0_tok_all

    def _L0_attn_setup():
        import jax, jax.numpy as jnp
        import numpy as np
        B, N, HID = (1, 512, 1024)
        H, KVH, D, W = (32, 8, 128, 64)
        THETA = 10000.0
        GATE_NORM = 16.0

        def rope(x, pos):
            half = jnp.arange(D // 2, dtype=jnp.float32)
            inv = 1.0 / THETA ** (2.0 * half / D)
            fr = pos[:, None].astype(jnp.float32) * inv[None, :]
            emb = jnp.concatenate([fr, fr], axis=-1)
            cos, sin = (jnp.cos(emb)[None, None], jnp.sin(emb)[None, None])
            x1, x2 = jnp.split(x, 2, axis=-1)
            rot = jnp.concatenate([-x2, x1], axis=-1)
            return x * cos + rot * sin

        def gla_scan(q, k, v, g):
            qt, kt, vt, gt = (jnp.moveaxis(t, 2, 0) for t in (q, k, v, g))
            b, h = (q.shape[0], q.shape[1])
            S0 = jnp.zeros((b, h, D, D), jnp.float32)

            def step(S, x):
                q_t, k_t, v_t, g_t = x
                S = S * jnp.exp(g_t)[..., None] + k_t[..., None] * v_t[..., None, :]
                return (S, jnp.einsum('bhk,bhkv->bhv', q_t, S))
            _, o = jax.lax.scan(step, S0, (qt, kt, vt, gt))
            return jnp.moveaxis(o, 0, 2)

        def sliding_window_attn(q, k, v):
            b, h, n, d = q.shape
            nb = n // W
            qb = q.reshape(b, h, nb, W, d)

            def two_blocks(x):
                xb = x.reshape(b, h, nb, W, d)
                prev = jnp.concatenate([jnp.zeros_like(xb[:, :, :1]), xb[:, :, :-1]], axis=2)
                return jnp.concatenate([prev, xb], axis=3)
            kb, vb = (two_blocks(k), two_blocks(v))
            scores = jnp.einsum('bhnqd,bhnkd->bhnqk', qb, kb) / jnp.sqrt(jnp.float32(d))
            a = jnp.arange(W)[:, None]
            c = jnp.arange(2 * W)[None, :]
            rel = a + W - c
            base = (rel >= 0) & (rel <= W)
            blk = jnp.arange(nb)[:, None, None]
            keypos = (blk - 1) * W + c[None]
            mask = base[None] & (keypos >= 0)
            scores = jnp.where(mask[None, None], scores, -jnp.inf)
            p = jax.nn.softmax(scores, axis=-1)
            ob = jnp.einsum('bhnqk,bhnkd->bhnqd', p, vb)
            return ob.reshape(b, h, n, d)
        key = jax.random.key(seed)
        ks = jax.random.split(key, 5)
        s = 0.02
        return {'hidden_states': jax.random.normal(ks[0], (B, N, HID), jnp.float32), 'Wq': jax.random.normal(ks[1], (HID, H * D), jnp.float32) * s, 'Wk': jax.random.normal(ks[2], (HID, KVH * D), jnp.float32) * s, 'Wv': jax.random.normal(ks[3], (HID, KVH * D), jnp.float32) * s, 'Wo': jax.random.normal(ks[4], (H * D, HID), jnp.float32) * s}
    _L0_attn_all = _L0_attn_setup()
    _L0_attn_in = {k: v for k, v in _L0_attn_all.items() if k in ('Wq', 'Wk', 'Wv', 'Wo')}
    del _L0_attn_all

    def _L0_ffn_setup():
        import jax, jax.numpy as jnp
        import numpy as np
        B, S, D_IN, D_OUT = (2, 512, 1024, 1024)
        E, K, R = (8, 2, 16)
        SCALING = 32.0 / 16.0
        key = jax.random.key(seed)
        ks = jax.random.split(key, 6)
        x = jax.random.normal(ks[0], (B, S, D_IN), dtype=jnp.float32)
        gate_w = jax.random.normal(ks[1], (E, D_IN), dtype=jnp.float32) * 0.02
        base_w = jax.random.normal(ks[2], (D_OUT, D_IN), dtype=jnp.float32) * 0.02
        base_b = jax.random.normal(ks[3], (D_OUT,), dtype=jnp.float32) * 0.02
        lora_A = jax.random.normal(ks[4], (E, R, D_IN), dtype=jnp.float32) * 0.02
        lora_B = jax.random.normal(ks[5], (E, D_OUT, R), dtype=jnp.float32) * 0.02
        return {'x': x, 'gate_w': gate_w, 'base_w': base_w, 'base_b': base_b, 'lora_A': lora_A, 'lora_B': lora_B}
    _L0_ffn_all = _L0_ffn_setup()
    _L0_ffn_in = {k: v for k, v in _L0_ffn_all.items() if k in ('gate_w', 'base_w', 'base_b', 'lora_A', 'lora_B')}
    del _L0_ffn_all
    return {'x': x, 'L0_tok_A_abslog': _L0_tok_in['A_abslog'], 'L0_tok_A_phase': _L0_tok_in['A_phase'], 'L0_attn_Wq': _L0_attn_in['Wq'], 'L0_attn_Wk': _L0_attn_in['Wk'], 'L0_attn_Wv': _L0_attn_in['Wv'], 'L0_attn_Wo': _L0_attn_in['Wo'], 'L0_ffn_gate_w': _L0_ffn_in['gate_w'], 'L0_ffn_base_w': _L0_ffn_in['base_w'], 'L0_ffn_base_b': _L0_ffn_in['base_b'], 'L0_ffn_lora_A': _L0_ffn_in['lora_A'], 'L0_ffn_lora_B': _L0_ffn_in['lora_B']}

def reference(x, L0_tok_A_abslog, L0_tok_A_phase, L0_attn_Wq, L0_attn_Wk, L0_attn_Wv, L0_attn_Wo, L0_ffn_gate_w, L0_ffn_base_w, L0_ffn_base_b, L0_ffn_lora_A, L0_ffn_lora_B):
    import jax
    import jax.numpy as jnp

    def _L0_tok_ref(A_abslog, A_phase, C, L):
        import jax, jax.numpy as jnp
        import numpy as np
        H, N, CH = (64, 64, 1)
        A = jnp.exp(A_abslog + 1j * A_phase)
        dtA = jnp.log(A)
        Cc = C[..., 0] + 1j * C[..., 1]
        Cc = Cc * (A - 1.0) / dtA
        t = jnp.arange(L, dtype=jnp.float32)
        K = jnp.exp(dtA[:, :, None] * t)
        K = jnp.einsum('chn,hnl->chl', Cc, K)
        return 2.0 * K.real

    def _L0_attn_ref(hidden_states, Wq, Wk, Wv, Wo):
        import jax, jax.numpy as jnp
        import numpy as np
        B, N, HID = (1, 512, 1024)
        H, KVH, D, W = (32, 8, 128, 64)
        THETA = 10000.0
        GATE_NORM = 16.0

        def rope(x, pos):
            half = jnp.arange(D // 2, dtype=jnp.float32)
            inv = 1.0 / THETA ** (2.0 * half / D)
            fr = pos[:, None].astype(jnp.float32) * inv[None, :]
            emb = jnp.concatenate([fr, fr], axis=-1)
            cos, sin = (jnp.cos(emb)[None, None], jnp.sin(emb)[None, None])
            x1, x2 = jnp.split(x, 2, axis=-1)
            rot = jnp.concatenate([-x2, x1], axis=-1)
            return x * cos + rot * sin

        def gla_scan(q, k, v, g):
            qt, kt, vt, gt = (jnp.moveaxis(t, 2, 0) for t in (q, k, v, g))
            b, h = (q.shape[0], q.shape[1])
            S0 = jnp.zeros((b, h, D, D), jnp.float32)

            def step(S, x):
                q_t, k_t, v_t, g_t = x
                S = S * jnp.exp(g_t)[..., None] + k_t[..., None] * v_t[..., None, :]
                return (S, jnp.einsum('bhk,bhkv->bhv', q_t, S))
            _, o = jax.lax.scan(step, S0, (qt, kt, vt, gt))
            return jnp.moveaxis(o, 0, 2)

        def sliding_window_attn(q, k, v):
            b, h, n, d = q.shape
            nb = n // W
            qb = q.reshape(b, h, nb, W, d)

            def two_blocks(x):
                xb = x.reshape(b, h, nb, W, d)
                prev = jnp.concatenate([jnp.zeros_like(xb[:, :, :1]), xb[:, :, :-1]], axis=2)
                return jnp.concatenate([prev, xb], axis=3)
            kb, vb = (two_blocks(k), two_blocks(v))
            scores = jnp.einsum('bhnqd,bhnkd->bhnqk', qb, kb) / jnp.sqrt(jnp.float32(d))
            a = jnp.arange(W)[:, None]
            c = jnp.arange(2 * W)[None, :]
            rel = a + W - c
            base = (rel >= 0) & (rel <= W)
            blk = jnp.arange(nb)[:, None, None]
            keypos = (blk - 1) * W + c[None]
            mask = base[None] & (keypos >= 0)
            scores = jnp.where(mask[None, None], scores, -jnp.inf)
            p = jax.nn.softmax(scores, axis=-1)
            ob = jnp.einsum('bhnqk,bhnkd->bhnqd', p, vb)
            return ob.reshape(b, h, n, d)
        b, n, _ = hidden_states.shape
        grp = H // KVH
        q = hidden_states @ Wq
        k = hidden_states @ Wk
        v = hidden_states @ Wv
        g = k
        q = q.reshape(b, n, H, D).transpose(0, 2, 1, 3)
        k = k.reshape(b, n, KVH, D).transpose(0, 2, 1, 3)
        v = v.reshape(b, n, KVH, D).transpose(0, 2, 1, 3)
        g = g.reshape(b, n, KVH, D).transpose(0, 2, 1, 3)
        k = jnp.repeat(k, grp, axis=1)
        v = jnp.repeat(v, grp, axis=1)
        g = jnp.repeat(g, grp, axis=1)
        sq, sk, sv = (q, k, v)
        qs = jax.nn.softmax(q.astype(jnp.float32), axis=-1)
        ks_ = jax.nn.softmax(k.astype(jnp.float32), axis=-1)
        gs = jax.nn.log_sigmoid(g.astype(jnp.float32)) / GATE_NORM
        o_lin = gla_scan(qs, ks_, v.astype(jnp.float32), gs)
        pos = jnp.arange(n)
        sq = rope(sq, pos)
        sk = rope(sk, pos)
        y = sliding_window_attn(sq, sk, sv)
        o_ = 0.5 * y + 0.5 * o_lin
        o_ = o_.astype(jnp.bfloat16).astype(jnp.float32)
        o = o_.transpose(0, 2, 1, 3).reshape(b, n, H * D) @ Wo
        return o

    def _L0_ffn_ref(x, gate_w, base_w, base_b, lora_A, lora_B):
        import jax, jax.numpy as jnp
        import numpy as np
        B, S, D_IN, D_OUT = (2, 512, 1024, 1024)
        E, K, R = (8, 2, 16)
        SCALING = 32.0 / 16.0
        gate_logits = jnp.einsum('bsd,ed->bse', x, gate_w)
        weights, selected = jax.lax.top_k(gate_logits, K)
        weights = jax.nn.softmax(weights.astype(jnp.float32), axis=2).astype(x.dtype)
        result = jnp.einsum('bsd,od->bso', x, base_w) + base_b
        w_full = jnp.sum(jax.nn.one_hot(selected, E, dtype=x.dtype) * weights[..., None], axis=2)
        low = jnp.einsum('bsd,erd->ebsr', x, lora_A)
        lora_out = jnp.einsum('ebsr,eor,bse->bso', low, lora_B, w_full)
        result = result + SCALING * lora_out
        return result
    h = _L0_tok_ref(L0_tok_A_abslog, L0_tok_A_phase, x, 1024)
    h = h + _L0_attn_ref(_layernorm(h, axis=-1), L0_attn_Wq, L0_attn_Wk, L0_attn_Wv, L0_attn_Wo)
    h = h + _L0_ffn_ref(_layernorm(h, axis=-1), L0_ffn_gate_w, L0_ffn_base_w, L0_ffn_base_b, L0_ffn_lora_A, L0_ffn_lora_B)
    return h

_drawn_inputs = setup_inputs


def setup_inputs(seed=0):
    import zlib

    import numpy as np

    out = dict(_drawn_inputs(seed))
    spreads = {}
    factors = {'L0_ffn_base_b': 3.883}
    for name, (base, spread) in spreads.items():
        noise = np.random.default_rng([zlib.crc32(name.encode()), seed]).standard_normal(out[name].shape)
        drawn = base * np.exp(spread * noise) if base else spread * noise
        out[name] = jnp.asarray(drawn.astype(out[name].dtype))
    for name, factor in factors.items():
        out[name] = (out[name] * factor).astype(out[name].dtype)
    return out
```

```python
from contextlib import ExitStack

import numpy as np
import concourse.bass as bass
from concourse import mybir

F32 = mybir.dt.float32
F16 = mybir.dt.float16
BF16 = mybir.dt.bfloat16
ALU = mybir.AluOpType
ACT = mybir.ActivationFunctionType
X = mybir.AxisListType.X
ds = bass.ds

P = 128
BATCH, POS, NST = 32, 64, 64
HID = 1024
TOK = BATCH * POS
TILES = TOK // P
KC = HID // P
HEADS, KVH, DH = 32, 8, 128
GRP = HEADS // KVH
QW, KVW = GRP * DH, 2 * DH
GW = QW + KVW
STEPS = KVH * TILES
NE, RANK = 8, 16
ER = NE * RANK
AGW = ER + NE
WS = 64.0
SCORE = 1.0 / (WS * float(np.sqrt(DH)))
LORA_SCALE = 2.0
EPS = 1e-5
BIG = 1e30
NA_, NB_ = 4, 256
NB1 = 16
MUL = [NB_ * a for a in range(NA_)] + [NB1 * b for b in range(16)] + list(range(16))
A0, B10, B20, NM = 0, NA_, NA_ + 16, len(MUL)
MONE = B20 + 1
HC = 4
MAGIC = 12582912.0
PI = float(np.pi)
C1 = 6.28125
C2 = float(np.float32(2 * np.pi - C1))
C3 = float(np.float32(2 * np.pi - C1 - C2))


def constants():
    p = np.arange(P)
    pos, seq = p % POS, p // POS
    inv = (1.0 / (np.float32(10000.0) ** (2.0 * np.arange(DH // 2, dtype=np.float32) / np.float32(DH)))).astype(np.float32)
    fr = pos[:, None].astype(np.float32) * inv[None, :]
    causal = pos[:, None] >= np.arange(POS)[None, :]
    s, t = p[:, None], p[None, :]
    mid = POS // 2 - 1
    cum = ((s % POS <= t % POS) * 1.0 - (s % POS <= mid) * 1.0) * (s // POS == t // POS) / 16.0
    return {
        "ident": np.eye(P, dtype=np.float32),
        "rope": np.concatenate([np.cos(fr), np.sin(fr), -np.sin(fr)], axis=1).astype(np.float32),
        "masks": np.concatenate([np.where(causal, 0.0, -BIG), causal * 1.0], axis=1).astype(np.float32),
        "cum": cum.astype(np.float32),
        "mult": np.broadcast_to(np.array(MUL, np.float32), (P, NM)).copy(),
        "before": np.broadcast_to((np.arange(NE)[None, :] < np.arange(NE)[:, None]).astype(np.float32).reshape(1, NE * NE), (P, NE * NE)).copy(),
    }


def from_one(eng, sem, value):
    if isinstance(value, int) and value <= 0:
        return
    eng.wait_ge(sem, value)


def turns(t, par, each):
    return (t - par) * (each // 2) + each


def tokens_phase(nc, C, abslog, phase, k_ident, k_mult, h_dram):
    NCH = POS // HC
    with ExitStack() as ctx:
        sb = lambda name, shape, dt=F32: ctx.enter_context(nc.sbuf_tensor(name, shape, dt))
        pb = lambda name, shape, dt=F32: ctx.enter_context(nc.psum_tensor(name, shape, dt))
        sem = lambda name: ctx.enter_context(nc.semaphore(name))
        ident, mult = sb("t_ident", [P, P]), sb("t_mult", [P, NM])
        la_in, ph_in = sb("la_in", [POS, 2, NST]), sb("ph_in", [POS, 2, NST])
        lp = sb("lp", [P, 2, POS])
        cin = sb("cin", [P, 16, NST, 2])
        cdup = sb("cdup", [P, 16, 2, 2, NST])
        X1, X2 = sb("X1", [P, POS, BATCH]), sb("X2", [P, POS, BATCH])
        ang, rnd, cosr, sinr, dec = (sb(f"t_{x}", [P, POS, NM]) for x in ("ang", "rnd", "cosr", "sinr", "dec"))
        halfpi = sb("halfpi", [P, 1])
        sm = sb("t_sm", [P, 10, POS])
        e1 = sb("e1", [P, 4, POS, NA_])
        TF1, TF2 = sb("TF1", [P, POS, NA_]), sb("TF2", [P, POS, NA_])
        U, V = sb("t_U", [P, POS, 16]), sb("t_V", [P, POS, 16])
        E2a, E2b = sb("E2a", [P, 2, HC, 16, 16]), sb("E2b", [P, 2, HC, 16, 16])
        Ga, Gb = sb("Ga", [P, 2, HC, NA_, BATCH]), sb("Gb", [P, 2, HC, NA_, BATCH])
        hst = sb("hst", [P, 2, HC, NB_])
        pT = [pb(f"t_pT{i}", [P, 512]) for i in range(4)]
        pH = [pb(f"t_pH{i}", [P, 2, NB_]) for i in range(4)]

        consts_in, params_in, c_in = sem("t_consts_in"), sem("t_params_in"), sem("t_c_in")
        params_t, params_copied = sem("t_params_t"), sem("t_params_copied")
        c_t, c_copied1, c_copied2 = sem("t_c_t"), sem("t_c_copied1"), sem("t_c_copied2")
        c_split = sem("t_c_split")
        link, alink = sem("t_link"), sem("t_alink")
        angles, dec_arg, trig, dec_done = sem("t_angles"), sem("t_dec_arg"), sem("t_trig"), sem("t_dec_done")
        ga_tmp, g_ready, e_ready, h_done, h_copied, h_out0 = (sem("t_" + x) for x in
            ("ga_tmp", "g_ready", "e_ready", "h_done", "h_copied", "h_out0"))
        h_out = [h_out0, sem("t_h_out1")]
        block = ctx.enter_context(nc.Block())

        @block.sync
        def _(sp):
            sp.dma_start(ident[:], k_ident).then_inc(consts_in, 16)
            sp.dma_start(mult[:], k_mult).then_inc(consts_in, 16)
            for dup in range(2):
                sp.dma_start(la_in[:, dup, :], abslog).then_inc(params_in, 16)
                sp.dma_start(ph_in[:, dup, :], phase).then_inc(params_in, 16)
            sp.dma_start(cin[:].rearrange("p i n r -> p i (n r)"),
                         C.rearrange("c h n r -> (c h) (n r)").rearrange("(i p) m -> p i m", p=P)).then_inc(c_in, 16)
            hv = h_dram.rearrange("(c h) (a b) -> a c h b", h=POS, b=NB_)

            def store(k, par):
                sp.wait_ge(h_copied, 2 * (k + 1))
                for a in range(NA_):
                    sp.dma_start(hv[a, :, ds(k * HC, HC), :], hst[a * BATCH:(a + 1) * BATCH, par]).then_inc(h_out[par], 16)
            with sp.Fori(0, NCH // 2) as half:
                k = half * 2
                store(k, 0)
                store(k + 1, 1)
            for s in h_out:
                sp.wait_ge(s, 16 * NA_ * NCH // 2)

        @block.tensor
        def _(pe):
            pe.wait_ge(consts_in, 32)
            pe.wait_ge(params_in, 64)
            nc.tensor.transpose(pT[0][:, 0:POS], la_in[:].rearrange("p a n -> p (a n)"), ident[0:POS, 0:POS])
            nc.tensor.transpose(pT[0][:, POS:2 * POS], ph_in[:].rearrange("p a n -> p (a n)"),
                                ident[0:POS, 0:POS]).then_inc(params_t, 1)
            pe.wait_ge(c_split, 1)
            pe.wait_ge(params_copied, 1)
            for i in range(0, 16, 4):
                b = (i // 4) % 2
                if i >= 8:
                    pe.wait_ge(c_copied1, i // 4 - 1)
                    pe.wait_ge(c_copied2, i // 4 - 1)
                for r in range(2):
                    for j in range(4):
                        last = nc.tensor.transpose(pT[2 * b + r][:, j * P:(j + 1) * P],
                                                   cdup[:, i + j, r].rearrange("p d n -> p (d n)"), ident[:])
                last.then_inc(c_t, 1)

            def product(k, par):
                pe.wait_ge(g_ready, k + 1)
                pe.wait_ge(e_ready, k + 1)
                from_one(pe, h_copied, 2 * (k - 1))
                for j in range(HC):
                    o = pH[2 * par + j // 2][:, j % 2, :]
                    w = Ga[:, par, j].rearrange("p a c -> p (a c)")
                    nc.tensor.matmul(o, w, E2a[:, par, j].rearrange("p x y -> p (x y)"), start=True, stop=False)
                    last = nc.tensor.matmul(o, w, E2b[:, par, j].rearrange("p x y -> p (x y)"), start=False, stop=True)
                    if j % 2:
                        last.then_inc(h_done, 1)
            product(0, 0)
            product(1, 1)
            with pe.Fori(1, NCH // 2) as half:
                k = half * 2
                product(k, 0)
                product(k + 1, 1)

        @block.scalar
        def _(act):
            def step(i, ins):
                ins.then_inc(alink, 1)
                act.wait_ge(alink, i)
            act.wait_ge(c_in, 16)
            for r in range(2):
                last = nc.scalar.activation(cdup[:, :, r], cin[:, :, :, r].unsqueeze(2).broadcast_to([P, 16, 2, NST]), ACT.Copy)
            last.then_inc(c_split, 1)
            act.wait_ge(angles, 1)
            nc.scalar.activation(sinr[:], ang[:], ACT.Sin)
            step(1, nc.scalar.activation(cosr[:], ang[:], ACT.Abs))
            act.wait_ge(consts_in, 32)
            nc.scalar.activation(cosr[:], cosr[:], ACT.Sin, bias=halfpi[:], scale=-1.0).then_inc(trig, 1)
            act.wait_ge(dec_arg, 1)
            nc.scalar.activation(dec[:], dec[:], ACT.Exp).then_inc(dec_done, 1)
            for i in range(4):
                act.wait_ge(c_t, i + 1)
                src = pT[2 * (i % 2) + 1][:].rearrange("p (c h) -> p h c", h=POS)
                nc.scalar.activation(X2[:, :, 8 * i:8 * i + 8], src, ACT.Copy).then_inc(c_copied2, 1)

            def copy_out(k, par):
                if not isinstance(k, int) or k >= 2:
                    act.wait_ge(h_out[par], turns(k - 2, par, 16 * NA_))
                for j in range(2):
                    act.wait_ge(h_done, 2 * k + j + 1)
                    nc.scalar.activation(hst[:, par, 2 * j:2 * j + 2, :], pH[2 * par + j][:], ACT.Copy).then_inc(h_copied, 1)
            copy_out(0, 0)
            copy_out(1, 1)
            with act.Fori(1, NCH // 2) as half:
                k = half * 2
                copy_out(k, 0)
                copy_out(k + 1, 1)

        @block.vector
        def _(dve):
            count = [0]

            def step(ins):
                count[0] += 1
                ins.then_inc(link, 1)
                dve.wait_ge(link, count[0])
            v = nc.vector
            v.memset(halfpi[:], PI / 2)
            dve.wait_ge(params_t, 1)
            v.tensor_copy(lp[:], pT[0][:, 0:2 * POS].rearrange("p (k h) -> p k h", k=2)).then_inc(params_copied, 1)
            dve.wait_ge(params_copied, 1)
            dve.wait_ge(consts_in, 32)
            mb = mult[:].unsqueeze(1).broadcast_to([P, POS, NM])
            step(v.tensor_tensor(ang[:], lp[:, 1, :].unsqueeze(2).broadcast_to([P, POS, NM]), mb, ALU.mult))
            step(v.tensor_scalar(rnd[:], ang[:], 1.0 / (2 * PI), MAGIC, ALU.mult, ALU.add))
            step(v.tensor_scalar(rnd[:], rnd[:], MAGIC, None, ALU.subtract))
            fl = lambda t: t[:].rearrange("p h m -> p (h m)")
            for c in (C1, C2, C3):
                step(v.scalar_tensor_tensor(fl(ang), fl(rnd), -c, fl(ang), ALU.mult, ALU.add))
            v.tensor_scalar(ang[:], ang[:], PI, -PI, ALU.min, ALU.max).then_inc(angles, 1)
            v.tensor_tensor(dec[:], lp[:, 0, :].unsqueeze(2).broadcast_to([P, POS, NM]), mb, ALU.mult).then_inc(dec_arg, 1)
            for i in range(4):
                dve.wait_ge(c_t, i + 1)
                src = pT[2 * (i % 2)][:].rearrange("p (c h) -> p h c", h=POS)
                v.tensor_copy(X1[:, :, 8 * i:8 * i + 8], src).then_inc(c_copied1, 1)
            dve.wait_ge(trig, 1)
            dve.wait_ge(dec_done, 1)
            v.tensor_tensor(sinr[:], sinr[:], dec[:], ALU.mult)
            step(v.tensor_tensor(cosr[:], cosr[:], dec[:], ALU.mult))
            la, w = lp[:, 0, :], ang[:, :, MONE]
            ar, den, den2, n1, n2, n3, n4, fr, fi = (sm[:, i, :] for i in range(9))
            ai = sinr[:, :, MONE]
            v.tensor_scalar(ar, cosr[:, :, MONE], 1.0, None, ALU.subtract)
            v.tensor_tensor(den, la, la, ALU.mult)
            step(v.tensor_tensor(den2, w, w, ALU.mult))
            v.tensor_tensor(n1, ar, la, ALU.mult)
            v.tensor_tensor(n2, ai, w, ALU.mult)
            v.tensor_tensor(n3, ai, la, ALU.mult)
            v.tensor_tensor(n4, ar, w, ALU.mult)
            step(v.tensor_tensor(den, den, den2, ALU.add))
            step(v.reciprocal(den, den))
            v.tensor_tensor(n1, n1, n2, ALU.add)
            step(v.tensor_tensor(n3, n3, n4, ALU.subtract))
            v.scalar_tensor_tensor(fr, n1, 2.0, den, ALU.mult, ALU.mult)
            step(v.scalar_tensor_tensor(fi, n3, 2.0, den, ALU.mult, ALU.mult))
            frb, fib = (t.unsqueeze(2).broadcast_to([P, POS, NA_]) for t in (fr, fi))
            ca, sa = cosr[:, :, A0:A0 + NA_], sinr[:, :, A0:A0 + NA_]
            for i, (x, y) in enumerate(((frb, ca), (fib, sa), (frb, sa), (fib, ca))):
                last = v.tensor_tensor(e1[:, i], x, y, ALU.mult)
            step(last)
            v.tensor_tensor(e1[:, 0], e1[:, 0], e1[:, 1], ALU.subtract)
            step(v.tensor_tensor(e1[:, 2], e1[:, 2], e1[:, 3], ALU.add))
            lo, hi = slice(0, 64), slice(64, 128)
            v.tensor_copy(TF1[lo], e1[lo, 0])
            v.tensor_scalar(TF1[hi], e1[hi, 2], -1.0, None, ALU.mult)
            v.tensor_scalar(TF2[lo], e1[lo, 2], -1.0, None, ALU.mult)
            v.tensor_scalar(TF2[hi], e1[hi, 0], -1.0, None, ALU.mult)
            cb, sb_ = cosr[:, :, B10:B10 + 16], sinr[:, :, B10:B10 + 16]
            v.tensor_copy(U[lo], cb[lo])
            v.tensor_copy(U[hi], sb_[hi])
            v.tensor_scalar(V[lo], sb_[lo], -1.0, None, ALU.mult)
            step(v.tensor_copy(V[hi], cb[hi]))
            dve.wait_ge(c_copied2, 4)
            dve.wait_ge(c_copied1, 4)

            def build(k, par):
                from_one(dve, h_done, 2 * (k - 1))
                for j in range(HC):
                    h1 = ds(k * HC + j, 1)
                    f = lambda t: t[:, h1, :].rearrange("p o a -> p (o a)").unsqueeze(2).broadcast_to([P, NA_, BATCH])
                    c = lambda t: t[:, h1, :].broadcast_to([P, NA_, BATCH])
                    v.tensor_tensor(Ga[:, par, j], c(X1), f(TF1), ALU.mult)
                    last = v.tensor_tensor(Gb[:, par, j], c(X2), f(TF2), ALU.mult)
                last.then_inc(ga_tmp, 1)
                dve.wait_ge(ga_tmp, k + 1)
                v.tensor_tensor(Ga[:, par], Ga[:, par], Gb[:, par], ALU.add).then_inc(g_ready, 1)
                hs = ds(k * HC, HC)
                o = lambda t: t[:, hs, :].unsqueeze(3).broadcast_to([P, HC, 16, 16])
                i = lambda t: t[:, hs, B20:B20 + 16].unsqueeze(2).broadcast_to([P, HC, 16, 16])
                v.tensor_tensor(E2a[:, par], o(U), i(cosr), ALU.mult)
                v.tensor_tensor(E2b[:, par], o(V), i(sinr), ALU.mult).then_inc(e_ready, 1)
            build(0, 0)
            build(1, 1)
            with dve.Fori(1, NCH // 2) as half:
                k = half * 2
                build(k, 0)
                build(k + 1, 1)


def norm_phase(nc, xh, xl, h_dram, base_w, gate_w, lora_A, lora_B, k_ident, bt_dram, ag_dram, lb_dram):
    with ExitStack() as ctx:
        sb = lambda name, shape, dt=F32: ctx.enter_context(nc.sbuf_tensor(name, shape, dt))
        pb = lambda name, shape, dt=F32: ctx.enter_context(nc.psum_tensor(name, shape, dt))
        sem = lambda name: ctx.enter_context(nc.semaphore(name))
        ident, eps, carry = sb("n_ident", [P, P]), sb("n_eps", [P, 1]), sb("n_carry", [P, 1])
        ht, xn = sb("n_ht", [P, 2, HID]), sb("n_xn", [P, 2, HID])
        st, mv, sd, rs = sb("n_st", [P, 2, 2, 6]), sb("n_mv", [P, 2, 2]), sb("n_sd", [P, 2, 1]), sb("n_rs", [P, 2, 1])
        wt = sb("n_wt", [P, KC, HID])
        at, gt = sb("n_at", [P, HID]), sb("n_gt", [NE, HID])
        lbt = sb("n_lbt", [P, KC, NE, RANK])
        wo_hi, wo_lo = sb("n_whi", [P, 2, KC, P], F16), sb("n_wlo", [P, 2, KC, P], F16)
        tmp = sb("n_tmp", [P, KC, P])
        ag = sb("n_ag", [P, 2, KC, AGW], F16)
        agt = sb("n_agt", [P, KC, AGW])
        lb = sb("n_lb", [P, 2, HID], F16)
        pX = [pb(f"n_pX{i}", [P, 2, 4, P]) for i in range(2)]
        pW = [pb(f"n_pW{i}", [P, 2, 4, P]) for i in range(2)]
        consts_in, w_in, h_in = sem("n_consts_in"), sem("n_w_in"), [sem("n_h_in0"), sem("n_h_in1")]
        var_ready, sd_ready, rs_ready, xn_ready, stats = (sem("n_" + x) for x in ("var", "sd", "rs", "xn", "stats"))
        mv_ready = sem("n_mv_ready")
        x_t, hi_done, lo_done = sem("n_x_t"), sem("n_hi"), sem("n_lo")
        w_t, w_hi, w_lo = (sem("n_" + x) for x in ("w_t", "w_hi", "w_lo"))
        w_out = [sem("n_w_out0"), sem("n_w_out1")]
        NW = KC + 2
        block = ctx.enter_context(nc.Block())

        @block.sync
        def _(sp):
            sp.dma_start(ident[:], k_ident).then_inc(consts_in, 16)
            hv = h_dram.rearrange("(t p) n -> t p n", p=P)

            def load(t, par):
                from_one(sp, xn_ready, t - 1)
                sp.dma_start(ht[:, par, :], hv[ds(t, 1)].rearrange("o p n -> p (o n)")).then_inc(h_in[par], 16)
            load(0, 0)
            load(1, 1)
            with sp.Fori(1, TILES // 2) as half:
                t = half * 2
                load(t, 0)
                load(t + 1, 1)
            for s in w_out:
                sp.wait_ge(s, 16 * NW)

        @block.gpsimd
        def _(pool):
            pool.dma_start(wt[:], base_w.rearrange("(k p) n -> p k n", p=P)).then_inc(w_in, 16)
            pool.dma_start(at[:], lora_A.rearrange("e r n -> (e r) n")).then_inc(w_in, 16)
            pool.dma_start(gt[:], gate_w).then_inc(w_in, 16)
            for k in range(KC):
                pool.dma_start(lbt[:, k], lora_B[:, k * P:(k + 1) * P, :].rearrange("e p r -> p e r")).then_inc(w_in, 16)
            for k in range(NW):
                pool.wait_ge(w_lo, k + 1)
                for i, part in enumerate((wo_hi, wo_lo)):
                    if k < KC:
                        pool.dma_start(bt_dram[i, :, :, k * P:(k + 1) * P], part[:, k % 2]).then_inc(w_out[k % 2], 16)
                    elif k == KC:
                        pool.dma_start(ag_dram[i], ag[:, i]).then_inc(w_out[k % 2], 16)
                    else:
                        pool.dma_start(lb_dram[i], lb[:, i]).then_inc(w_out[k % 2], 16)

        @block.tensor
        def _(pe):
            pe.wait_ge(consts_in, 16)
            pe.wait_ge(w_in, 16 * (3 + KC))

            def weights(k):
                if k >= 2:
                    pe.wait_ge(w_lo, k - 1)
                for j in range(KC):
                    dst = pW[k % 2][:, j // 4, j % 4, :]
                    if k < KC:
                        last = nc.tensor.transpose(dst, wt[:, k, j * P:(j + 1) * P], ident[:])
                    elif k == KC:
                        last = nc.tensor.transpose(dst, at[:, j * P:(j + 1) * P], ident[:])
                    else:
                        last = nc.tensor.transpose(dst, lbt[:, j].rearrange("p e r -> p (e r)"), ident[:])
                last.then_inc(w_t, 1)
            for j in range(KC):
                nc.tensor.transpose(pX[0][:, j // 4, j % 4, 0:NE], gt[:, j * P:(j + 1) * P], ident[0:NE, 0:NE])
            for k in range(NW):
                weights(k)

            def tile(t, par):
                pe.wait_ge(xn_ready, t + 1)
                from_one(pe, hi_done, t - 1)
                from_one(pe, lo_done, t - 1)
                for j in range(KC):
                    last = nc.tensor.transpose(pX[par][:, j // 4, j % 4, :], xn[:, par, j * P:(j + 1) * P], ident[:])
                last.then_inc(x_t, 1)
            pe.wait_ge(w_lo, NW)
            tile(0, 0)
            tile(1, 1)
            with pe.Fori(1, TILES // 2) as half:
                t = half * 2
                tile(t, 0)
                tile(t + 1, 1)

        @block.scalar
        def _(act):
            for k in range(NW):
                act.wait_ge(w_t, k + 1)
                if k >= 2:
                    act.wait_ge(w_out[k % 2], 32 * (k // 2))
                if k >= 1:
                    act.wait_ge(w_lo, k)
                if k < KC:
                    nc.scalar.activation(wo_hi[:, k % 2].rearrange("p (x k) n -> p x k n", x=2), pW[k % 2][:], ACT.Copy, scale=WS).then_inc(w_hi, 1)
                elif k == KC:
                    nc.scalar.activation(ag[:, 0, :, 0:ER].rearrange("p (x k) n -> p x k n", x=2), pW[k % 2][:], ACT.Copy, scale=WS)
                    nc.scalar.activation(ag[:, 0, :, ER:AGW].rearrange("p (x k) n -> p x k n", x=2), pX[0][:, :, :, 0:NE], ACT.Copy, scale=WS).then_inc(w_hi, 1)
                else:
                    nc.scalar.activation(lb[:, 0, :], pW[k % 2][:].rearrange("p x k n -> p (x k n)"), ACT.Copy, scale=WS).then_inc(w_hi, 1)

            def root(t, par):
                act.wait_ge(var_ready, t + 1)
                nc.scalar.activation(sd[:, par, :], mv[:, par, 1:2], ACT.Sqrt, bias=eps[:]).then_inc(sd_ready, 1)

            def high(t, par):
                act.wait_ge(x_t, t + 1)
                nc.scalar.activation(xh[:, :, ds(t * P, P)].rearrange("p (x k) n -> p x k n", x=2), pX[par][:], ACT.Copy).then_inc(hi_done, 1)
            root(0, 0)
            root(1, 1)
            high(0, 0)
            with act.Fori(1, TILES // 2) as half:
                t = half * 2
                root(t, 0)
                high(t - 1, 1)
                root(t + 1, 1)
                high(t, 0)
            high(TILES - 1, 1)

        @block.vector
        def _(dve):
            v = nc.vector
            v.memset(eps[:], EPS)
            for k in range(NW):
                dve.wait_ge(w_hi, k + 1)
                if k < KC:
                    v.scalar_tensor_tensor(wo_lo[:, k % 2].rearrange("p k n -> p (k n)"), pW[k % 2][:].rearrange("p x k n -> p (x k n)"), WS,
                                           wo_hi[:, k % 2].rearrange("p k n -> p (k n)"), ALU.mult, ALU.subtract).then_inc(w_lo, 1)
                elif k == KC:
                    v.scalar_tensor_tensor(ag[:, 1, :, 0:ER], pW[k % 2][:].rearrange("p x k n -> p (x k) n"), WS, ag[:, 0, :, 0:ER], ALU.mult, ALU.subtract)
                    v.scalar_tensor_tensor(ag[:, 1, :, ER:AGW], pX[0][:].rearrange("p x k n -> p (x k) n")[:, :, 0:NE], WS, ag[:, 0, :, ER:AGW],
                                           ALU.mult, ALU.subtract).then_inc(w_lo, 1)
                else:
                    v.scalar_tensor_tensor(lb[:, 1, :], pW[k % 2][:].rearrange("p x k n -> p (x k n)"), WS, lb[:, 0, :],
                                           ALU.mult, ALU.subtract).then_inc(w_lo, 1)

            def moments(t, par):
                dve.wait_ge(h_in[par], turns(t, par, 16))
                for i in range(2):
                    last = v.bn_stats(st[:, par, i, :], ht[:, par, i * 512:(i + 1) * 512])
                last.then_inc(stats, 1)
                dve.wait_ge(stats, t + 1)
                v.memset(carry[:], 0.0)
                v.bn_aggr(mv[:, par, :], st[:, par]).then_inc(var_ready, 1)

            def normalise(t, par):
                dve.wait_ge(sd_ready, t + 1)
                v.reciprocal(rs[:, par, :], sd[:, par, :]).then_inc(rs_ready, 1)
                dve.wait_ge(rs_ready, t + 1)
                dve.wait_ge(var_ready, t + 1)
                from_one(dve, x_t, t - 1)
                v.tensor_scalar(xn[:, par, :], ht[:, par, :], mv[:, par, 0:1], rs[:, par, :], ALU.subtract, ALU.mult).then_inc(xn_ready, 1)

            def low(t, par):
                dve.wait_ge(hi_done, t + 1)
                dst = xl[:, :, ds(t * P, P)]
                v.tensor_tensor(dst.rearrange("p (x k) n -> p x k n", x=2), pX[par][:],
                                xh[:, :, ds(t * P, P)].rearrange("p (x k) n -> p x k n", x=2), ALU.subtract).then_inc(lo_done, 1)
            moments(0, 0)
            moments(1, 1)
            normalise(0, 0)
            normalise(1, 1)
            low(0, 0)
            with dve.Fori(1, TILES // 2) as half:
                t = half * 2
                moments(t, 0)
                normalise(t, 0)
                low(t - 1, 1)
                moments(t + 1, 1)
                normalise(t + 1, 1)
                low(t, 0)
            low(TILES - 1, 1)


def attention_phase(nc, xh, xl, Wq, Wk, Wv, Wo, k_ident, k_rope, k_masks, k_cum, ot_dram, wo_dram):
    with ExitStack() as ctx:
        sb = lambda name, shape, dt=F32: ctx.enter_context(nc.sbuf_tensor(name, shape, dt))
        pb = lambda name, shape, dt=F32: ctx.enter_context(nc.psum_tensor(name, shape, dt))
        sem = lambda name: ctx.enter_context(nc.semaphore(name))
        H2 = GRP // 2
        ident, rope = sb("ident", [P, P]), sb("rope", [P, 3, DH // 2])
        masks, cum = sb("masks", [P, 2, POS]), sb("cum", [P, P])
        Wg = sb("Wg", [P, 2, 2, KC, GW], F16)
        wst = sb("wst", [P, KC, GW])
        ost = sb("ost", [P, HID])
        oh, ol = sb("oh", [P, HID], F16), sb("ol", [P, HID], F16)
        K = sb("K", [P, 2, DH])
        Vz = sb("Vz", [P, 4, 2, DH])
        kabs, kexp, kln, gate = (sb(n, [P, 2, DH]) for n in ("kabs", "kexp", "kln", "gate"))
        eG, eGn = sb("eG", [P, 2, DH]), sb("eGn", [P, 2, DH])
        qmx, qnb, qsum, qrs = (sb(n, [P, 2, GRP]) for n in ("qmx", "qnb", "qsum", "qrs"))
        kmx, knb, ksum, krs = (sb(n, [P, 2, 1]) for n in ("kmx", "knb", "ksum", "krs"))
        smx, snb, ssum, srs = (sb(n, [P, 2, 4]) for n in ("smx", "snb", "ssum", "srs"))
        E, Ek = sb("E", [P, 2, GRP, DH]), sb("Ek", [P, 2, DH])
        t1, t2 = sb("t1", [P, GRP, 2, DH // 2]), sb("t2", [P, GRP, 2, DH // 2])
        kt1, kt2 = sb("kt1", [P, 2, DH // 2]), sb("kt2", [P, 2, DH // 2])
        QR, QD = sb("QR", [P, 2, GRP, DH]), sb("QD", [P, 2, GRP, DH])
        KR, KD = sb("KR", [P, 2, DH]), sb("KD", [P, 2, DH])
        QT, ET = sb("QT", [P, 2, GRP, POS]), sb("ET", [P, 2, GRP, POS])
        KT = sb("KT", [P, 2, P])
        S2, L, Es, PR = (sb(n, [P, 2, 4, POS]) for n in ("S2", "L", "Es", "PR"))
        PT = sb("PT", [P, 2, H2, P])
        OT = sb("OT", [P, 2, GRP, 2, POS], BF16)

        QP = [pb(f"QP{i}", [P, QW]) for i in range(2)]
        KVP = pb("KVP", [P, 512])
        TQ, TE = pb("TQ", [P, GRP, P]), pb("TE", [P, GRP, P])
        KG = pb("KG", [P, 4, P])
        SC = pb("SC", [P, 2, 4, POS])
        OP = pb("OP", [P, 2, GRP, POS])
        PTP = KVP[:, 256:512].rearrange("p (h n) -> p h n", h=H2)

        consts_in, w_in, w_scaled, w_ready, z_ready = (sem(n) for n in ("consts_in", "w_in", "w_scaled", "w_ready", "z_ready"))
        wo_in, wo_scaled, wo_ready, wo_out = (sem(n) for n in ("wo_in", "wo_scaled", "wo_ready", "wo_out"))
        kv_done, kv_copied, q_done = sem("kv_done"), sem("kv_copied"), sem("q_done")
        qmax_raw, qmax_ready, q_read, qexp_done, q_terms, q_roped, qrs_ready, q_decayed = (sem(n) for n in
            ("qmax_raw", "qmax_ready", "q_read", "qexp_done", "q_terms", "q_roped", "qrs_ready", "q_decayed"))
        kmax_raw, kmax_ready, kexp_done, k_terms, k_roped, krs_ready, k_decayed = (sem(n) for n in
            ("kmax_raw", "kmax_ready", "kexp_done", "k_terms", "k_roped", "krs_ready", "k_decayed"))
        kabs_done, knegexp_done, kln_done, gate_ready, G_done, eG_done = (sem(n) for n in
            ("kabs_done", "knegexp_done", "kln_done", "gate_ready", "G_done", "eG_done"))
        t_done, qt_copied, kt_copied = sem("t_done"), sem("qt_copied"), sem("kt_copied")
        sc_done, s_read, smax_raw, smax_ready, sexp_done, srs_ready, p_ready = (sem(n) for n in
            ("sc_done", "s_read", "smax_raw", "smax_ready", "sexp_done", "srs_ready", "p_ready"))
        pt_done, pt_copied, o_done, o_copied, o_out0 = (sem(n) for n in ("pt_done", "pt_copied", "o_done", "o_copied", "o_out0"))
        o_out = [o_out0, sem("o_out1")]
        block = ctx.enter_context(nc.Block())

        def steps(eng, a, b, c):
            def step(n, par):
                b0 = not isinstance(n, int) or 1 <= n <= STEPS
                c0 = not isinstance(n, int) or 2 <= n <= STEPS + 1
                a0 = not isinstance(n, int) or n < STEPS
                for name, k in eng_order:
                    if k == 0 and a0:
                        a[name](n, par)
                    if k == 1 and b0:
                        b[name](n - 1, (par + 3) % 4)
                    if k == 2 and c0:
                        c[name](n - 2, (par + 2) % 4)
            eng_order = a["order"]
            for n in range(4):
                step(n, n)
            with eng.Fori(1, STEPS // 4) as quad:
                n = quad * 4
                for i in range(4):
                    step(n + i, i)
            step(STEPS, 0)
            step(STEPS + 1, 1)

        @block.sync
        def _(sp):
            sp.dma_start(ident[:], k_ident).then_inc(consts_in, 16)
            sp.dma_start(rope[:].rearrange("p a b -> p (a b)"), k_rope).then_inc(consts_in, 16)
            sp.dma_start(masks[:].rearrange("p a b -> p (a b)"), k_masks).then_inc(consts_in, 16)
            sp.dma_start(cum[:], k_cum).then_inc(consts_in, 16)
            for g in range(KVH):
                from_one(sp, w_ready, g)
                rows = lambda W: W.rearrange("(c p) n -> p c n", p=P)
                sp.dma_start(wst[:, :, 0:QW], rows(Wq)[:, :, g * QW:(g + 1) * QW]).then_inc(w_in, 16)
                sp.dma_start(wst[:, :, QW:QW + DH], rows(Wk)[:, :, g * DH:(g + 1) * DH]).then_inc(w_in, 16)
                sp.dma_start(wst[:, :, QW + DH:GW], rows(Wv)[:, :, g * DH:(g + 1) * DH]).then_inc(w_in, 16)
                for j in range(HEADS // KVH):
                    i = g * (HEADS // KVH) + j
                    from_one(sp, wo_ready, i)
                    sp.dma_start(ost[:], Wo[i * P:(i + 1) * P, :]).then_inc(wo_in, 16)

        @block.gpsimd
        def _(pool):
            nc.gpsimd.memset(Vz[:], 0.0).then_inc(z_ready, 1)
            for g in range(KVH):
                pool.wait_ge(w_in, 48 * (g + 1))
                if g >= 2:
                    pool.wait_ge(q_done, TILES * (g - 1))
                if g >= 1:
                    pool.wait_ge(w_ready, g)
                nc.gpsimd.tensor_scalar(Wg[:, g % 2, 0], wst[:], WS, None, ALU.mult)
                pool.wait_ge(z_ready, 1)
                nc.gpsimd.tensor_scalar(wst[:], wst[:], WS, None, ALU.mult).then_inc(w_scaled, 1)
                pool.wait_ge(w_scaled, g + 1)
                nc.gpsimd.tensor_tensor(Wg[:, g % 2, 1], wst[:], Wg[:, g % 2, 0], ALU.subtract).then_inc(w_ready, 1)
                for j in range(HEADS // KVH):
                    i = g * (HEADS // KVH) + j
                    pool.wait_ge(wo_in, 16 * (i + 1))
                    from_one(pool, wo_out, 32 * i)
                    nc.gpsimd.tensor_scalar(oh[:], ost[:], WS, None, ALU.mult)
                    nc.gpsimd.tensor_scalar(ost[:], ost[:], WS, None, ALU.mult).then_inc(wo_scaled, 1)
                    pool.wait_ge(wo_scaled, i + 1)
                    nc.gpsimd.tensor_tensor(ol[:], ost[:], oh[:], ALU.subtract).then_inc(wo_ready, 1)
                    pool.wait_ge(wo_ready, i + 1)
                    pool.dma_start(wo_dram[0, :, i, :], oh[:]).then_inc(wo_out, 16)
                    pool.dma_start(wo_dram[1, :, i, :], ol[:]).then_inc(wo_out, 16)
            pool.wait_ge(wo_out, 32 * HEADS)

        @block.tensor
        def _(pe):
            mm = nc.tensor.matmul

            def project(out, n, cols, chunks):
                g = n // TILES
                tok = ds((n % TILES) * P, P)
                par = g % 2
                for c in chunks:
                    wv = [Wg[:, ds(par, 1), i, c, cols].rearrange("p o n -> p (o n)") for i in range(2)]
                    mm(out, xh[:, c, tok], wv[0], start=(c == 0), stop=False, skip_group_check=True)
                    mm(out, xh[:, c, tok], wv[1], start=False, stop=False, skip_group_check=True)
                    last = mm(out, xl[:, c, tok], wv[0], start=False, stop=(c == KC - 1), skip_group_check=True)
                return last

            def kv(n, s):
                pe.wait_ge(w_ready, n // TILES + 1)
                from_one(pe, kv_copied, n)
                project(KVP[:, 0:KVW], n, slice(QW, GW), range(KC)).then_inc(kv_done, 1)

            def transposes(n, s):
                p = s % 2
                pe.wait_ge(q_roped, n + 1)
                pe.wait_ge(q_decayed, n + 1)
                pe.wait_ge(k_roped, n + 1)
                pe.wait_ge(k_decayed, n + 1)
                from_one(pe, qt_copied, 2 * n)
                from_one(pe, kt_copied, n)
                for h in range(GRP):
                    nc.tensor.transpose(TQ[:, h, :], QR[:, p, h, :], ident[:])
                for h in range(GRP):
                    nc.tensor.transpose(TE[:, h, :], QD[:, p, h, :], ident[:])
                nc.tensor.transpose(KG[:, 1, :], KR[:, p, :], ident[:])
                nc.tensor.transpose(KG[:, 2, :], KD[:, p, :], ident[:]).then_inc(t_done, 1)

            def q_first(n, s):
                if not isinstance(n, int) or n >= 2:
                    pe.wait_ge(q_read, n - 1)
                    pe.wait_ge(qexp_done, n - 1)
                project(QP[s % 2][:], n, slice(0, QW), range(KC // 2))

            def q_last(n, s):
                project(QP[s % 2][:], n, slice(0, QW), range(KC // 2, KC)).then_inc(q_done, 1)

            def cumulate(n, s):
                pe.wait_ge(gate_ready, n + 1)
                from_one(pe, eG_done, n)
                from_one(pe, kt_copied, n)
                mm(KG[:, 0, :], cum[:], gate[:, s % 2, :], start=True, stop=True, skip_group_check=True).then_inc(G_done, 1)

            def scores(n, s):
                pe.wait_ge(qt_copied, 2 * (n + 1))
                pe.wait_ge(kt_copied, n + 1)
                from_one(pe, s_read, n)
                for kind, src in ((0, QT), (1, ET)):
                    for hp in range(H2):
                        for b in range(2):
                            last = mm(SC[:, kind, 2 * hp + b, :], src[:, b, 2 * hp:2 * hp + 2, :].rearrange("p h t -> p (h t)"),
                                      KT[:, kind, b * POS:(b + 1) * POS], start=True, stop=True, skip_group_check=True)
                last.then_inc(sc_done, 1)

            def p_transpose(n, s):
                pe.wait_ge(p_ready, n + 1)
                pe.wait_ge(kv_copied, n + 3 if not isinstance(n, int) else min(n + 3, STEPS))
                from_one(pe, pt_copied, n)
                for hp in range(H2):
                    last = nc.tensor.transpose(PTP[:, hp, :], PR[:, s % 2, 2 * hp:2 * hp + 2, :].rearrange("p b t -> p (b t)"), ident[:])
                last.then_inc(pt_done, 1)

            def values(n, s):
                pe.wait_ge(pt_copied, n + 1)
                pe.wait_ge(kv_copied, n + 1)
                from_one(pe, o_copied, n)
                for b in range(2):
                    last = mm(OP[:, b].rearrange("p h t -> p (h t)"), Vz[:, s, b, :], PT[:, s % 2].rearrange("p h n -> p (h n)"),
                              start=True, stop=True, skip_group_check=True)
                last.then_inc(o_done, 1)

            pe.wait_ge(consts_in, 64)
            order = [("kv", 0), ("t", 1), ("qa", 0), ("G", 0), ("pt", 2), ("qb", 0), ("v", 2), ("s", 1)]
            steps(pe, {"order": order, "kv": kv, "qa": q_first, "G": cumulate, "qb": q_last},
                  {"t": transposes, "s": scores}, {"pt": p_transpose, "v": values})

        @block.scalar
        def _(act):
            a = nc.scalar.activation

            def q_exp(n, s):
                p = s % 2
                act.wait_ge(q_done, n + 1)
                act.wait_ge(qmax_ready, n + 1)
                from_one(act, q_decayed, n - 1)
                for h in range(GRP):
                    last = a(E[:, p, h, :], QP[p][:, h * DH:(h + 1) * DH], ACT.Exp, bias=qnb[:, p, h:h + 1], scale=1.0 / WS,
                             accum_out=qsum[:, p, h:h + 1])
                last.then_inc(qexp_done, 1)

            def s_exp(n, s):
                p = s % 2
                act.wait_ge(smax_ready, n + 1)
                from_one(act, p_ready, n - 1)
                for j in range(4):
                    last = a(Es[:, p, j, :], S2[:, p, j, :], ACT.Exp, bias=snb[:, p, j:j + 1], scale=SCORE, accum_out=ssum[:, p, j:j + 1])
                last.then_inc(sexp_done, 1)

            def kv_copy(n, s):
                p = s % 2
                act.wait_ge(kv_done, n + 1)
                if not isinstance(n, int) or n >= 2:
                    act.wait_ge(k_roped, n - 1)
                    act.wait_ge(gate_ready, n - 1)
                if not isinstance(n, int) or n >= 4:
                    act.wait_ge(o_done, n - 3)
                a(K[:, p, :], KVP[:, 0:DH], ACT.Copy, scale=1.0 / WS)
                for b in range(2):
                    r = slice(b * POS, (b + 1) * POS)
                    last = a(Vz[r, s, b, :], KVP[r, DH:2 * DH], ACT.Copy, scale=1.0 / WS)
                last.then_inc(kv_copied, 1)

            def gates(n, s):
                p = s % 2
                act.wait_ge(kv_copied, n + 1)
                a(kabs[:, p, :], K[:, p, :], ACT.Abs).then_inc(kabs_done, 1)
                act.wait_ge(kabs_done, n + 1)
                a(kexp[:, p, :], kabs[:, p, :], ACT.Exp, scale=-1.0).then_inc(knegexp_done, 1)
                act.wait_ge(knegexp_done, n + 1)
                a(kln[:, p, :], kexp[:, p, :], ACT.Ln, bias=1.0).then_inc(kln_done, 1)
                act.wait_ge(kmax_ready, n + 1)
                from_one(act, k_decayed, n - 1)
                a(Ek[:, p, :], K[:, p, :], ACT.Exp, bias=knb[:, p, :], accum_out=ksum[:, p, :]).then_inc(kexp_done, 1)

            def t_copy(n, s):
                act.wait_ge(t_done, n + 1)
                from_one(act, sc_done, n)
                for src, dst in ((TQ, QT), (TE, ET)):
                    a(dst[:].rearrange("p b h t -> p h b t"), src[:].rearrange("p h (b t) -> p h b t", b=2), ACT.Copy).then_inc(qt_copied, 1)

            def decays(n, s):
                p = s % 2
                act.wait_ge(G_done, n + 1)
                if not isinstance(n, int) or n >= 2:
                    act.wait_ge(q_decayed, n - 1)
                    act.wait_ge(k_decayed, n - 1)
                a(eG[:, p, :], KG[:, 0, :], ACT.Exp)
                a(eGn[:, p, :], KG[:, 0, :], ACT.Exp, scale=-1.0).then_inc(eG_done, 1)

            def o_copy(n, s):
                act.wait_ge(o_done, n + 1)
                if not isinstance(n, int) or n >= 2:
                    act.wait_ge(o_out[s % 2], turns(n - 2, s % 2, 16))
                a(OT[:, s % 2].rearrange("p h b t -> p b h t"), OP[:], ACT.Copy, scale=0.5).then_inc(o_copied, 1)
                act.wait_ge(o_copied, n + 1)
                g, t = n // TILES, n % TILES
                dst = ot_dram[ds(t, 1), :, ds(g, 1), :].rearrange("o d u m -> (o d) (u m)")
                act.dma_start(dst, OT[:, s % 2].rearrange("p h b t -> p (h b t)")).then_inc(o_out[s % 2], 16)

            act.wait_ge(z_ready, 1)
            order = [("qe", 1), ("se", 2), ("kvc", 0), ("g", 0), ("tc", 1), ("d", 0), ("o", 2)]
            steps(act, {"order": order, "kvc": kv_copy, "g": gates, "d": decays}, {"qe": q_exp, "tc": t_copy}, {"se": s_exp, "o": o_copy})
            for s in o_out:
                act.wait_ge(s, 16 * STEPS // 2)

        @block.vector
        def _(dve):
            v = nc.vector

            def rope_tab(i, dims):
                t = rope[:, i, :]
                for _ in range(len(dims) - 2):
                    t = t.unsqueeze(1)
                return t.broadcast_to(dims)

            def q_max(n, s):
                p = s % 2
                dve.wait_ge(q_done, n + 1)
                from_one(dve, qexp_done, n - 1)
                v.tensor_reduce(qmx[:, p, :], QP[p][:].rearrange("p (h d) -> p h d", h=GRP), X, ALU.max).then_inc(qmax_raw, 1)
                dve.wait_ge(qmax_raw, n + 1)
                v.tensor_scalar(qnb[:, p, :], qmx[:, p, :], -1.0 / WS, None, ALU.mult).then_inc(qmax_ready, 1)

            def q_rope(n, s):
                p = s % 2
                q4 = QP[p][:].rearrange("p (h x d) -> p h x d", h=GRP, x=2)
                dve.wait_ge(qexp_done, n + 1)
                from_one(dve, q_roped, n)
                v.tensor_tensor(t1[:], q4, rope_tab(0, [P, GRP, 2, DH // 2]), ALU.mult)
                v.tensor_tensor(t2[:, :, 0, :], q4[:, :, 1, :], rope_tab(2, [P, GRP, DH // 2]), ALU.mult)
                v.tensor_tensor(t2[:, :, 1, :], q4[:, :, 0, :], rope_tab(1, [P, GRP, DH // 2]), ALU.mult).then_inc(q_read, 1)
                dve.wait_ge(q_read, n + 1)
                from_one(dve, t_done, n - 1)
                v.tensor_tensor(QR[:, p].rearrange("p h d -> p (h d)"), t1[:].rearrange("p h x d -> p (h x d)"),
                                t2[:].rearrange("p h x d -> p (h x d)"), ALU.add).then_inc(q_roped, 1)

            def q_decay(n, s):
                p = s % 2
                dve.wait_ge(qexp_done, n + 1)
                dve.wait_ge(eG_done, n + 1)
                v.reciprocal(qrs[:, p, :], qsum[:, p, :]).then_inc(qrs_ready, 1)
                dve.wait_ge(qrs_ready, n + 1)
                for h in range(GRP):
                    last = v.scalar_tensor_tensor(QD[:, p, h, :], E[:, p, h, :], qrs[:, p, h:h + 1], eG[:, p, :], ALU.mult, ALU.mult)
                last.then_inc(q_decayed, 1)

            def s_soft(n, s):
                p = s % 2
                dve.wait_ge(sc_done, n + 1)
                from_one(dve, sexp_done, n - 1)
                mk = lambda i: masks[:, i, :].unsqueeze(1).broadcast_to([P, 4, POS])
                v.tensor_tensor(S2[:, p], SC[:, 0], mk(0), ALU.add)
                v.scalar_tensor_tensor(L[:, p], SC[:, 1], BIG, mk(1), ALU.min, ALU.mult).then_inc(s_read, 1)
                dve.wait_ge(s_read, n + 1)
                v.tensor_reduce(smx[:, p, :], S2[:, p], X, ALU.max).then_inc(smax_raw, 1)
                dve.wait_ge(smax_raw, n + 1)
                v.tensor_scalar(snb[:, p, :], smx[:, p, :], -SCORE, None, ALU.mult).then_inc(smax_ready, 1)

            def s_prob(n, s):
                p = s % 2
                dve.wait_ge(sexp_done, n + 1)
                v.reciprocal(srs[:, p, :], ssum[:, p, :]).then_inc(srs_ready, 1)
                dve.wait_ge(srs_ready, n + 1)
                from_one(dve, pt_done, n - 1)
                for j in range(4):
                    last = v.scalar_tensor_tensor(PR[:, p, j, :], Es[:, p, j, :], srs[:, p, j:j + 1], L[:, p, j, :], ALU.mult, ALU.add)
                last.then_inc(p_ready, 1)

            def k_rope(n, s):
                p = s % 2
                dve.wait_ge(kv_copied, n + 1)
                from_one(dve, kexp_done, n - 1)
                v.tensor_reduce(kmx[:, p, :], K[:, p, :], X, ALU.max).then_inc(kmax_raw, 1)
                k3 = K[:, p, :].rearrange("p (x d) -> p x d", x=2)
                from_one(dve, k_roped, n)
                v.tensor_tensor(kt1[:], k3, rope_tab(0, [P, 2, DH // 2]), ALU.mult)
                dve.wait_ge(kmax_raw, n + 1)
                v.tensor_scalar(knb[:, p, :], kmx[:, p, :], -1.0, None, ALU.mult).then_inc(kmax_ready, 1)
                v.tensor_tensor(kt2[:, 0, :], k3[:, 1, :], rope[:, 2, :], ALU.mult)
                v.tensor_tensor(kt2[:, 1, :], k3[:, 0, :], rope[:, 1, :], ALU.mult).then_inc(k_terms, 1)
                dve.wait_ge(k_terms, n + 1)
                from_one(dve, t_done, n - 1)
                v.tensor_tensor(KR[:, p, :], kt1[:].rearrange("p x d -> p (x d)"), kt2[:].rearrange("p x d -> p (x d)"),
                                ALU.add).then_inc(k_roped, 1)
                dve.wait_ge(kln_done, n + 1)
                from_one(dve, G_done, n - 1)
                v.scalar_tensor_tensor(gate[:, p, :], K[:, p, :], 0.0, kln[:, p, :], ALU.min, ALU.subtract).then_inc(gate_ready, 1)

            def k_tcopy(n, s):
                dve.wait_ge(t_done, n + 1)
                from_one(dve, sc_done, n)
                v.tensor_copy(KT[:], KG[:, 1:3, :]).then_inc(kt_copied, 1)

            def k_decay(n, s):
                p = s % 2
                dve.wait_ge(kexp_done, n + 1)
                dve.wait_ge(eG_done, n + 1)
                v.reciprocal(krs[:, p, :], ksum[:, p, :]).then_inc(krs_ready, 1)
                dve.wait_ge(krs_ready, n + 1)
                from_one(dve, t_done, n - 1)
                v.scalar_tensor_tensor(KD[:, p, :], Ek[:, p, :], krs[:, p, :], eGn[:, p, :], ALU.mult, ALU.mult).then_inc(k_decayed, 1)

            def pt_copy(n, s):
                dve.wait_ge(pt_done, n + 1)
                from_one(dve, o_done, n - 1)
                v.tensor_copy(PT[:, s % 2], PTP).then_inc(pt_copied, 1)

            dve.wait_ge(consts_in, 64)
            order = [("qm", 1), ("ss", 2), ("qr", 1), ("qd", 1), ("sp", 2), ("kr", 0), ("ktc", 1), ("kd", 0), ("ptc", 2)]
            steps(dve, {"order": order, "kr": k_rope, "kd": k_decay}, {"qm": q_max, "qr": q_rope, "qd": q_decay, "ktc": k_tcopy},
                  {"ss": s_soft, "sp": s_prob, "ptc": pt_copy})


def output_phase(nc, h_dram, ot_dram, wo_dram, bt_dram, ag_dram, lb_dram, base_b, k_ident, k_before, out):
    with ExitStack() as ctx:
        sb = lambda name, shape, dt=F32: ctx.enter_context(nc.sbuf_tensor(name, shape, dt))
        pb = lambda name, shape, dt=F32: ctx.enter_context(nc.psum_tensor(name, shape, dt))
        sem = lambda name: ctx.enter_context(nc.semaphore(name))
        HALF = HID // 2
        ident, before, eps = sb("o_ident", [P, P]), sb("o_before", [P, NE, NE]), sb("o_eps", [P, 1])
        carry = sb("o_carry", [P, 1])
        Wo = sb("o_Wo", [P, 2, HEADS, HID], F16)
        BT = sb("o_BT", [P, 2, KC, HID], F16)
        AG = sb("o_AG", [P, 2, KC, AGW], F16)
        LB = sb("o_LB", [P, 2, HID], F16)
        bias = sb("o_bias", [P, HID])
        oT = sb("o_oT", [P, 4, HEADS // 2, P], BF16)
        ht = sb("o_ht", [P, 2, HID])
        xn = sb("o_xn", [P, HID])
        x2h, x2l = sb("o_x2h", [P, KC, P], F16), sb("o_x2l", [P, KC, P], F16)
        st, mv, sd, rs = sb("o_st", [P, 2, 6]), sb("o_mv", [P, 2]), sb("o_sd", [P, 1]), sb("o_rs", [P, 1])
        lg, top, ntop = sb("o_lg", [P, NE]), sb("o_top", [P, 1]), sb("o_ntop", [P, 1])
        gt_, eq_ = sb("o_gt", [P, NE, NE]), sb("o_eq", [P, NE, NE])
        rank, sel, ew, wsum, wr, wf = (sb("o_" + x, [P, n]) for x, n in (("rank", NE), ("sel", NE), ("ew", NE), ("wsum", 1), ("wr", 1), ("wf", NE)))
        lw = sb("o_lw", [P, NE, RANK])
        lwh, lwl = sb("o_lwh", [P, P], F16), sb("o_lwl", [P, P], F16)
        Y = [pb(f"o_Y{i}", [P, HALF]) for i in range(2)]
        XT = [pb(f"o_XT{i}", [P, 4, P]) for i in range(2)]
        F = [pb(f"o_F{i}", [P, HALF]) for i in range(2)]
        LG, LWT = pb("o_LG", [P, 512]), pb("o_LWT", [P, 512])

        consts_in, ffn_in = sem("o_consts_in"), sem("o_ffn_in")
        h_in, out_done = ([sem(f"o_{x}{i}") for i in range(2)] for x in ("h_in", "out_done"))
        o_in = [sem(f"o_o_in{i}") for i in range(4)]
        NWP = 8
        wo_in = [sem(f"o_wo_in{i}") for i in range(NWP)]
        o_used, y_done, h2_ready, stats, var_ready, sd_ready, rs_ready, xn_ready, x_t, x_hi, x_lo = (sem("o_" + x) for x in
            ("o_used", "y_done", "h2_ready", "stats", "var_ready", "sd_ready", "rs_ready", "xn_ready", "x_t", "x_hi", "x_lo"))
        lg_done, link, ew_ready, lw_ready, lw_t, lw_hi, lw_lo, f_done, hb_ready, fin_ready, top_ready = (sem("o_" + x) for x in
            ("lg_done", "link", "ew_ready", "lw_ready", "lw_t", "lw_hi", "lw_lo", "f_done", "hb_ready", "fin_ready", "top_ready"))
        link2 = sem("o_link2")
        block = ctx.enter_context(nc.Block())

        def steps(order, fns):
            def step(t, par):
                for name, lag in order:
                    if not isinstance(t, int) or 0 <= t - lag < TILES:
                        fns[name](t - lag, (par + lag) % 2)
            return step

        def run(eng, order, fns):
            step = steps(order, fns)
            step(0, 0)
            step(1, 1)
            with eng.Fori(1, TILES // 2) as half:
                t = half * 2
                step(t, 0)
                step(t + 1, 1)
            step(TILES, 0)

        @block.sync
        def _(sp):
            ov = ot_dram.rearrange("t d g m -> t d (g m)").rearrange("t d (x m) -> t d x m", x=2)
            hv = h_dram.rearrange("(t p) n -> t p n", p=P)

            def load(t, par):
                if not isinstance(t, int) or t >= 2:
                    sp.wait_ge(o_used, 2 * (t - 1))
                for x in range(2):
                    sp.dma_start(oT[:, 2 * par + x].rearrange("p h n -> p (h n)"),
                                 ov[ds(t, 1), :, x, :].rearrange("o d m -> (o d) m")).then_inc(o_in[2 * par + x], 16)
                if not isinstance(t, int) or t >= 2:
                    sp.wait_ge(out_done[par], turns(t - 2, par, 16))
                sp.dma_start(ht[:, par, :], hv[ds(t, 1)].rearrange("o p n -> (o p) n")).then_inc(h_in[par], 16)
            load(0, 0)
            for i in range(NWP):
                n = HEADS // NWP
                for x in range(2):
                    sp.dma_start(Wo[:, x, i * n:(i + 1) * n, :], wo_dram[x, :, i * n:(i + 1) * n, :]).then_inc(wo_in[i], 16)
            load(1, 1)
            with sp.Fori(1, TILES // 2) as half:
                t = half * 2
                load(t, 0)
                load(t + 1, 1)

        @block.tensor
        def _(pe):
            mm = nc.tensor.matmul

            def project(t, par, x):
                pe.wait_ge(o_in[2 * par + x], turns(t, par, 16))
                if x == 0:
                    from_one(pe, h2_ready, t)
                for h in range(HEADS // 2):
                    k = x * HEADS // 2 + h
                    if isinstance(t, int) and t == 0 and k % (HEADS // NWP) == 0:
                        pe.wait_ge(wo_in[k // (HEADS // NWP)], 32)
                    for i in range(2):
                        for y in range(2):
                            last = mm(Y[y][:], oT[:, 2 * par + x, h, :], Wo[:, i, k, y * HALF:(y + 1) * HALF],
                                      start=(k == 0 and i == 0), stop=(k == HEADS - 1 and i == 1))
                last.then_inc(o_used, 1)

            def x_transpose(t, par):
                pe.wait_ge(xn_ready, t + 1)
                from_one(pe, x_lo, t)
                for c in range(KC):
                    last = nc.tensor.transpose(XT[c // 4][:, c % 4, :], xn[:, c * P:(c + 1) * P], ident[:])
                last.then_inc(x_t, 1)

            def gates(t, par):
                if isinstance(t, int) and t == 0:
                    pe.wait_ge(ffn_in, 16 * 4)
                pe.wait_ge(x_lo, t + 1)
                from_one(pe, lw_ready, t)
                for c in range(KC):
                    mm(LG[:, 0:AGW], x2h[:, c, :], AG[:, 0, c, :], start=(c == 0), stop=False)
                    mm(LG[:, 0:AGW], x2h[:, c, :], AG[:, 1, c, :], start=False, stop=False)
                    last = mm(LG[:, 0:AGW], x2l[:, c, :], AG[:, 0, c, :], start=False, stop=(c == KC - 1))
                last.then_inc(lg_done, 1)

            def base(t, par):
                from_one(pe, fin_ready, t)
                for y in range(2):
                    cols = slice(y * HALF, (y + 1) * HALF)
                    for c in range(KC):
                        mm(F[y][:], x2h[:, c, :], BT[:, 0, c, cols], start=(c == 0), stop=False)
                        mm(F[y][:], x2h[:, c, :], BT[:, 1, c, cols], start=False, stop=False)
                        mm(F[y][:], x2l[:, c, :], BT[:, 0, c, cols], start=False, stop=False)
                    if y == 0:
                        pe.wait_ge(lw_ready, t + 1)
                        from_one(pe, lw_lo, t)
                        nc.tensor.transpose(LWT[:, 0:P], lw[:].rearrange("p e r -> p (e r)"), ident[:]).then_inc(lw_t, 1)
                pe.wait_ge(lw_lo, t + 1)
                for y in range(2):
                    cols = slice(y * HALF, (y + 1) * HALF)
                    mm(F[y][:], lwh[:], LB[:, 0, cols], start=False, stop=False)
                    mm(F[y][:], lwh[:], LB[:, 1, cols], start=False, stop=False)
                    last = mm(F[y][:], lwl[:], LB[:, 0, cols], start=False, stop=True)
                last.then_inc(f_done, 1)

            pe.wait_ge(consts_in, 48)
            run(pe, [("ya", 0), ("xt", 1), ("yb", 0), ("g", 1), ("f", 1)],
                {"ya": lambda t, p: project(t, p, 0), "yb": lambda t, p: project(t, p, 1), "xt": x_transpose, "g": gates, "f": base})

        @block.scalar
        def _(act):
            act.dma_start(ident[:], k_ident).then_inc(consts_in, 16)
            act.dma_start(before[:].rearrange("p a b -> p (a b)"), k_before).then_inc(consts_in, 16)
            act.dma_start(bias[:], base_b.rearrange("(a n) -> a n", a=1).broadcast_to([P, HID])).then_inc(consts_in, 16)
            for x in range(2):
                act.dma_start(BT[:, x], bt_dram[x]).then_inc(ffn_in, 16)
            act.dma_start(AG[:].rearrange("p x k n -> p x (k n)"), ag_dram.rearrange("x p k n -> p x (k n)")).then_inc(ffn_in, 16)
            act.dma_start(LB[:], lb_dram.rearrange("x p n -> p x n")).then_inc(ffn_in, 16)
            a = nc.scalar.activation

            def root(t, par):
                act.wait_ge(var_ready, t + 1)
                a(sd[:], mv[:, 1:2], ACT.Sqrt, bias=eps[:]).then_inc(sd_ready, 1)

            def high(t, par):
                act.wait_ge(x_t, t + 1)
                from_one(act, f_done, t)
                for i in range(2):
                    last = a(x2h[:, 4 * i:4 * i + 4, :], XT[i][:], ACT.Copy)
                last.then_inc(x_hi, 1)

            def weigh(t, par):
                act.wait_ge(top_ready, t + 1)
                a(ew[:], lg[:], ACT.Exp, bias=ntop[:]).then_inc(ew_ready, 1)

            def lw_high(t, par):
                act.wait_ge(lw_t, t + 1)
                from_one(act, f_done, t)
                a(lwh[:], LWT[:, 0:P], ACT.Copy).then_inc(lw_hi, 1)

            def store(t, par):
                act.wait_ge(fin_ready, t + 1)
                act.dma_start(out.rearrange("(t p) n -> t p n", p=P)[ds(t, 1)].rearrange("o p n -> (o p) n"),
                              ht[:, par, :]).then_inc(out_done[par], 16)
            run(act, [("h", 1), ("r", 0), ("w", 1), ("l", 1), ("s", 1)],
                {"r": root, "h": high, "w": weigh, "l": lw_high, "s": store})
            for s in out_done:
                act.wait_ge(s, 16 * TILES // 2)

        @block.vector
        def _(dve):
            v = nc.vector
            NL = 6

            def residual(t, par):
                dve.wait_ge(o_used, 2 * (t + 1))
                dve.wait_ge(h_in[par], turns(t, par, 16))
                for y in range(2):
                    hs = ht[:, par, y * HALF:(y + 1) * HALF]
                    last = v.scalar_tensor_tensor(hs, Y[y][:], 1.0 / WS, hs, ALU.mult, ALU.add)
                last.then_inc(h2_ready, 1)
                dve.wait_ge(h2_ready, t + 1)
                for y in range(2):
                    last = v.bn_stats(st[:, y, :], ht[:, par, y * HALF:(y + 1) * HALF])
                last.then_inc(stats, 1)
                dve.wait_ge(stats, t + 1)
                v.memset(carry[:], 0.0)
                v.bn_aggr(mv[:], st[:]).then_inc(var_ready, 1)

            def normalise(t, par):
                dve.wait_ge(sd_ready, t + 1)
                v.reciprocal(rs[:], sd[:]).then_inc(rs_ready, 1)
                dve.wait_ge(rs_ready, t + 1)
                dve.wait_ge(var_ready, t + 1)
                from_one(dve, x_t, t)
                v.tensor_scalar(xn[:], ht[:, par, :], mv[:, 0:1], rs[:], ALU.subtract, ALU.mult).then_inc(xn_ready, 1)
                dve.wait_ge(xn_ready, t + 1)
                v.tensor_tensor(ht[:, par, :], ht[:, par, :], bias[:], ALU.add).then_inc(hb_ready, 1)

            def low(t, par):
                dve.wait_ge(x_hi, t + 1)
                for i in range(2):
                    last = v.tensor_tensor(x2l[:, 4 * i:4 * i + 4, :], XT[i][:], x2h[:, 4 * i:4 * i + 4, :], ALU.subtract)
                last.then_inc(x_lo, 1)

            def gating(t, par):
                dve.wait_ge(lg_done, t + 1)
                b = NL * t

                def step(i, ins):
                    ins.then_inc(link, 1)
                    dve.wait_ge(link, b + i)
                step(1, v.tensor_scalar(lg[:], LG[:, ER:AGW], 1.0 / WS, None, ALU.mult))
                v.tensor_reduce(top[:], lg[:], X, ALU.max)
                me = lg[:].unsqueeze(2).broadcast_to([P, NE, NE])
                other = lg[:].unsqueeze(1).broadcast_to([P, NE, NE])
                v.tensor_tensor(gt_[:], other, me, ALU.is_gt)
                step(2, v.tensor_tensor(eq_[:], other, me, ALU.is_equal))
                v.tensor_scalar(ntop[:], top[:], -1.0, None, ALU.mult).then_inc(top_ready, 1)
                step(3, v.tensor_tensor(eq_[:], eq_[:], before[:], ALU.mult))
                step(4, v.tensor_tensor(gt_[:], gt_[:], eq_[:], ALU.add))
                step(5, v.tensor_reduce(rank[:], gt_[:], X, ALU.add))
                step(6, v.tensor_scalar(sel[:], rank[:], 1.5, None, ALU.is_lt))

            def weights(t, par):
                dve.wait_ge(ew_ready, t + 1)
                b = 4 * t

                def step(i, ins):
                    ins.then_inc(link2, 1)
                    dve.wait_ge(link2, b + i)
                step(1, v.tensor_tensor(ew[:], ew[:], sel[:], ALU.mult))
                step(2, v.tensor_reduce(wsum[:], ew[:], X, ALU.add))
                step(3, v.reciprocal(wr[:], wsum[:]))
                step(4, v.tensor_scalar(wf[:], ew[:], wr[:], LORA_SCALE / WS, ALU.mult, ALU.mult))
                from_one(dve, lw_t, t)
                v.tensor_tensor(lw[:], LG[:, 0:ER].rearrange("p (e r) -> p e r", e=NE), wf[:].unsqueeze(2).broadcast_to([P, NE, RANK]),
                                ALU.mult).then_inc(lw_ready, 1)

            def lw_low(t, par):
                dve.wait_ge(lw_hi, t + 1)
                v.tensor_tensor(lwl[:], LWT[:, 0:P], lwh[:], ALU.subtract).then_inc(lw_lo, 1)

            def finish(t, par):
                dve.wait_ge(f_done, t + 1)
                dve.wait_ge(hb_ready, t + 1)
                for y in range(2):
                    hs = ht[:, par, y * HALF:(y + 1) * HALF]
                    last = v.scalar_tensor_tensor(hs, F[y][:], 1.0 / WS, hs, ALU.mult, ALU.add)
                last.then_inc(fin_ready, 1)

            v.memset(eps[:], EPS)
            dve.wait_ge(consts_in, 48)
            run(dve, [("lo", 1), ("r", 0), ("g", 1), ("w", 1), ("ll", 1), ("n", 0), ("f", 1)],
                {"r": residual, "n": normalise, "lo": low, "g": gating, "w": weights, "ll": lw_low, "f": finish})


def block_kernel(nc, x, abslog, phase, Wq, Wk, Wv, Wo, gate_w, base_w, base_b, lora_A, lora_B,
                 k_ident, k_rope, k_masks, k_cum, k_mult, k_before, out):
    scratch = lambda name, shape, dt: nc.dram_tensor(name, shape, dt).ap()
    h_dram = scratch("h_dram", (TOK, HID), F32)
    ot_dram = scratch("ot_dram", (TILES, P, KVH, GRP * P), BF16)
    wo_dram = scratch("wo_dram", (2, P, HEADS, HID), F16)
    bt_dram = scratch("bt_dram", (2, P, KC, HID), F16)
    ag_dram = scratch("ag_dram", (2, P, KC, AGW), F16)
    lb_dram = scratch("lb_dram", (2, P, HID), F16)
    tokens_phase(nc, x, abslog, phase, k_ident, k_mult, h_dram)
    with nc.sbuf_tensor("xh", [P, KC, TOK], F16) as xh, nc.sbuf_tensor("xl", [P, KC, TOK], F16) as xl:
        norm_phase(nc, xh, xl, h_dram, base_w, gate_w, lora_A, lora_B, k_ident, bt_dram, ag_dram, lb_dram)
        attention_phase(nc, xh, xl, Wq, Wk, Wv, Wo, k_ident, k_rope, k_masks, k_cum, ot_dram, wo_dram)
    output_phase(nc, h_dram, ot_dram, wo_dram, bt_dram, ag_dram, lb_dram, base_b, k_ident, k_before,
                 out.rearrange("b n d -> (b n) d"))


_INS = ['x', 'L0_tok_A_abslog', 'L0_tok_A_phase', 'L0_attn_Wq', 'L0_attn_Wk', 'L0_attn_Wv', 'L0_attn_Wo',
        'L0_ffn_gate_w', 'L0_ffn_base_w', 'L0_ffn_base_b', 'L0_ffn_lora_A', 'L0_ffn_lora_B']


def kernel(**inputs):
    import numpy as _np
    import concourse.bacc as _bacc
    from concourse import mybir as _mybir
    from concourse.bass_utils import run_bass_kernel_spmd as _run

    nc = _bacc.Bacc("TRN2", target_bir_lowering=False, num_devices=1)
    arrays, args = {}, []
    for name, a in [(n, inputs[n]) for n in _INS] + list(constants().items()):
        a = _np.ascontiguousarray(a)
        arrays[f"in_{name}_dram"] = a
        args.append(nc.dram_tensor(f"in_{name}_dram", a.shape, _mybir.dt.from_np(a.dtype), kind="ExternalInput").ap())
    args.append(nc.dram_tensor("out_0_dram", (BATCH, POS, HID), _mybir.dt.float32, kind="ExternalOutput").ap())
    block_kernel(nc, *args)
    r = _run(nc, [arrays], core_ids=[0])
    return r.results[0]["out_0_dram"]
```

```python
from contextlib import ExitStack

import numpy as np
import concourse.bass as bass
from concourse import mybir

F32 = mybir.dt.float32
F16 = mybir.dt.float16
BF16 = mybir.dt.bfloat16
ALU = mybir.AluOpType
ACT = mybir.ActivationFunctionType
X = mybir.AxisListType.X
ds = bass.ds

P = 128
BATCH, POS, NST = 32, 64, 64
HID = 1024
TOK = BATCH * POS
TILES = TOK // P
KC = HID // P
HEADS, KVH, DH = 32, 8, 128
GRP = HEADS // KVH
QW, KVW = GRP * DH, 2 * DH
GW = QW + KVW
STEPS = KVH * TILES
NE, RANK = 8, 16
ER = NE * RANK
AGW = ER + NE
WS = 64.0
SCORE = 1.0 / float(np.sqrt(DH))
LORA_SCALE = 2.0
EPS = 1e-5
BIG = 1e30
PART = 4
PARTS, KEPT = HEADS // PART, 2
NA_, NB_ = 4, 256
NB1 = 16
MUL = [NB_ * a for a in range(NA_)] + [NB1 * b for b in range(16)] + list(range(16))
A0, B10, B20, NM = 0, NA_, NA_ + 16, len(MUL)
MONE = B20 + 1
HC = 4
MAGIC = 12582912.0
PI = float(np.pi)
C1 = 6.28125
C2 = float(np.float32(2 * np.pi - C1))


def constants():
    p = np.arange(P)
    pos, seq = p % POS, p // POS
    inv = (1.0 / (np.float32(10000.0) ** (2.0 * np.arange(DH // 2, dtype=np.float32) / np.float32(DH)))).astype(np.float32)
    fr = pos[:, None].astype(np.float32) * inv[None, :]
    causal = pos[:, None] >= np.arange(POS)[None, :]
    s, t = p[:, None], p[None, :]
    mid = POS // 2 - 1
    cum = ((s % POS <= t % POS) * 1.0 - (s % POS <= mid) * 1.0) * (s // POS == t // POS) / 16.0
    return {
        "ident": np.eye(P, dtype=np.float32),
        "minus": -np.eye(P, dtype=np.float16),
        "rope": np.concatenate([t / s for s in (1.0, WS) for t in (np.cos(fr), np.sin(fr), -np.sin(fr))], axis=1).astype(np.float32),
        "masks": np.concatenate([np.where(causal, 0.0, -BIG), causal * 1.0], axis=1).astype(np.float32),
        "cum": cum.astype(np.float32),
        "mult": np.broadcast_to(np.array(MUL, np.float32), (P, NM)).copy(),
        "before": np.broadcast_to((np.arange(NE)[None, :] < np.arange(NE)[:, None]).astype(np.float32).reshape(1, NE * NE), (P, NE * NE)).copy(),
    }


def from_one(eng, sem, value):
    if isinstance(value, int) and value <= 0:
        return
    eng.wait_ge(sem, value)


def turns(t, par, each):
    return (t - par) * (each // 2) + each


def tokens_phase(nc, C, abslog, phase, base_w, gate_w, lora_A, lora_B, k_ident, k_mult,
                 h_dram, bt_dram, ag_dram, lb_dram):
    NCH = POS // HC
    NW = KC + 2
    with ExitStack() as ctx:
        sb = lambda name, shape, dt=F32: ctx.enter_context(nc.sbuf_tensor(name, shape, dt))
        pb = lambda name, shape, dt=F32: ctx.enter_context(nc.psum_tensor(name, shape, dt))
        sem = lambda name: ctx.enter_context(nc.semaphore("t_" + name))
        ident, mult = sb("t_ident", [P, P]), sb("t_mult", [P, NM])
        la_in, ph_in = sb("la_in", [POS, 2, NST]), sb("ph_in", [POS, 2, NST])
        lp = sb("lp", [P, 2, POS])
        cin = sb("cin", [P, 16, NST, 2])
        cdup = sb("cdup", [P, 16, 2, 2, NST])
        X1, X2 = sb("X1", [P, POS, BATCH]), sb("X2", [P, POS, BATCH])
        ang, rnd, cosr, sinr, dec = (sb(f"t_{x}", [P, POS, NM]) for x in ("ang", "rnd", "cosr", "sinr", "dec"))
        halfpi = sb("halfpi", [P, 1])
        sm = sb("t_sm", [P, 10, POS])
        e1 = sb("e1", [P, 4, POS, NA_])
        TF1, TF2 = sb("TF1", [P, POS, NA_]), sb("TF2", [P, POS, NA_])
        U, V = sb("t_U", [P, POS, 16]), sb("t_V", [P, POS, 16])
        E2a, E2b = sb("E2a", [P, 2, HC, 16, 16]), sb("E2b", [P, 2, HC, 16, 16])
        Ga, Gb = sb("Ga", [P, 2, HC, NA_, BATCH]), sb("Gb", [P, 2, HC, NA_, BATCH])
        hst = sb("hst", [P, 2, HC, NB_])
        wt = sb("w_rows", [P, 2, HID])
        gt = sb("gate_rows", [NE, HID])
        lbt = sb("lb_rows", [P, KC, NE, RANK])
        w_hi, w_lo = sb("w_hi", [P, 2, KC, P], F16), sb("w_lo", [P, 2, KC, P], F16)
        ag = sb("ag_parts", [P, 2, KC, AGW], F16)
        lb = sb("lb_parts", [P, 2, HID], F16)
        bank = [pb(f"t_bank{i}", [P, 512]) for i in range(8)]
        pH = [b[:].rearrange("p (j b) -> p j b", j=2) for b in bank[4:8]]
        pW = [bank[0:2], bank[2:4]]

        consts_in, params_in, c_in, c_split = sem("consts_in"), sem("params_in"), sem("c_in"), sem("c_split")
        params_t, params_copied, c_t, c_copied1, c_copied2 = (sem(x) for x in
            ("params_t", "params_copied", "c_t", "c_copied1", "c_copied2"))
        link, alink, angles, dec_arg, trig, dec_done = (sem(x) for x in ("link", "alink", "angles", "dec_arg", "trig", "dec_done"))
        g_terms, g_ready, e_ready, h_done, h_copied = (sem(x) for x in ("g_terms", "g_ready", "e_ready", "h_done", "h_copied"))
        h_out, w_in, w_out = ([sem(f"{x}{i}") for i in range(2)] for x in ("h_out", "w_in", "w_out"))
        rest_in, w_t, w_high, w_low = sem("rest_in"), sem("w_t"), sem("w_high"), sem("w_low")
        block = ctx.enter_context(nc.Block())

        @block.sync
        def _(sp):
            for dup in range(2):
                sp.dma_start(la_in[:, dup, :], abslog).then_inc(params_in, 16)
                sp.dma_start(ph_in[:, dup, :], phase).then_inc(params_in, 16)
            sp.dma_start(ident[:], k_ident).then_inc(consts_in, 16)
            sp.dma_start(mult[:], k_mult).then_inc(consts_in, 16)
            sp.dma_start(cin[:].rearrange("p i n r -> p i (n r)"),
                         C.rearrange("c h n r -> (c h) (n r)").rearrange("(i p) m -> p i m", p=P)).then_inc(c_in, 16)
            hv = h_dram.rearrange("(c h) (a b) -> a c h b", h=POS, b=NB_)

            def store(k, par):
                sp.wait_ge(h_copied, 2 * (k + 1))
                for a in range(NA_):
                    sp.dma_start(hv[a, :, ds(k * HC, HC), :], hst[a * BATCH:(a + 1) * BATCH, par]).then_inc(h_out[par], 16)
            with sp.Fori(0, NCH // 2) as half:
                store(half * 2, 0)
                store(half * 2 + 1, 1)
            for s in h_out:
                sp.wait_ge(s, 16 * NA_ * NCH // 2)

        @block.gpsimd
        def _(pool):
            def load(k):
                src = base_w[k * P:(k + 1) * P, :] if k < KC else lora_A.rearrange("e r n -> (e r) n")
                pool.dma_start(wt[:, k % 2, :], src).then_inc(w_in[k % 2], 16)
            load(0)
            load(1)
            pool.dma_start(gt[:], gate_w).then_inc(rest_in, 16)
            for k in range(KC):
                pool.dma_start(lbt[:, k], lora_B[:, k * P:(k + 1) * P, :].rearrange("e p r -> p e r")).then_inc(rest_in, 16)
            for k in range(NW):
                pool.wait_ge(w_low, k + 1)
                if k + 2 <= KC:
                    load(k + 2)
                for i, part in enumerate((w_hi, w_lo)):
                    dst, src = ((bt_dram[i, :, :, k * P:(k + 1) * P], part[:, k % 2]) if k < KC else
                                (ag_dram[i], ag[:, i]) if k == KC else (lb_dram[i], lb[:, i]))
                    pool.dma_start(dst, src).then_inc(w_out[k % 2], 16)
            for s in w_out:
                pool.wait_ge(s, 16 * NW)

        @block.tensor
        def _(pe):
            pe.wait_ge(params_in, 64)
            pe.wait_ge(consts_in, 32)
            nc.tensor.transpose(bank[7][:, 0:POS], la_in[:].rearrange("p a n -> p (a n)"), ident[0:POS, 0:POS])
            nc.tensor.transpose(bank[7][:, POS:2 * POS], ph_in[:].rearrange("p a n -> p (a n)"),
                                ident[0:POS, 0:POS]).then_inc(params_t, 1)
            pe.wait_ge(c_split, 1)
            for i in range(4):
                if i == 3:
                    pe.wait_ge(params_copied, 1)
                for r in range(2):
                    for j in range(4):
                        last = nc.tensor.transpose(bank[2 * i + r][:, j * P:(j + 1) * P],
                                                   cdup[:, 4 * i + j, r].rearrange("p d n -> p (d n)"), ident[:])
                last.then_inc(c_t, 1)

            def product(k, par):
                pe.wait_ge(g_ready, k + 1)
                pe.wait_ge(e_ready, k + 1)
                from_one(pe, h_copied, 2 * (k - 1))
                for j in range(HC):
                    o = pH[2 * par + j // 2][:, j % 2, :]
                    w = Ga[:, par, j].rearrange("p a c -> p (a c)")
                    nc.tensor.matmul(o, w, E2a[:, par, j].rearrange("p x y -> p (x y)"), start=True, stop=False)
                    last = nc.tensor.matmul(o, w, E2b[:, par, j].rearrange("p x y -> p (x y)"), start=False, stop=True)
                    if j % 2:
                        last.then_inc(h_done, 1)

            def weights(k):
                if k <= KC:
                    pe.wait_ge(w_in[k % 2], 16 * (k // 2 + 1))
                if k == KC:
                    pe.wait_ge(rest_in, 16 * (KC + 1))
                if k >= 2:
                    pe.wait_ge(w_low, k - 1 if k <= KC else k)
                for j in range(KC):
                    src = wt[:, k % 2, j * P:(j + 1) * P] if k <= KC else lbt[:, j].rearrange("p e r -> p (e r)")
                    last = nc.tensor.transpose(pW[k % 2][j // 4][:, (j % 4) * P:(j % 4 + 1) * P], src, ident[:])
                if k == KC:
                    pe.wait_ge(w_low, KC)
                    for j in range(KC):
                        last = nc.tensor.transpose(pW[1][0][:, j * NE:(j + 1) * NE], gt[:, j * P:(j + 1) * P], ident[0:NE, 0:NE])
                last.then_inc(w_t, 1)
            pe.wait_ge(c_copied1, 4)
            pe.wait_ge(c_copied2, 4)
            for k in range(NW):
                weights(k)
                product(k, k % 2)
            with pe.Fori(NW // 2, NCH // 2) as half:
                product(half * 2, 0)
                product(half * 2 + 1, 1)

        @block.scalar
        def _(act):
            a = nc.scalar.activation
            act.wait_ge(c_in, 16)
            for r in range(2):
                last = a(cdup[:, :, r], cin[:, :, :, r].unsqueeze(2).broadcast_to([P, 16, 2, NST]), ACT.Copy)
            last.then_inc(c_split, 1)
            act.wait_ge(dec_arg, 1)
            a(dec[:], dec[:], ACT.Exp).then_inc(dec_done, 1)
            act.wait_ge(angles, 1)
            a(cosr[:], ang[:], ACT.Abs).then_inc(alink, 1)
            a(sinr[:], ang[:], ACT.Sin)
            act.wait_ge(alink, 1)
            a(cosr[:], cosr[:], ACT.Sin, bias=halfpi[:], scale=-1.0).then_inc(trig, 1)
            for i in range(4):
                act.wait_ge(c_t, i + 1)
                src = bank[2 * i + 1][:].rearrange("p (c h) -> p h c", h=POS)
                a(X2[:, :, 8 * i:8 * i + 8], src, ACT.Copy).then_inc(c_copied2, 1)

            def copy_out(k, par):
                if not isinstance(k, int) or k >= 2:
                    act.wait_ge(h_out[par], turns(k - 2, par, 16 * NA_))
                for j in range(2):
                    act.wait_ge(h_done, 2 * k + j + 1)
                    a(hst[:, par, 2 * j:2 * j + 2, :], pH[2 * par + j], ACT.Copy).then_inc(h_copied, 1)

            def high(k):
                act.wait_ge(w_t, k + 1)
                if k >= 2:
                    act.wait_ge(w_out[k % 2], 32 * (k // 2))
                for x in range(2):
                    src = pW[k % 2][x][:]
                    if k < KC:
                        dst = w_hi[:, k % 2, 4 * x:4 * x + 4, :].rearrange("p k n -> p (k n)")
                    elif k == KC:
                        dst, src = ag[:, 0, 4 * x:4 * x + 4, 0:ER], src.rearrange("p (k n) -> p k n", k=4)
                    else:
                        dst = lb[:, 0, x * 512:(x + 1) * 512]
                    last = a(dst, src, ACT.Copy, scale=WS)
                if k == KC:
                    last = a(ag[:, 0, :, ER:AGW], pW[1][0][:, 0:KC * NE].rearrange("p (k n) -> p k n", k=KC), ACT.Copy, scale=WS)
                last.then_inc(w_high, 1)
            for k in range(NW):
                high(k)
                copy_out(k, k % 2)
            with act.Fori(NW // 2, NCH // 2) as half:
                copy_out(half * 2, 0)
                copy_out(half * 2 + 1, 1)

        @block.vector
        def _(dve):
            count = [0]

            def step(ins):
                count[0] += 1
                ins.then_inc(link, 1)
                dve.wait_ge(link, count[0])
            v = nc.vector
            v.memset(halfpi[:], PI / 2)
            dve.wait_ge(params_t, 1)
            v.tensor_copy(lp[:], bank[7][:, 0:2 * POS].rearrange("p (k h) -> p k h", k=2)).then_inc(params_copied, 1)
            dve.wait_ge(params_copied, 1)
            dve.wait_ge(consts_in, 32)
            mb = mult[:].unsqueeze(1).broadcast_to([P, POS, NM])
            v.tensor_tensor(dec[:], lp[:, 0, :].unsqueeze(2).broadcast_to([P, POS, NM]), mb, ALU.mult).then_inc(dec_arg, 1)
            step(v.tensor_tensor(ang[:], lp[:, 1, :].unsqueeze(2).broadcast_to([P, POS, NM]), mb, ALU.mult))
            step(v.tensor_scalar(rnd[:], ang[:], 1.0 / (2 * PI), MAGIC, ALU.mult, ALU.add))
            step(v.tensor_scalar(rnd[:], rnd[:], MAGIC, None, ALU.subtract))
            fl = lambda t: t[:].rearrange("p h m -> p (h m)")
            for c in (C1, C2):
                step(v.scalar_tensor_tensor(fl(ang), fl(rnd), -c, fl(ang), ALU.mult, ALU.add))
            v.tensor_scalar(ang[:], ang[:], PI, -PI, ALU.min, ALU.max).then_inc(angles, 1)
            for i in range(4):
                dve.wait_ge(c_t, i + 1)
                src = bank[2 * i][:].rearrange("p (c h) -> p h c", h=POS)
                v.tensor_copy(X1[:, :, 8 * i:8 * i + 8], src).then_inc(c_copied1, 1)
            dve.wait_ge(trig, 1)
            dve.wait_ge(dec_done, 1)
            v.tensor_tensor(sinr[:], sinr[:], dec[:], ALU.mult)
            step(v.tensor_tensor(cosr[:], cosr[:], dec[:], ALU.mult))
            la, w = lp[:, 0, :], ang[:, :, MONE]
            ar, den, den2, n1, n2, n3, n4, fr, fi = (sm[:, i, :] for i in range(9))
            ai = sinr[:, :, MONE]
            v.tensor_scalar(ar, cosr[:, :, MONE], 1.0, None, ALU.subtract)
            v.tensor_tensor(den, la, la, ALU.mult)
            step(v.tensor_tensor(den2, w, w, ALU.mult))
            v.tensor_tensor(n1, ar, la, ALU.mult)
            v.tensor_tensor(n2, ai, w, ALU.mult)
            v.tensor_tensor(n3, ai, la, ALU.mult)
            v.tensor_tensor(n4, ar, w, ALU.mult)
            step(v.tensor_tensor(den, den, den2, ALU.add))
            step(v.reciprocal(den, den))
            v.tensor_tensor(n1, n1, n2, ALU.add)
            step(v.tensor_tensor(n3, n3, n4, ALU.subtract))
            v.scalar_tensor_tensor(fr, n1, 2.0, den, ALU.mult, ALU.mult)
            step(v.scalar_tensor_tensor(fi, n3, 2.0, den, ALU.mult, ALU.mult))
            frb, fib = (t.unsqueeze(2).broadcast_to([P, POS, NA_]) for t in (fr, fi))
            ca, sa = cosr[:, :, A0:A0 + NA_], sinr[:, :, A0:A0 + NA_]
            for i, (x, y) in enumerate(((frb, ca), (fib, sa), (frb, sa), (fib, ca))):
                last = v.tensor_tensor(e1[:, i], x, y, ALU.mult)
            step(last)
            v.tensor_tensor(e1[:, 0], e1[:, 0], e1[:, 1], ALU.subtract)
            step(v.tensor_tensor(e1[:, 2], e1[:, 2], e1[:, 3], ALU.add))
            lo, hi = slice(0, 64), slice(64, 128)
            v.tensor_copy(TF1[lo], e1[lo, 0])
            v.tensor_scalar(TF1[hi], e1[hi, 2], -1.0, None, ALU.mult)
            v.tensor_scalar(TF2[lo], e1[lo, 2], -1.0, None, ALU.mult)
            v.tensor_scalar(TF2[hi], e1[hi, 0], -1.0, None, ALU.mult)
            cb, sb_ = cosr[:, :, B10:B10 + 16], sinr[:, :, B10:B10 + 16]
            v.tensor_copy(U[lo], cb[lo])
            v.tensor_copy(U[hi], sb_[hi])
            v.tensor_scalar(V[lo], sb_[lo], -1.0, None, ALU.mult)
            step(v.tensor_copy(V[hi], cb[hi]))
            dve.wait_ge(c_copied2, 4)
            dve.wait_ge(c_copied1, 4)

            def build(k, par):
                from_one(dve, h_done, 2 * (k - 1))
                hs = ds(k * HC, HC)
                c = lambda t: t[:, hs, :].unsqueeze(2).broadcast_to([P, HC, NA_, BATCH])
                f = lambda t: t[:, hs, :].unsqueeze(3).broadcast_to([P, HC, NA_, BATCH])
                v.tensor_tensor(Ga[:, par], c(X1), f(TF1), ALU.mult)
                v.tensor_tensor(Gb[:, par], c(X2), f(TF2), ALU.mult).then_inc(g_terms, 1)
                o = lambda t: t[:, hs, :].unsqueeze(3).broadcast_to([P, HC, 16, 16])
                i = lambda t: t[:, hs, B20:B20 + 16].unsqueeze(2).broadcast_to([P, HC, 16, 16])
                v.tensor_tensor(E2a[:, par], o(U), i(cosr), ALU.mult)
                v.tensor_tensor(E2b[:, par], o(V), i(sinr), ALU.mult).then_inc(e_ready, 1)
                dve.wait_ge(g_terms, k + 1)
                v.tensor_tensor(Ga[:, par], Ga[:, par], Gb[:, par], ALU.add).then_inc(g_ready, 1)

            def low(k):
                dve.wait_ge(w_high, k + 1)
                for x in range(2):
                    src = pW[k % 2][x][:]
                    if k < KC:
                        hi_, lo_ = (t[:, k % 2, 4 * x:4 * x + 4, :].rearrange("p k n -> p (k n)") for t in (w_hi, w_lo))
                    elif k == KC:
                        hi_, lo_ = (ag[:, i, 4 * x:4 * x + 4, 0:ER] for i in range(2))
                        src = src.rearrange("p (k n) -> p k n", k=4)
                    else:
                        hi_, lo_ = (lb[:, i, x * 512:(x + 1) * 512] for i in range(2))
                    last = v.scalar_tensor_tensor(lo_, src, WS, hi_, ALU.mult, ALU.subtract)
                if k == KC:
                    last = v.scalar_tensor_tensor(ag[:, 1, :, ER:AGW], pW[1][0][:, 0:KC * NE].rearrange("p (k n) -> p k n", k=KC), WS,
                                                  ag[:, 0, :, ER:AGW], ALU.mult, ALU.subtract)
                last.then_inc(w_low, 1)
            for k in range(NW):
                build(k, k % 2)
                low(k)
            with dve.Fori(NW // 2, NCH // 2) as half:
                build(half * 2, 0)
                build(half * 2 + 1, 1)


def norm_phase(nc, xh, xl, h_dram, k_ident, k_minus):
    with ExitStack() as ctx:
        sb = lambda name, shape, dt=F32: ctx.enter_context(nc.sbuf_tensor(name, shape, dt))
        sem = lambda name: ctx.enter_context(nc.semaphore("n_" + name))
        NB = 4
        ident, minus, eps, carry = sb("n_ident", [P, P]), sb("n_minus", [P, P], F16), sb("n_eps", [P, 1]), sb("n_carry", [P, 1])
        ht, xn = sb("n_ht", [P, NB, HID]), sb("n_xn", [P, 2, HID])
        st, mv, sd, rs = sb("n_st", [P, 2, 2, 6]), sb("n_mv", [P, 2, 2]), sb("n_sd", [P, 2, 1]), sb("n_rs", [P, 2, 1])
        pX = [[ctx.enter_context(nc.psum_tensor(f"n_pX{i}{j}", [P, 4, P], F32)) for j in range(2)] for i in range(2)]
        consts_in, h_in = sem("consts_in"), [sem(f"h_in{i}") for i in range(NB)]
        stats, var_ready, sd_ready, rs_ready, xn_ready, x_t, hi_done, lo_t, lo_done = (sem(x) for x in
            ("stats", "var_ready", "sd_ready", "rs_ready", "xn_ready", "x_t", "hi_done", "lo_t", "lo_done"))
        block = ctx.enter_context(nc.Block())

        def steps(eng, order, fns):
            def step(t, i):
                for name, lag in order:
                    if not isinstance(t, int) or 0 <= t - lag < TILES:
                        fns[name](t - lag, (i - lag) % NB)
            for t in range(NB):
                step(t, t)
            with eng.Fori(1, TILES // NB) as quad:
                for i in range(NB):
                    step(quad * NB + i, i)
            step(TILES, 0)
            step(TILES + 1, 1)

        @block.sync
        def _(sp):
            hv = h_dram.rearrange("(t p) n -> t p n", p=P)
            sp.dma_start(ident[:], k_ident).then_inc(consts_in, 16)
            sp.dma_start(minus[:], k_minus).then_inc(consts_in, 16)

            def load(t, i):
                if not isinstance(t, int) or t >= NB:
                    sp.wait_ge(xn_ready, t - NB + 1)
                sp.dma_start(ht[:, i, :], hv[ds(t, 1)].rearrange("o p n -> (o p) n")).then_inc(h_in[i], 16)
            for t in range(NB):
                load(t, t)
            with sp.Fori(1, TILES // NB) as quad:
                for i in range(NB):
                    load(quad * NB + i, i)

        @block.tensor
        def _(pe):
            def transposes(t, i):
                pe.wait_ge(xn_ready, t + 1)
                from_one(pe, lo_done, t - 1)
                for j in range(KC):
                    last = nc.tensor.matmul(pX[i % 2][j // 4][:, j % 4, :], xn[:, i % 2, j * P:(j + 1) * P], ident[:],
                                            start=(j % 4 == 0), stop=False, is_transpose=True, skip_group_check=True)
                last.then_inc(x_t, 1)

            def take_off(t, i):
                pe.wait_ge(hi_done, t + 1)
                for j in range(2):
                    for c in range(4):
                        last = nc.tensor.matmul(pX[i % 2][j][:, c, :], minus[:], xh[:, 4 * j + c, ds(t * P, P)],
                                                start=False, stop=(c == 3), skip_group_check=True)
                last.then_inc(lo_t, 1)
            pe.wait_ge(consts_in, 32)
            steps(pe, [("t", 0), ("o", 1)], {"t": transposes, "o": take_off})

        @block.scalar
        def _(act):
            a = nc.scalar.activation

            def root(t, i):
                act.wait_ge(var_ready, t + 1)
                a(sd[:, i % 2, :], mv[:, i % 2, 1:2], ACT.Sqrt, bias=eps[:]).then_inc(sd_ready, 1)

            def high(t, i):
                act.wait_ge(x_t, t + 1)
                for j in range(2):
                    last = a(xh[:, 4 * j:4 * j + 4, ds(t * P, P)], pX[i % 2][j][:], ACT.Copy)
                last.then_inc(hi_done, 1)

            def low(t, i):
                act.wait_ge(lo_t, t + 1)
                for j in range(2):
                    last = a(xl[:, 4 * j:4 * j + 4, ds(t * P, P)], pX[i % 2][j][:], ACT.Copy)
                last.then_inc(lo_done, 1)
            steps(act, [("r", 0), ("h", 0), ("l", 1)], {"r": root, "h": high, "l": low})

        @block.vector
        def _(dve):
            v = nc.vector
            v.memset(eps[:], EPS)

            def moments(t, i):
                dve.wait_ge(h_in[i], (t - i) * (16 // NB) + 16)
                from_one(dve, sd_ready, t - 1)
                for j in range(2):
                    last = v.bn_stats(st[:, i % 2, j, :], ht[:, i, j * 512:(j + 1) * 512])
                last.then_inc(stats, 1)
                dve.wait_ge(stats, t + 1)
                v.memset(carry[:], 0.0)
                v.bn_aggr(mv[:, i % 2, :], st[:, i % 2]).then_inc(var_ready, 1)

            def normalise(t, i):
                dve.wait_ge(sd_ready, t + 1)
                v.reciprocal(rs[:, i % 2, :], sd[:, i % 2, :]).then_inc(rs_ready, 1)
                dve.wait_ge(rs_ready, t + 1)
                dve.wait_ge(var_ready, t + 1)
                from_one(dve, x_t, t - 1)
                v.tensor_scalar(xn[:, i % 2, :], ht[:, i, :], mv[:, i % 2, 0:1], rs[:, i % 2, :], ALU.subtract,
                                ALU.mult).then_inc(xn_ready, 1)
            steps(dve, [("m", 0), ("n", 1)], {"m": moments, "n": normalise})


def attention_phase(nc, xh, xl, Wg, WoS, Wq, Wk, Wv, Wo, k_ident, k_rope, k_masks, k_cum, ot_dram, wo_dram):
    with ExitStack() as ctx:
        sb = lambda name, shape, dt=F32: ctx.enter_context(nc.sbuf_tensor(name, shape, dt))
        pb = lambda name, shape, dt=F32: ctx.enter_context(nc.psum_tensor(name, shape, dt))
        sem = lambda name: ctx.enter_context(nc.semaphore(name))
        H2 = GRP // 2
        ident, rope = sb("ident", [P, P]), sb("rope", [P, 6, DH // 2])
        masks, cum = sb("masks", [P, 2, POS]), sb("cum", [P, P])
        wst, ost = sb("wst", [P, 4, GW]), sb("ost", [P, HID])
        oh, ol = sb("oh", [P, HID], F16), sb("ol", [P, HID], F16)
        K = sb("K", [P, 2, DH])
        Vz = sb("Vz", [P, 4, 2, DH])
        kabs, kexp, kln, gate = (sb(n, [P, 2, DH]) for n in ("kabs", "kexp", "kln", "gate"))
        eG, eGn = sb("eG", [P, 2, DH]), sb("eGn", [P, 2, DH])
        qmx, qnb, qsum, qrs = (sb(n, [P, 2, GRP]) for n in ("qmx", "qnb", "qsum", "qrs"))
        kmx, knb, ksum, krs = (sb(n, [P, 2, 1]) for n in ("kmx", "knb", "ksum", "krs"))
        smx, snb, ssum, srs = (sb(n, [P, 2, 4]) for n in ("smx", "snb", "ssum", "srs"))
        E, Ek = sb("E", [P, 2, GRP, DH]), sb("Ek", [P, 2, DH])
        t1, t2 = sb("t1", [P, GRP, 2, DH // 2]), sb("t2", [P, GRP, 2, DH // 2])
        kt1, kt2 = sb("kt1", [P, 2, DH // 2]), sb("kt2", [P, 2, DH // 2])
        QR, QD = sb("QR", [P, 2, GRP, DH]), sb("QD", [P, 2, GRP, DH])
        KR, KD = sb("KR", [P, 2, DH]), sb("KD", [P, 2, DH])
        QT, ET = sb("QT", [P, 2, 2, GRP, POS], F16), sb("ET", [P, 2, GRP, POS])
        KRT, KDT = sb("KRT", [P, 2, P], F16), sb("KDT", [P, P])
        S2, L, Es, PR = (sb(n, [P, 2, 4, POS]) for n in ("S2", "L", "Es", "PR"))
        PT = sb("PT", [P, 2, H2, P])
        OT = sb("OT", [P, 2, GRP, 2, POS], BF16)

        QP = [pb(f"QP{i}", [P, QW]) for i in range(2)]
        KVP = pb("KVP", [P, 512])
        TQ, TE = pb("TQ", [P, GRP, P]), pb("TE", [P, GRP, P])
        KG = pb("KG", [P, 4, P])
        SC = pb("SC", [P, 2, 4, POS])
        OP = pb("OP", [P, 2, GRP, POS])
        PTP = KVP[:, 256:512].rearrange("p (h n) -> p h n", h=H2)

        consts_in, z_ready, w_high, w_ready = (sem(n) for n in ("consts_in", "z_ready", "w_high", "w_ready"))
        w_in = [sem(f"w_in{i}") for i in range(4)]
        wo_in, wo_high, wo_ready, wo_out, wo_kept = (sem(n) for n in ("wo_in", "wo_high", "wo_ready", "wo_out", "wo_kept"))
        rows = lambda W: W.rearrange("(c p) n -> c p n", p=P)
        kv_done, kv_copied, q_done = sem("kv_done"), sem("kv_copied"), sem("q_done")
        qmax_raw, qmax_ready, q_read, qexp_done, q_terms, q_roped, qrs_ready, q_decayed = (sem(n) for n in
            ("qmax_raw", "qmax_ready", "q_read", "qexp_done", "q_terms", "q_roped", "qrs_ready", "q_decayed"))
        kmax_raw, kmax_ready, kexp_done, k_terms, k_roped, krs_ready, k_decayed = (sem(n) for n in
            ("kmax_raw", "kmax_ready", "kexp_done", "k_terms", "k_roped", "krs_ready", "k_decayed"))
        kabs_done, knegexp_done, kln_done, gate_ready, G_done, eG_done = (sem(n) for n in
            ("kabs_done", "knegexp_done", "kln_done", "gate_ready", "G_done", "eG_done"))
        t_done, kt_done, qt_copied, kt_high, kt_copied, qt_low = (sem(n) for n in
            ("t_done", "kt_done", "qt_copied", "kt_high", "kt_copied", "qt_low"))
        sc_done, s_read, smax_raw, smax_ready, sexp_done, srs_ready, p_ready = (sem(n) for n in
            ("sc_done", "s_read", "smax_raw", "smax_ready", "sexp_done", "srs_ready", "p_ready"))
        pt_done, pt_copied, o_done, o_copied, o_out0 = (sem(n) for n in ("pt_done", "pt_copied", "o_done", "o_copied", "o_out0"))
        o_out = [o_out0, sem("o_out1")]
        block = ctx.enter_context(nc.Block())
        LASTU = (KVH - 1) * TILES // 4

        def steps(eng, order, weights, fns):
            def step(n, i, piece=None):
                for name, lag in order:
                    if name == "w":
                        if piece:
                            weights(*piece)
                    elif not isinstance(n, int) or 0 <= n - lag < STEPS:
                        fns[name](n - lag, (i - lag) % 4)

            def quads(quad, more):
                for i in range(4):
                    step(quad * 4 + i, i, (quad, i, more))
            quads(0, True)
            with eng.Fori(1, LASTU) as quad:
                quads(quad, True)
            with eng.Fori(LASTU, STEPS // 4) as quad:
                quads(quad, False)
            step(STEPS, 0)
            step(STEPS + 1, 1)
            step(STEPS + 2, 2)

        @block.sync
        def _(sp):
            sp.dma_start(ident[:], k_ident).then_inc(consts_in, 16)
            sp.dma_start(rope[:].rearrange("p a b -> p (a b)"), k_rope).then_inc(consts_in, 16)
            sp.dma_start(masks[:].rearrange("p a b -> p (a b)"), k_masks).then_inc(consts_in, 16)
            sp.dma_start(cum[:], k_cum).then_inc(consts_in, 16)

            def store(n, par):
                sp.wait_ge(o_copied, n + 1)
                g, t = n // TILES, n % TILES
                dst = ot_dram[ds(t, 1), :, ds(g, 1), :].rearrange("o d u m -> (o d) (u m)")
                sp.dma_start(dst, OT[:, par].rearrange("p h b t -> p (h b t)")).then_inc(o_out[par], 16)
            with sp.Fori(0, STEPS // 2) as half:
                for i in range(2):
                    store(half * 2 + i, i)
            for s in o_out:
                sp.wait_ge(s, 16 * STEPS // 2)

        @block.gpsimd
        def _(pool):
            nc.gpsimd.memset(Vz[:], 0.0).then_inc(z_ready, 1)

            def load_chunk(g, c, slot):
                for W, at, n in ((Wq, 0, QW), (Wk, QW, DH), (Wv, QW + DH, DH)):
                    src = rows(W)[ds(c, 1), :, ds(g * n, n)].rearrange("o p n -> (o p) n")
                    pool.dma_start(wst[:, slot, at:at + n], src).then_inc(w_in[slot], 16)

            def unit(u, more):
                if more:
                    for i in range(2):
                        pool.wait_ge(w_ready, 5 + i if isinstance(u, int) else KC - 1 + 2 * u + i)
                        load_chunk(u // 4 + 1, (u % 4) * 2 + i, i)
                from_one(pool, wo_ready, u)
                pool.dma_start(ost[:], rows(Wo)[ds(u, 1)].rearrange("o p n -> (o p) n")).then_inc(wo_in, 16)
                pool.wait_ge(wo_ready, u + 1)
                for x, part in enumerate((oh, ol)):
                    pool.dma_start(wo_dram[x, :, ds(u, 1), :].rearrange("p o n -> p (o n)"), part[:]).then_inc(wo_out, 16)
            for c in range(KC):
                from_one(pool, w_ready, c - 3)
                load_chunk(0, c, c % 4)
            unit(0, True)
            with pool.Fori(1, LASTU) as u:
                unit(u, True)
            pool.wait_ge(wo_out, 32 * LASTU)
            pool.wait_ge(q_done, (KVH - 1) * TILES)
            for part in range(KEPT):
                for x in range(2):
                    pool.dma_start(WoS[part][:, x], wo_dram[x, :, part * PART:(part + 1) * PART, :]).then_inc(wo_kept, 16)
            with pool.Fori(LASTU, HEADS) as u:
                unit(u, False)
            pool.wait_ge(wo_out, 32 * HEADS)
            pool.wait_ge(wo_kept, 32 * KEPT)

        @block.tensor
        def _(pe):
            mm = nc.tensor.matmul

            def project(out, n, cols, chunks):
                g = n // TILES
                tok = ds((n % TILES) * P, P)
                par = g % 2
                for c in chunks:
                    wv = [Wg[:, ds(par, 1), i, c, cols].rearrange("p o n -> p (o n)") for i in range(2)]
                    mm(out, xh[:, c, tok], wv[0], start=(c == 0), stop=False, skip_group_check=True)
                    mm(out, xh[:, c, tok], wv[1], start=False, stop=False, skip_group_check=True)
                    last = mm(out, xl[:, c, tok], wv[0], start=False, stop=(c == KC - 1), skip_group_check=True)
                return last

            def kv(n, s):
                pe.wait_ge(w_ready, (n // TILES + 1) * KC)
                from_one(pe, kv_copied, n)
                project(KVP[:, 0:KVW], n, slice(QW, GW), range(KC)).then_inc(kv_done, 1)

            def transposes(n, s):
                p = s % 2
                pe.wait_ge(q_roped, n + 1)
                pe.wait_ge(q_decayed, n + 1)
                pe.wait_ge(k_roped, n + 1)
                pe.wait_ge(k_decayed, n + 1)
                from_one(pe, qt_copied, 2 * n)
                from_one(pe, kt_copied, n)
                from_one(pe, qt_low, n)
                nc.tensor.transpose(KG[:, 1, :], KR[:, p, :], ident[:])
                nc.tensor.transpose(KG[:, 2, :], KD[:, p, :], ident[:]).then_inc(kt_done, 1)
                for h in range(GRP):
                    nc.tensor.transpose(TQ[:, h, :], QR[:, p, h, :], ident[:])
                for h in range(GRP):
                    last = nc.tensor.transpose(TE[:, h, :], QD[:, p, h, :], ident[:])
                last.then_inc(t_done, 1)

            def q_first(n, s):
                if not isinstance(n, int) or n >= 2:
                    pe.wait_ge(q_read, n - 1)
                    pe.wait_ge(qexp_done, n - 1)
                project(QP[s % 2][:], n, slice(0, QW), range(KC // 2))

            def q_fifth(n, s):
                project(QP[s % 2][:], n, slice(0, QW), [KC // 2])

            def q_sixth(n, s):
                project(QP[s % 2][:], n, slice(0, QW), [KC // 2 + 1])

            def q_last(n, s):
                project(QP[s % 2][:], n, slice(0, QW), range(KC - 2, KC)).then_inc(q_done, 1)

            def cumulate(n, s):
                pe.wait_ge(gate_ready, n + 1)
                from_one(pe, eG_done, n)
                from_one(pe, kt_copied, n)
                mm(KG[:, 0, :], cum[:], gate[:, s % 2, :], start=True, stop=True, skip_group_check=True).then_inc(G_done, 1)

            def scores(n, s):
                pe.wait_ge(qt_copied, 2 * (n + 1))
                pe.wait_ge(qt_low, n + 1)
                pe.wait_ge(kt_copied, n + 1)
                from_one(pe, s_read, n)
                for hp in range(H2):
                    for b in range(2):
                        keys = slice(b * POS, (b + 1) * POS)
                        rows = lambda t: t[:, b, 2 * hp:2 * hp + 2, :].rearrange("p h t -> p (h t)")
                        for i, (x, y) in enumerate(((0, 0), (0, 1), (1, 0))):
                            mm(SC[:, 0, 2 * hp + b, :], rows(QT[:, x]), KRT[:, y, keys], start=(i == 0), stop=(i == 2),
                               skip_group_check=True)
                        last = mm(SC[:, 1, 2 * hp + b, :], rows(ET), KDT[:, keys], start=True, stop=True, skip_group_check=True)
                last.then_inc(sc_done, 1)

            def p_transpose(n, s):
                pe.wait_ge(p_ready, n + 1)
                pe.wait_ge(kv_copied, n + 3 if not isinstance(n, int) else min(n + 3, STEPS))
                from_one(pe, pt_copied, n)
                for hp in range(H2):
                    last = nc.tensor.transpose(PTP[:, hp, :], PR[:, s % 2, 2 * hp:2 * hp + 2, :].rearrange("p b t -> p (b t)"), ident[:])
                last.then_inc(pt_done, 1)

            def values(n, s):
                pe.wait_ge(pt_copied, n + 1)
                pe.wait_ge(kv_copied, n + 1)
                from_one(pe, o_copied, n)
                for b in range(2):
                    last = mm(OP[:, b].rearrange("p h t -> p (h t)"), Vz[:, s, b, :], PT[:, s % 2].rearrange("p h n -> p (h n)"),
                              start=True, stop=True, skip_group_check=True)
                last.then_inc(o_done, 1)

            pe.wait_ge(consts_in, 64)
            steps(pe, [("kv", 0), ("qa", 0), ("t", 1), ("q5", 0), ("G", 0), ("q6", 0), ("pt", 2), ("qc", 0), ("v", 2), ("s", 1)], None,
                  {"kv": kv, "qa": q_first, "G": cumulate, "q5": q_fifth, "q6": q_sixth, "qc": q_last, "t": transposes, "s": scores,
                   "pt": p_transpose, "v": values})

        @block.scalar
        def _(act):
            a = nc.scalar.activation

            def q_exp(n, s):
                p = s % 2
                act.wait_ge(q_done, n + 1)
                act.wait_ge(qmax_ready, n + 1)
                from_one(act, q_decayed, n - 1)
                for h in range(GRP):
                    last = a(E[:, p, h, :], QP[p][:, h * DH:(h + 1) * DH], ACT.Exp, bias=qnb[:, p, h:h + 1], scale=1.0 / WS,
                             accum_out=qsum[:, p, h:h + 1])
                last.then_inc(qexp_done, 1)

            def s_exp(n, s):
                p = s % 2
                act.wait_ge(smax_ready, n + 1)
                from_one(act, p_ready, n - 1)
                for j in range(4):
                    last = a(Es[:, p, j, :], S2[:, p, j, :], ACT.Exp, bias=snb[:, p, j:j + 1], scale=SCORE, accum_out=ssum[:, p, j:j + 1])
                last.then_inc(sexp_done, 1)

            def kv_copy(n, s):
                p = s % 2
                act.wait_ge(kv_done, n + 1)
                if not isinstance(n, int) or n >= 2:
                    act.wait_ge(k_roped, n - 1)
                    act.wait_ge(gate_ready, n - 1)
                if not isinstance(n, int) or n >= 4:
                    act.wait_ge(o_done, n - 3)
                a(K[:, p, :], KVP[:, 0:DH], ACT.Copy, scale=1.0 / WS)
                for b in range(2):
                    r = slice(b * POS, (b + 1) * POS)
                    last = a(Vz[r, s, b, :], KVP[r, DH:2 * DH], ACT.Copy, scale=1.0 / WS)
                last.then_inc(kv_copied, 1)

            def gates(n, s):
                p = s % 2
                act.wait_ge(kv_copied, n + 1)
                a(kabs[:, p, :], K[:, p, :], ACT.Abs).then_inc(kabs_done, 1)
                act.wait_ge(kabs_done, n + 1)
                a(kexp[:, p, :], kabs[:, p, :], ACT.Exp, scale=-1.0).then_inc(knegexp_done, 1)
                act.wait_ge(knegexp_done, n + 1)
                a(kln[:, p, :], kexp[:, p, :], ACT.Ln, bias=1.0).then_inc(kln_done, 1)
                act.wait_ge(kmax_ready, n + 1)
                from_one(act, k_decayed, n - 1)
                a(Ek[:, p, :], K[:, p, :], ACT.Exp, bias=knb[:, p, :], accum_out=ksum[:, p, :]).then_inc(kexp_done, 1)

            def t_copy(n, s):
                act.wait_ge(t_done, n + 1)
                from_one(act, sc_done, n)
                for src, dst in ((TQ, QT[:, 0]), (TE, ET[:])):
                    a(dst.rearrange("p b h t -> p h b t"), src[:].rearrange("p h (b t) -> p h b t", b=2), ACT.Copy).then_inc(qt_copied, 1)

            def decays(n, s):
                p = s % 2
                act.wait_ge(G_done, n + 1)
                if not isinstance(n, int) or n >= 2:
                    act.wait_ge(q_decayed, n - 1)
                    act.wait_ge(k_decayed, n - 1)
                a(eG[:, p, :], KG[:, 0, :], ACT.Exp)
                a(eGn[:, p, :], KG[:, 0, :], ACT.Exp, scale=-1.0).then_inc(eG_done, 1)

            def o_copy(n, s):
                act.wait_ge(o_done, n + 1)
                if not isinstance(n, int) or n >= 2:
                    act.wait_ge(o_out[s % 2], turns(n - 2, s % 2, 16))
                a(OT[:, s % 2].rearrange("p h b t -> p b h t"), OP[:], ACT.Copy, scale=0.5).then_inc(o_copied, 1)

            def w_piece(u, i, more):
                if i < 2 and more:
                    act.wait_ge(w_in[i], 3 * 16 * 2 + 3 * 16 * (u + 1))
                    g, c = u // 4 + 1, (u % 4) * 2 + i
                    a(Wg[:, ds(g % 2, 1), 0, ds(c, 1), :].rearrange("p a b n -> p (a b n)"), wst[:, i, :], ACT.Copy,
                      scale=WS).then_inc(w_high, 1)
                if i == 2:
                    act.wait_ge(wo_in, 16 * (u + 1))
                    from_one(act, wo_out, 32 * u)
                    a(oh[:], ost[:], ACT.Copy, scale=WS).then_inc(wo_high, 1)

            act.preload_act_table_set("natural_log_exp_and_others")
            for c in range(KC):
                act.wait_ge(w_in[c % 4], 3 * 16 * (c // 4 + 1))
                a(Wg[:, 0, 0, c, :], wst[:, c % 4, :], ACT.Copy, scale=WS).then_inc(w_high, 1)
            act.wait_ge(z_ready, 1)
            steps(act, [("qe", 1), ("o", 3), ("se", 2), ("kvc", 0), ("g", 0), ("tc", 1), ("d", 0), ("w", 0)], w_piece,
                  {"kvc": kv_copy, "g": gates, "d": decays, "qe": q_exp, "tc": t_copy, "se": s_exp, "o": o_copy})

        @block.vector
        def _(dve):
            v = nc.vector

            def rope_tab(i, dims):
                t = rope[:, i, :]
                for _ in range(len(dims) - 2):
                    t = t.unsqueeze(1)
                return t.broadcast_to(dims)

            def q_max(n, s):
                p = s % 2
                dve.wait_ge(q_done, n + 1)
                from_one(dve, qexp_done, n - 1)
                v.tensor_reduce(qmx[:, p, :], QP[p][:].rearrange("p (h d) -> p h d", h=GRP), X, ALU.max).then_inc(qmax_raw, 1)
                dve.wait_ge(qmax_raw, n + 1)
                v.tensor_scalar(qnb[:, p, :], qmx[:, p, :], -1.0 / WS, None, ALU.mult).then_inc(qmax_ready, 1)

            def q_rope(n, s):
                p = s % 2
                q4 = QP[p][:].rearrange("p (h x d) -> p h x d", h=GRP, x=2)
                dve.wait_ge(qexp_done, n + 1)
                from_one(dve, q_roped, n)
                v.tensor_tensor(t1[:], q4, rope_tab(3, [P, GRP, 2, DH // 2]), ALU.mult)
                v.tensor_tensor(t2[:, :, 0, :], q4[:, :, 1, :], rope_tab(5, [P, GRP, DH // 2]), ALU.mult)
                v.tensor_tensor(t2[:, :, 1, :], q4[:, :, 0, :], rope_tab(4, [P, GRP, DH // 2]), ALU.mult).then_inc(q_read, 1)
                dve.wait_ge(q_read, n + 1)
                from_one(dve, t_done, n - 1)
                v.tensor_tensor(QR[:, p].rearrange("p h d -> p (h d)"), t1[:].rearrange("p h x d -> p (h x d)"),
                                t2[:].rearrange("p h x d -> p (h x d)"), ALU.add).then_inc(q_roped, 1)

            def q_decay(n, s):
                p = s % 2
                dve.wait_ge(qexp_done, n + 1)
                dve.wait_ge(eG_done, n + 1)
                v.reciprocal(qrs[:, p, :], qsum[:, p, :]).then_inc(qrs_ready, 1)
                dve.wait_ge(qrs_ready, n + 1)
                for h in range(GRP):
                    last = v.scalar_tensor_tensor(QD[:, p, h, :], E[:, p, h, :], qrs[:, p, h:h + 1], eG[:, p, :], ALU.mult, ALU.mult)
                last.then_inc(q_decayed, 1)

            def s_soft(n, s):
                p = s % 2
                dve.wait_ge(sc_done, n + 1)
                from_one(dve, sexp_done, n - 1)
                mk = lambda i: masks[:, i, :].unsqueeze(1).broadcast_to([P, 4, POS])
                v.tensor_tensor(S2[:, p], SC[:, 0], mk(0), ALU.add)
                v.scalar_tensor_tensor(L[:, p], SC[:, 1], BIG, mk(1), ALU.min, ALU.mult).then_inc(s_read, 1)
                dve.wait_ge(s_read, n + 1)
                v.tensor_reduce(smx[:, p, :], S2[:, p], X, ALU.max).then_inc(smax_raw, 1)
                dve.wait_ge(smax_raw, n + 1)
                v.tensor_scalar(snb[:, p, :], smx[:, p, :], -SCORE, None, ALU.mult).then_inc(smax_ready, 1)

            def s_prob(n, s):
                p = s % 2
                dve.wait_ge(sexp_done, n + 1)
                v.reciprocal(srs[:, p, :], ssum[:, p, :]).then_inc(srs_ready, 1)
                dve.wait_ge(srs_ready, n + 1)
                from_one(dve, pt_done, n - 1)
                for j in range(4):
                    last = v.scalar_tensor_tensor(PR[:, p, j, :], Es[:, p, j, :], srs[:, p, j:j + 1], L[:, p, j, :], ALU.mult, ALU.add)
                last.then_inc(p_ready, 1)

            def k_rope(n, s):
                p = s % 2
                dve.wait_ge(kv_copied, n + 1)
                from_one(dve, kexp_done, n - 1)
                v.tensor_reduce(kmx[:, p, :], K[:, p, :], X, ALU.max).then_inc(kmax_raw, 1)
                k3 = K[:, p, :].rearrange("p (x d) -> p x d", x=2)
                from_one(dve, k_roped, n)
                v.tensor_tensor(kt1[:], k3, rope_tab(0, [P, 2, DH // 2]), ALU.mult)
                dve.wait_ge(kmax_raw, n + 1)
                v.tensor_scalar(knb[:, p, :], kmx[:, p, :], -1.0, None, ALU.mult).then_inc(kmax_ready, 1)
                v.tensor_tensor(kt2[:, 0, :], k3[:, 1, :], rope[:, 2, :], ALU.mult)
                v.tensor_tensor(kt2[:, 1, :], k3[:, 0, :], rope[:, 1, :], ALU.mult).then_inc(k_terms, 1)
                dve.wait_ge(k_terms, n + 1)
                from_one(dve, t_done, n - 1)
                v.tensor_tensor(KR[:, p, :], kt1[:].rearrange("p x d -> p (x d)"), kt2[:].rearrange("p x d -> p (x d)"),
                                ALU.add).then_inc(k_roped, 1)
                dve.wait_ge(kln_done, n + 1)
                from_one(dve, G_done, n - 1)
                v.scalar_tensor_tensor(gate[:, p, :], K[:, p, :], 0.0, kln[:, p, :], ALU.min, ALU.subtract).then_inc(gate_ready, 1)

            def k_tcopy(n, s):
                dve.wait_ge(kt_done, n + 1)
                from_one(dve, sc_done, n)
                v.tensor_copy(KRT[:, 0, :], KG[:, 1, :]).then_inc(kt_high, 1)
                v.tensor_copy(KDT[:], KG[:, 2, :])
                dve.wait_ge(kt_high, n + 1)
                v.tensor_tensor(KRT[:, 1, :], KG[:, 1, :], KRT[:, 0, :], ALU.subtract).then_inc(kt_copied, 1)

            def q_tlow(n, s):
                dve.wait_ge(qt_copied, 2 * n + 1)
                v.tensor_tensor(QT[:, 1].rearrange("p b h t -> p h b t"), TQ[:].rearrange("p h (b t) -> p h b t", b=2),
                                QT[:, 0].rearrange("p b h t -> p h b t"), ALU.subtract).then_inc(qt_low, 1)

            def k_decay(n, s):
                p = s % 2
                dve.wait_ge(kexp_done, n + 1)
                dve.wait_ge(eG_done, n + 1)
                v.reciprocal(krs[:, p, :], ksum[:, p, :]).then_inc(krs_ready, 1)
                dve.wait_ge(krs_ready, n + 1)
                from_one(dve, t_done, n - 1)
                v.scalar_tensor_tensor(KD[:, p, :], Ek[:, p, :], krs[:, p, :], eGn[:, p, :], ALU.mult, ALU.mult).then_inc(k_decayed, 1)

            def pt_copy(n, s):
                dve.wait_ge(pt_done, n + 1)
                from_one(dve, o_done, n - 1)
                v.tensor_copy(PT[:, s % 2], PTP).then_inc(pt_copied, 1)

            def w_piece(u, i, more):
                if i < 2 and more:
                    dve.wait_ge(w_high, KC + 1 + 2 * u + i)
                    g, c = u // 4 + 1, (u % 4) * 2 + i
                    hi, lo = (Wg[:, ds(g % 2, 1), x, ds(c, 1), :].rearrange("p a b n -> p (a b n)") for x in range(2))
                    v.scalar_tensor_tensor(lo, wst[:, i, :], WS, hi, ALU.mult, ALU.subtract).then_inc(w_ready, 1)
                if i == 2:
                    dve.wait_ge(wo_high, u + 1)
                    v.scalar_tensor_tensor(ol[:], ost[:], WS, oh[:], ALU.mult, ALU.subtract).then_inc(wo_ready, 1)

            for c in range(KC):
                dve.wait_ge(w_high, c + 1)
                v.scalar_tensor_tensor(Wg[:, 0, 1, c, :], wst[:, c % 4, :], WS, Wg[:, 0, 0, c, :], ALU.mult,
                                       ALU.subtract).then_inc(w_ready, 1)
            dve.wait_ge(consts_in, 64)
            steps(dve, [("qm", 1), ("ss", 2), ("qr", 1), ("qd", 1), ("kr", 0), ("ktc", 1), ("sp", 2), ("qtl", 1), ("kd", 0), ("ptc", 2), ("w", 0)], w_piece,
                  {"kr": k_rope, "kd": k_decay, "qm": q_max, "qr": q_rope, "qd": q_decay, "ktc": k_tcopy, "qtl": q_tlow, "ss": s_soft,
                   "sp": s_prob, "ptc": pt_copy})


def output_phase(nc, WoS, h_dram, ot_dram, wo_dram, bt_dram, ag_dram, lb_dram, base_b, k_ident, k_before, out):
    with ExitStack() as ctx:
        sb = lambda name, shape, dt=F32: ctx.enter_context(nc.sbuf_tensor(name, shape, dt))
        pb = lambda name, shape, dt=F32: ctx.enter_context(nc.psum_tensor(name, shape, dt))
        sem = lambda name: ctx.enter_context(nc.semaphore(name))
        HALF = HID // 2
        ident, before, eps = sb("o_ident", [P, P]), sb("o_before", [P, NE, NE]), sb("o_eps", [P, 1])
        carry = sb("o_carry", [P, 1])
        BT = sb("o_BT", [P, 2, KC, HID], F16)
        AG = sb("o_AG", [P, 2, KC, AGW], F16)
        LB = sb("o_LB", [P, 2, HID], F16)
        bias = sb("o_bias", [P, HID])
        oT = sb("o_oT", [P, 4, HEADS // 2, P], BF16)
        ht = sb("o_ht", [P, 2, HID])
        xn = sb("o_xn", [P, HID])
        x2h, x2l = sb("o_x2h", [P, KC, P], F16), sb("o_x2l", [P, KC, P], F16)
        st, mv, sd, rs = sb("o_st", [P, 2, 6]), sb("o_mv", [P, 2]), sb("o_sd", [P, 1]), sb("o_rs", [P, 1])
        lg, top, ntop = sb("o_lg", [P, NE]), sb("o_top", [P, 1]), sb("o_ntop", [P, 1])
        gt_, eq_ = sb("o_gt", [P, NE, NE]), sb("o_eq", [P, NE, NE])
        rank, sel, ew, wsum, wr, wf = (sb("o_" + x, [P, n]) for x, n in (("rank", NE), ("sel", NE), ("ew", NE), ("wsum", 1), ("wr", 1), ("wf", NE)))
        lw = sb("o_lw", [P, NE, RANK])
        lwh, lwl = sb("o_lwh", [P, P], F16), sb("o_lwl", [P, P], F16)
        Y = [pb(f"o_Y{i}", [P, HALF]) for i in range(2)]
        XT = [pb(f"o_XT{i}", [P, 4, P]) for i in range(2)]
        F = [pb(f"o_F{i}", [P, HALF]) for i in range(2)]
        LG, LWT = pb("o_LG", [P, 512]), pb("o_LWT", [P, 512])

        consts_in, ffn_in = sem("o_consts_in"), sem("o_ffn_in")
        h_in, out_done = ([sem(f"o_{x}{i}") for i in range(2)] for x in ("h_in", "out_done"))
        o_in = [sem(f"o_o_in{i}") for i in range(4)]
        wo_in = [sem(f"o_wo_in{i}") for i in range(KEPT, PARTS)]
        o_used, y_done, h2_ready, stats, var_ready, sd_ready, rs_ready, xn_ready, x_t, x_hi, x_lo = (sem("o_" + x) for x in
            ("o_used", "y_done", "h2_ready", "stats", "var_ready", "sd_ready", "rs_ready", "xn_ready", "x_t", "x_hi", "x_lo"))
        lg_done, link, ew_ready, lw_ready, lw_t, lw_hi, lw_lo, f_done, hb_ready, fin_ready, top_ready = (sem("o_" + x) for x in
            ("lg_done", "link", "ew_ready", "lw_ready", "lw_t", "lw_hi", "lw_lo", "f_done", "hb_ready", "fin_ready", "top_ready"))
        link2 = sem("o_link2")
        block = ctx.enter_context(nc.Block())

        def steps(order, fns):
            def step(t, par):
                for name, lag in order:
                    if not isinstance(t, int) or 0 <= t - lag < TILES:
                        fns[name](t - lag, (par + lag) % 2)
            return step

        def run(eng, order, fns):
            step = steps(order, fns)
            for name, lag in order:
                if name not in ("ya", "yb", "r"):
                    fns[name](1 - lag, (1 + lag) % 2)
            with eng.Fori(1, TILES // 2) as half:
                step(half * 2, 0)
                step(half * 2 + 1, 1)
            step(TILES, 0)

        @block.sync
        def _(sp):
            ov = ot_dram.rearrange("t d g m -> t d (g m)").rearrange("t d (x m) -> t d x m", x=2)
            hv = h_dram.rearrange("(t p) n -> t p n", p=P)

            def load(t, par):
                if not isinstance(t, int) or t >= 2:
                    sp.wait_ge(o_used, t - 1)
                for x in range(2):
                    sp.dma_start(oT[:, 2 * par + x].rearrange("p h n -> p (h n)"),
                                 ov[ds(t, 1), :, x, :].rearrange("o d m -> (o d) m")).then_inc(o_in[2 * par + x], 16)
                if not isinstance(t, int) or t >= 2:
                    sp.wait_ge(out_done[par], turns(t - 2, par, 16))
                sp.dma_start(ht[:, par, :], hv[ds(t, 1)].rearrange("o p n -> (o p) n")).then_inc(h_in[par], 16)
            load(0, 0)
            load(1, 1)
            for part in range(KEPT, PARTS):
                for x in range(2):
                    sp.dma_start(WoS[part][:, x], wo_dram[x, :, part * PART:(part + 1) * PART, :]).then_inc(wo_in[part - KEPT], 16)
            for x in range(2):
                sp.dma_start(BT[:, x], bt_dram[x]).then_inc(ffn_in, 16)
            sp.dma_start(AG[:].rearrange("p x k n -> p x (k n)"), ag_dram.rearrange("x p k n -> p x (k n)")).then_inc(ffn_in, 16)
            sp.dma_start(LB[:], lb_dram.rearrange("x p n -> p x n")).then_inc(ffn_in, 16)
            with sp.Fori(1, TILES // 2) as half:
                load(half * 2, 0)
                load(half * 2 + 1, 1)

        @block.tensor
        def _(pe):
            mm = nc.tensor.matmul

            def products(out, par, k):
                for i in range(2):
                    for y in range(2):
                        last = mm(out[y][:], oT[:, 2 * par + k // (HEADS // 2), k % (HEADS // 2), :],
                                  WoS[k // PART][:, i, k % PART, y * HALF:(y + 1) * HALF],
                                  start=(k == 0 and i == 0), stop=(k == HEADS - 1 and i == 1))
                return last

            def project(t, par, x):
                pe.wait_ge(o_in[2 * par + x], turns(t, par, 16))
                if x == 0:
                    pe.wait_ge(h2_ready, t)
                for h in range(HEADS // 2):
                    last = products(Y, par, x * HEADS // 2 + h)
                if x == 1:
                    last.then_inc(o_used, 1)

            def x_transpose(t, par):
                pe.wait_ge(xn_ready, t + 1)
                from_one(pe, x_lo, t)
                for c in range(KC):
                    last = nc.tensor.transpose(XT[c // 4][:, c % 4, :], xn[:, c * P:(c + 1) * P], ident[:])
                last.then_inc(x_t, 1)

            def gates(t, par):
                if isinstance(t, int) and t == 0:
                    pe.wait_ge(ffn_in, 16 * 4)
                pe.wait_ge(x_lo, t + 1)
                from_one(pe, lw_ready, t)
                for c in range(KC):
                    mm(LG[:, 0:AGW], x2h[:, c, :], AG[:, 0, c, :], start=(c == 0), stop=False)
                    mm(LG[:, 0:AGW], x2h[:, c, :], AG[:, 1, c, :], start=False, stop=False)
                    last = mm(LG[:, 0:AGW], x2l[:, c, :], AG[:, 0, c, :], start=False, stop=(c == KC - 1))
                last.then_inc(lg_done, 1)

            def base(t, par):
                from_one(pe, fin_ready, t)
                if isinstance(t, int) and t == 0:
                    pe.wait_ge(h2_ready, 2)
                for y in range(2):
                    cols = slice(y * HALF, (y + 1) * HALF)
                    for c in range(KC):
                        mm(F[y][:], x2h[:, c, :], BT[:, 0, c, cols], start=(c == 0), stop=False)
                        mm(F[y][:], x2h[:, c, :], BT[:, 1, c, cols], start=False, stop=False)
                        mm(F[y][:], x2l[:, c, :], BT[:, 0, c, cols], start=False, stop=False)
                    if y == 0:
                        pe.wait_ge(lw_ready, t + 1)
                        from_one(pe, lw_lo, t)
                        nc.tensor.transpose(LWT[:, 0:P], lw[:].rearrange("p e r -> p (e r)"), ident[:]).then_inc(lw_t, 1)
                pe.wait_ge(lw_lo, t + 1)
                for y in range(2):
                    cols = slice(y * HALF, (y + 1) * HALF)
                    mm(F[y][:], lwh[:], LB[:, 0, cols], start=False, stop=False)
                    mm(F[y][:], lwh[:], LB[:, 1, cols], start=False, stop=False)
                    last = mm(F[y][:], lwl[:], LB[:, 0, cols], start=False, stop=True)
                last.then_inc(f_done, 1)

            for i in range(4):
                pe.wait_ge(o_in[i], 16)
            for part in range(PARTS):
                if part >= KEPT:
                    pe.wait_ge(wo_in[part - KEPT], 32)
                for par, to in enumerate((Y, F)):
                    for k in range(part * PART, (part + 1) * PART):
                        last = products(to, par, k)
                    if part == PARTS - 1:
                        last.then_inc(o_used, 1)
            pe.wait_ge(consts_in, 48)
            run(pe, [("ya", 0), ("xt", 1), ("yb", 0), ("g", 1), ("f", 1)],
                {"ya": lambda t, p: project(t, p, 0), "yb": lambda t, p: project(t, p, 1), "xt": x_transpose, "g": gates, "f": base})

        @block.scalar
        def _(act):
            act.dma_start(ident[:], k_ident).then_inc(consts_in, 16)
            act.dma_start(before[:].rearrange("p a b -> p (a b)"), k_before).then_inc(consts_in, 16)
            act.dma_start(bias[:], base_b.rearrange("(a n) -> a n", a=1).broadcast_to([P, HID])).then_inc(consts_in, 16)
            a = nc.scalar.activation

            def root(t, par):
                act.wait_ge(var_ready, t + 1)
                a(sd[:], mv[:, 1:2], ACT.Sqrt, bias=eps[:]).then_inc(sd_ready, 1)

            def high(t, par):
                act.wait_ge(x_t, t + 1)
                from_one(act, f_done, t)
                for i in range(2):
                    last = a(x2h[:, 4 * i:4 * i + 4, :], XT[i][:], ACT.Copy)
                last.then_inc(x_hi, 1)

            def weigh(t, par):
                act.wait_ge(top_ready, t + 1)
                a(ew[:], lg[:], ACT.Exp, bias=ntop[:]).then_inc(ew_ready, 1)

            def lw_high(t, par):
                act.wait_ge(lw_t, t + 1)
                from_one(act, f_done, t)
                a(lwh[:], LWT[:, 0:P], ACT.Copy).then_inc(lw_hi, 1)

            def store(t, par):
                act.wait_ge(fin_ready, t + 1)
                act.dma_start(out.rearrange("(t p) n -> t p n", p=P)[ds(t, 1)].rearrange("o p n -> (o p) n"),
                              ht[:, par, :]).then_inc(out_done[par], 16)
            root(0, 0)
            root(1, 1)
            run(act, [("h", 1), ("r", 0), ("w", 1), ("l", 1), ("s", 1)],
                {"r": root, "h": high, "w": weigh, "l": lw_high, "s": store})
            for s in out_done:
                act.wait_ge(s, 16 * TILES // 2)

        @block.vector
        def _(dve):
            v = nc.vector
            NL = 6

            def residual(t, par, Y=Y):
                dve.wait_ge(o_used, t + 1)
                dve.wait_ge(h_in[par], turns(t, par, 16))
                for y in range(2):
                    hs = ht[:, par, y * HALF:(y + 1) * HALF]
                    last = v.scalar_tensor_tensor(hs, Y[y][:], 1.0 / WS, hs, ALU.mult, ALU.add)
                last.then_inc(h2_ready, 1)
                dve.wait_ge(h2_ready, t + 1)
                for y in range(2):
                    last = v.bn_stats(st[:, y, :], ht[:, par, y * HALF:(y + 1) * HALF])
                last.then_inc(stats, 1)
                dve.wait_ge(stats, t + 1)
                v.memset(carry[:], 0.0)
                v.bn_aggr(mv[:], st[:]).then_inc(var_ready, 1)

            def normalise(t, par):
                dve.wait_ge(sd_ready, t + 1)
                v.reciprocal(rs[:], sd[:]).then_inc(rs_ready, 1)
                dve.wait_ge(rs_ready, t + 1)
                dve.wait_ge(var_ready, t + 1)
                from_one(dve, x_t, t)
                v.tensor_scalar(xn[:], ht[:, par, :], mv[:, 0:1], rs[:], ALU.subtract, ALU.mult).then_inc(xn_ready, 1)
                dve.wait_ge(xn_ready, t + 1)
                v.tensor_tensor(ht[:, par, :], ht[:, par, :], bias[:], ALU.add).then_inc(hb_ready, 1)

            def low(t, par):
                dve.wait_ge(x_hi, t + 1)
                for i in range(2):
                    last = v.tensor_tensor(x2l[:, 4 * i:4 * i + 4, :], XT[i][:], x2h[:, 4 * i:4 * i + 4, :], ALU.subtract)
                last.then_inc(x_lo, 1)

            def gating(t, par):
                dve.wait_ge(lg_done, t + 1)
                b = NL * t

                def step(i, ins):
                    ins.then_inc(link, 1)
                    dve.wait_ge(link, b + i)
                step(1, v.tensor_scalar(lg[:], LG[:, ER:AGW], 1.0 / WS, None, ALU.mult))
                v.tensor_reduce(top[:], lg[:], X, ALU.max)
                me = lg[:].unsqueeze(2).broadcast_to([P, NE, NE])
                other = lg[:].unsqueeze(1).broadcast_to([P, NE, NE])
                v.tensor_tensor(gt_[:], other, me, ALU.is_gt)
                step(2, v.tensor_tensor(eq_[:], other, me, ALU.is_equal))
                v.tensor_scalar(ntop[:], top[:], -1.0, None, ALU.mult).then_inc(top_ready, 1)
                step(3, v.tensor_tensor(eq_[:], eq_[:], before[:], ALU.mult))
                step(4, v.tensor_tensor(gt_[:], gt_[:], eq_[:], ALU.add))
                step(5, v.tensor_reduce(rank[:], gt_[:], X, ALU.add))
                step(6, v.tensor_scalar(sel[:], rank[:], 1.5, None, ALU.is_lt))

            def weights(t, par):
                dve.wait_ge(ew_ready, t + 1)
                b = 4 * t

                def step(i, ins):
                    ins.then_inc(link2, 1)
                    dve.wait_ge(link2, b + i)
                step(1, v.tensor_tensor(ew[:], ew[:], sel[:], ALU.mult))
                step(2, v.tensor_reduce(wsum[:], ew[:], X, ALU.add))
                step(3, v.reciprocal(wr[:], wsum[:]))
                step(4, v.tensor_scalar(wf[:], ew[:], wr[:], LORA_SCALE / WS, ALU.mult, ALU.mult))
                from_one(dve, lw_t, t)
                v.tensor_tensor(lw[:], LG[:, 0:ER].rearrange("p (e r) -> p e r", e=NE), wf[:].unsqueeze(2).broadcast_to([P, NE, RANK]),
                                ALU.mult).then_inc(lw_ready, 1)

            def lw_low(t, par):
                dve.wait_ge(lw_hi, t + 1)
                v.tensor_tensor(lwl[:], LWT[:, 0:P], lwh[:], ALU.subtract).then_inc(lw_lo, 1)

            def finish(t, par):
                dve.wait_ge(f_done, t + 1)
                dve.wait_ge(hb_ready, t + 1)
                for y in range(2):
                    hs = ht[:, par, y * HALF:(y + 1) * HALF]
                    last = v.scalar_tensor_tensor(hs, F[y][:], 1.0 / WS, hs, ALU.mult, ALU.add)
                last.then_inc(fin_ready, 1)

            v.memset(eps[:], EPS)
            dve.wait_ge(consts_in, 48)
            residual(0, 0)
            normalise(0, 0)
            residual(1, 1, F)
            run(dve, [("lo", 1), ("r", 0), ("g", 1), ("w", 1), ("ll", 1), ("n", 0), ("f", 1)],
                {"r": residual, "n": normalise, "lo": low, "g": gating, "w": weights, "ll": lw_low, "f": finish})


def block_kernel(nc, x, abslog, phase, Wq, Wk, Wv, Wo, gate_w, base_w, base_b, lora_A, lora_B,
                 k_ident, k_minus, k_rope, k_masks, k_cum, k_mult, k_before, out):
    scratch = lambda name, shape, dt: nc.dram_tensor(name, shape, dt).ap()
    h_dram = scratch("h_dram", (TOK, HID), F32)
    ot_dram = scratch("ot_dram", (TILES, P, KVH, GRP * P), BF16)
    wo_dram = scratch("wo_dram", (2, P, HEADS, HID), F16)
    bt_dram = scratch("bt_dram", (2, P, KC, HID), F16)
    ag_dram = scratch("ag_dram", (2, P, KC, AGW), F16)
    lb_dram = scratch("lb_dram", (2, P, HID), F16)
    tokens_phase(nc, x, abslog, phase, base_w, gate_w, lora_A, lora_B, k_ident, k_mult, h_dram, bt_dram, ag_dram, lb_dram)
    nx, ng = KC * TOK, 2 * KC * GW
    part = 2 * PART * HID
    with nc.sbuf_tensor("arena", [P, PARTS * part], F16) as arena:
        xh, xl = (arena[:, i * nx:(i + 1) * nx].rearrange("p (k n) -> p k n", k=KC) for i in range(2))
        Wg = arena[:, 2 * nx:2 * nx + 2 * ng].rearrange("p (g x k n) -> p g x k n", g=2, x=2, k=KC)
        assert 2 * nx + 2 * ng <= (PARTS - 1) * part and 2 * nx + ng >= 5 * part and 2 * nx == 4 * part
        WoS = [arena[:, i * part:(i + 1) * part].rearrange("p (x h n) -> p x h n", x=2, h=PART) for i in (7, 4, 0, 1, 2, 3, 5, 6)]
        norm_phase(nc, xh, xl, h_dram, k_ident, k_minus)
        attention_phase(nc, xh, xl, Wg, WoS, Wq, Wk, Wv, Wo, k_ident, k_rope, k_masks, k_cum, ot_dram, wo_dram)
        output_phase(nc, WoS, h_dram, ot_dram, wo_dram, bt_dram, ag_dram, lb_dram, base_b, k_ident, k_before,
                     out.rearrange("b n d -> (b n) d"))


_INS = ['x', 'L0_tok_A_abslog', 'L0_tok_A_phase', 'L0_attn_Wq', 'L0_attn_Wk', 'L0_attn_Wv', 'L0_attn_Wo',
        'L0_ffn_gate_w', 'L0_ffn_base_w', 'L0_ffn_base_b', 'L0_ffn_lora_A', 'L0_ffn_lora_B']


def kernel(**inputs):
    import numpy as _np
    import concourse.bacc as _bacc
    from concourse import mybir as _mybir
    from concourse.bass_utils import run_bass_kernel_spmd as _run

    nc = _bacc.Bacc("TRN2", target_bir_lowering=False, num_devices=1)
    arrays, args = {}, []
    for name, a in [(n, inputs[n]) for n in _INS] + list(constants().items()):
        a = _np.ascontiguousarray(a)
        arrays[f"in_{name}_dram"] = a
        args.append(nc.dram_tensor(f"in_{name}_dram", a.shape, _mybir.dt.from_np(a.dtype), kind="ExternalInput").ap())
    args.append(nc.dram_tensor("out_0_dram", (BATCH, POS, HID), _mybir.dt.float32, kind="ExternalOutput").ap())
    block_kernel(nc, *args)
    r = _run(nc, [arrays], core_ids=[0])
    return r.results[0]["out_0_dram"]
```

```python
from contextlib import ExitStack

import numpy as np
import concourse.bass as bass
from concourse import mybir

F32 = mybir.dt.float32
F16 = mybir.dt.float16
BF16 = mybir.dt.bfloat16
ALU = mybir.AluOpType
ACT = mybir.ActivationFunctionType
X = mybir.AxisListType.X
ds = bass.ds

P = 128
BATCH, POS, NST = 32, 64, 64
HID = 1024
TOK = BATCH * POS
TILES = TOK // P
KC = HID // P
HEADS, KVH, DH = 32, 8, 128
GRP = HEADS // KVH
QW, KVW = GRP * DH, 2 * DH
GW = QW + KVW
STEPS = KVH * TILES
NE, RANK = 8, 16
ER = NE * RANK
AGW = ER + NE
WS = 64.0
VS, PS = 8.0, 1024.0
SCORE = 1.0 / float(np.sqrt(DH))
LORA_SCALE = 2.0
EPS = 1e-5
BIG = 1e30
PART = 4
PARTS, KEPT = HEADS // PART, 2
NA_, NB_ = 4, 256
NB1 = 16
MUL = [NB_ * a for a in range(NA_)] + [NB1 * b for b in range(16)] + list(range(16))
A0, B10, B20, NM = 0, NA_, NA_ + 16, len(MUL)
MONE = B20 + 1
HC = 4
MAGIC = 12582912.0
PI = float(np.pi)
C1 = 6.28125
C2 = float(np.float32(2 * np.pi - C1))


def constants():
    p = np.arange(P)
    pos, seq = p % POS, p // POS
    inv = (1.0 / (np.float32(10000.0) ** (2.0 * np.arange(DH // 2, dtype=np.float32) / np.float32(DH)))).astype(np.float32)
    fr = pos[:, None].astype(np.float32) * inv[None, :]
    causal = pos[:, None] >= np.arange(POS)[None, :]
    s, t = p[:, None], p[None, :]
    mid = POS // 2 - 1
    cum = ((s % POS <= t % POS) * 1.0 - (s % POS <= mid) * 1.0) * (s // POS == t // POS) / 16.0
    return {
        "ident": np.eye(P, dtype=np.float32),
        "minus": np.concatenate([-np.eye(P), -np.eye(P) / WS], axis=1).astype(np.float16),
        "rope": np.concatenate([t / s for s in (1.0, WS) for t in (np.cos(fr), np.sin(fr), -np.sin(fr))], axis=1).astype(np.float32),
        "masks": np.concatenate([np.where(causal, 0.0, -BIG), causal * 1.0], axis=1).astype(np.float32),
        "cum": cum.astype(np.float32),
        "mult": np.broadcast_to(np.array(MUL, np.float32), (P, NM)).copy(),
        "before": np.broadcast_to((np.arange(NE)[None, :] < np.arange(NE)[:, None]).astype(np.float32).reshape(1, NE * NE), (P, NE * NE)).copy(),
    }


def from_one(eng, sem, value):
    if isinstance(value, int) and value <= 0:
        return
    eng.wait_ge(sem, value)


def turns(t, par, each):
    return (t - par) * (each // 2) + each


def tokens_phase(nc, C, abslog, phase, base_w, gate_w, lora_A, lora_B, k_ident, k_minus, k_mult,
                 Wq, Wk, Wv, space, w0, w0_in, h_dram, bt_dram, ag_dram, lb_dram):
    NCH = POS // HC
    NW = KC + 2
    EARLY = 3
    BESIDE = NW - EARLY
    assert BESIDE % 2
    with ExitStack() as ctx:
        sb = lambda name, shape, dt=F32: ctx.enter_context(nc.sbuf_tensor(name, shape, dt))
        pb = lambda name, shape, dt=F32: ctx.enter_context(nc.psum_tensor(name, shape, dt))
        sem = lambda name: ctx.enter_context(nc.semaphore("t_" + name))
        ident, mult, minus = sb("t_ident", [P, P]), sb("t_mult", [P, NM]), sb("t_minus", [P, 2, P], F16)
        la_in, ph_in = sb("la_in", [POS, 2, NST]), sb("ph_in", [POS, 2, NST])
        lp = sb("lp", [P, 2, POS])
        used = [0]

        def buffer(*shape):
            n = int(np.prod(shape))
            used[0] += n
            names = "abcde"[:len(shape)]
            return space[:, used[0] - n:used[0]].rearrange(f"p ({' '.join(names)}) -> p {' '.join(names)}",
                                                           **dict(zip(names, shape)))
        cin = buffer(16, NST, 2)
        cdup = buffer(16, 2, 2, NST)
        X1, X2 = buffer(POS, BATCH), buffer(POS, BATCH)
        ang, rnd, cosr, sinr, dec = (buffer(POS, NM) for _ in range(5))
        halfpi = sb("halfpi", [P, 1])
        sm = sb("t_sm", [P, 10, POS])
        e1 = sb("e1", [P, 4, POS, NA_])
        TF1, TF2 = sb("TF1", [P, POS, NA_]), sb("TF2", [P, POS, NA_])
        U, V = buffer(POS, 16), buffer(POS, 16)
        E2a, E2b = sb("E2a", [P, 2, HC, 16, 16]), sb("E2b", [P, 2, HC, 16, 16])
        Ga, Gb = sb("Ga", [P, 2, HC, NA_, BATCH]), sb("Gb", [P, 2, HC, NA_, BATCH])
        hst = sb("hst", [P, 2, HC, NB_])
        wt = sb("w_rows", [P, 2, HID])
        gt = sb("gate_rows", [NE, HID])
        lbt = sb("lb_rows", [P, KC, NE, RANK])
        w_hi, w_lo = sb("w_hi", [P, 2, KC, P], F16), sb("w_lo", [P, 2, KC, P], F16)
        ag = sb("ag_parts", [P, 2, KC, AGW], F16)
        lb = sb("lb_parts", [P, 2, HID], F16)
        bank = [pb(f"t_bank{i}", [P, 512]) for i in range(8)]
        pH = [b[:].rearrange("p (j b) -> p j b", j=2) for b in bank[4:8]]
        pW = [bank[0:2], bank[2:4]]

        consts_in, params_in, c_in, c_split = sem("consts_in"), sem("params_in"), sem("c_in"), sem("c_split")
        params_t, params_copied, c_t, c_copied1, c_copied2 = (sem(x) for x in
            ("params_t", "params_copied", "c_t", "c_copied1", "c_copied2"))
        link, alink, angles, dec_arg, trig, dec_done = (sem(x) for x in ("link", "alink", "angles", "dec_arg", "trig", "dec_done"))
        g_terms, g_ready, e_ready, h_done, h_copied = (sem(x) for x in ("g_terms", "g_ready", "e_ready", "h_done", "h_copied"))
        h_out, w_in, w_out = ([sem(f"{x}{i}") for i in range(2)] for x in ("h_out", "w_in", "w_out"))
        tables, e2_ready = sem("tables"), sem("e2_ready")
        minus_in, rest_in, w_t, w_high, w_left, w_low = (sem(x) for x in ("minus_in", "rest_in", "w_t", "w_high", "w_left", "w_low"))
        block = ctx.enter_context(nc.Block())

        @block.sync
        def _(sp):
            for dup in range(2):
                sp.dma_start(la_in[:, dup, :], abslog).then_inc(params_in, 16)
                sp.dma_start(ph_in[:, dup, :], phase).then_inc(params_in, 16)
            sp.dma_start(ident[:], k_ident).then_inc(consts_in, 16)
            sp.dma_start(mult[:], k_mult).then_inc(consts_in, 16)
            sp.dma_start(minus[:].rearrange("p x n -> p (x n)"), k_minus).then_inc(minus_in, 16)
            sp.dma_start(cin[:].rearrange("p i n r -> p i (n r)"),
                         C.rearrange("c h n r -> (c h) (n r)").rearrange("(i p) m -> p i m", p=P)).then_inc(c_in, 16)
            for W, at, n in ((Wq, 0, QW), (Wk, QW, DH), (Wv, QW + DH, DH)):
                sp.dma_start(w0[:, :, at:at + n], W[:, 0:n].rearrange("(c p) n -> p c n", p=P)).then_inc(w0_in, 16)
            hv = h_dram.rearrange("(c h) (a b) -> a c h b", h=POS, b=NB_)

            def store(k, par):
                sp.wait_ge(h_copied, 2 * (k + 1))
                for a in range(NA_):
                    sp.dma_start(hv[a, :, ds(k * HC, HC), :], hst[a * BATCH:(a + 1) * BATCH, par]).then_inc(h_out[par], 16)
            with sp.Fori(0, NCH // 2) as half:
                store(half * 2, 0)
                store(half * 2 + 1, 1)
            for s in h_out:
                sp.wait_ge(s, 16 * NA_ * NCH // 2)

        @block.gpsimd
        def _(pool):
            def load(k):
                src = base_w[k * P:(k + 1) * P, :] if k < KC else lora_A.rearrange("e r n -> (e r) n")
                pool.dma_start(wt[:, k % 2, :], src).then_inc(w_in[k % 2], 16)
            load(0)
            load(1)
            pool.dma_start(gt[:], gate_w).then_inc(rest_in, 16)
            for k in range(KC):
                pool.dma_start(lbt[:, k], lora_B[:, k * P:(k + 1) * P, :].rearrange("e p r -> p e r")).then_inc(rest_in, 16)

            def build(k, par):
                pool.wait_ge(h_done, 2 * (k - 1))
                o = V[:, ds(k * HC, HC), :].unsqueeze(3).broadcast_to([P, HC, 16, 16])
                i = sinr[:, ds(k * HC, HC), B20:B20 + 16].unsqueeze(2).broadcast_to([P, HC, 16, 16])
                nc.gpsimd.tensor_tensor(E2b[:, par], o, i, ALU.mult).then_inc(e2_ready, 1)

            def store(k):
                pool.wait_ge(w_low, k + 1)
                if k + 2 <= KC:
                    load(k + 2)
                for i, part in enumerate((w_hi, w_lo)):
                    dst, src = ((bt_dram[i, :, :, k * P:(k + 1) * P], part[:, k % 2]) if k < KC else
                                (ag_dram[i], ag[:, i]) if k == KC else (lb_dram[i], lb[:, i]))
                    pool.dma_start(dst, src).then_inc(w_out[k % 2], 16)
            for k in range(EARLY):
                store(k)
            pool.wait_ge(tables, 1)
            for k in range(BESIDE):
                if k:
                    build(k + 1, (k + 1) % 2)
                store(EARLY + k)
            with pool.Fori((BESIDE + 1) // 2, NCH // 2) as half:
                build(half * 2, 0)
                build(half * 2 + 1, 1)
            for s in w_out:
                pool.wait_ge(s, 16 * NW)

        @block.tensor
        def _(pe):
            pe.wait_ge(params_in, 64)
            pe.wait_ge(consts_in, 32)
            nc.tensor.transpose(bank[7][:, 0:POS], la_in[:].rearrange("p a n -> p (a n)"), ident[0:POS, 0:POS])
            nc.tensor.transpose(bank[7][:, POS:2 * POS], ph_in[:].rearrange("p a n -> p (a n)"),
                                ident[0:POS, 0:POS]).then_inc(params_t, 1)
            pe.wait_ge(c_split, 1)
            for i in range(4):
                if i == 3:
                    pe.wait_ge(params_copied, 1)
                for r in range(2):
                    for j in range(4):
                        last = nc.tensor.transpose(bank[2 * i + r][:, j * P:(j + 1) * P],
                                                   cdup[:, 4 * i + j, r].rearrange("p d n -> p (d n)"), ident[:])
                last.then_inc(c_t, 1)

            def product(k, par):
                pe.wait_ge(g_ready, k + 1)
                pe.wait_ge(e_ready, k + 1)
                if not isinstance(k, int) or k >= 2:
                    pe.wait_ge(e2_ready, k - 1)
                from_one(pe, h_copied, 2 * (k - 1))
                for j in range(HC):
                    o = pH[2 * par + j // 2][:, j % 2, :]
                    w = Ga[:, par, j].rearrange("p a c -> p (a c)")
                    nc.tensor.matmul(o, w, E2a[:, par, j].rearrange("p x y -> p (x y)"), start=True, stop=False)
                    last = nc.tensor.matmul(o, w, E2b[:, par, j].rearrange("p x y -> p (x y)"), start=False, stop=True)
                    if j % 2:
                        last.then_inc(h_done, 1)

            def weights(k):
                if k <= KC:
                    pe.wait_ge(w_in[k % 2], 16 * (k // 2 + 1))
                if k == KC:
                    pe.wait_ge(rest_in, 16 * (KC + 1))
                if k >= 2:
                    pe.wait_ge(w_low, k - 1 if k <= KC else k)
                for j in range(KC):
                    src = wt[:, k % 2, j * P:(j + 1) * P] if k <= KC else lbt[:, j].rearrange("p e r -> p (e r)")
                    last = nc.tensor.matmul(pW[k % 2][j // 4][:, (j % 4) * P:(j % 4 + 1) * P], src, ident[:],
                                            start=(j % 4 == 0), stop=False, is_transpose=True, skip_group_check=True)
                if k == KC:
                    pe.wait_ge(w_low, KC)
                    for j in range(KC):
                        last = nc.tensor.matmul(pW[1][0][:, j * NE:(j + 1) * NE], gt[:, j * P:(j + 1) * P], ident[0:NE, 0:NE],
                                                start=(j == 0), stop=False, is_transpose=True, skip_group_check=True)
                last.then_inc(w_t, 1)

            def take_off(k):
                pe.wait_ge(w_high, k + 1)
                for x in range(2):
                    if k == KC:
                        for j in range(4):
                            last = nc.tensor.matmul(pW[0][x][:, j * P:(j + 1) * P], minus[:, 1, :], ag[:, 0, 4 * x + j, 0:ER],
                                                    start=False, stop=(j == 3), skip_group_check=True)
                    else:
                        hi = w_hi[:, k % 2, 4 * x:4 * x + 4, :].rearrange("p k n -> p (k n)") if k < KC else lb[:, 0, x * 512:(x + 1) * 512]
                        last = nc.tensor.matmul(pW[k % 2][x][:], minus[:, 1, :], hi, start=False, stop=True, skip_group_check=True)
                if k == KC:
                    for j in range(KC):
                        last = nc.tensor.matmul(pW[1][0][:, j * NE:(j + 1) * NE], minus[:, 1, :], ag[:, 0, j, ER:AGW],
                                                start=False, stop=(j == KC - 1), skip_group_check=True)
                last.then_inc(w_left, 1)
            pe.wait_ge(c_copied1, 4)
            pe.wait_ge(c_copied2, 4)
            pe.wait_ge(minus_in, 16)
            for k in range(EARLY):
                weights(k)
                take_off(k)
            for k in range(BESIDE):
                weights(EARLY + k)
                product(k, k % 2)
                take_off(EARLY + k)
            product(BESIDE, 1)
            with pe.Fori((BESIDE + 1) // 2, NCH // 2) as half:
                product(half * 2, 0)
                product(half * 2 + 1, 1)

        @block.scalar
        def _(act):
            a = nc.scalar.activation
            act.wait_ge(c_in, 16)
            for r in range(2):
                last = a(cdup[:, :, r], cin[:, :, :, r].unsqueeze(2).broadcast_to([P, 16, 2, NST]), ACT.Copy)
            last.then_inc(c_split, 1)
            act.wait_ge(dec_arg, 1)
            a(dec[:], dec[:], ACT.Exp).then_inc(dec_done, 1)
            act.wait_ge(angles, 1)
            a(cosr[:], ang[:], ACT.Abs).then_inc(alink, 1)
            a(sinr[:], ang[:], ACT.Sin)
            act.wait_ge(alink, 1)
            a(cosr[:], cosr[:], ACT.Sin, bias=halfpi[:], scale=-1.0).then_inc(trig, 1)
            for i in range(4):
                act.wait_ge(c_t, i + 1)
                src = bank[2 * i + 1][:].rearrange("p (c h) -> p h c", h=POS)
                a(X2[:, :, 8 * i:8 * i + 8], src, ACT.Copy).then_inc(c_copied2, 1)

            def copy_out(k, par):
                if not isinstance(k, int) or k >= 2:
                    act.wait_ge(h_out[par], turns(k - 2, par, 16 * NA_))
                for j in range(2):
                    act.wait_ge(h_done, 2 * k + j + 1)
                    a(hst[:, par, 2 * j:2 * j + 2, :], pH[2 * par + j], ACT.Copy).then_inc(h_copied, 1)

            def split(k, i):
                act.wait_ge((w_t, w_left)[i], k + 1)
                if k >= 2 and i == 0:
                    act.wait_ge(w_out[k % 2], 32 * (k // 2))
                for x in range(2):
                    src = pW[k % 2][x][:]
                    if k < KC:
                        dst = (w_hi, w_lo)[i][:, k % 2, 4 * x:4 * x + 4, :].rearrange("p k n -> p (k n)")
                    elif k == KC:
                        dst, src = ag[:, i, 4 * x:4 * x + 4, 0:ER], src.rearrange("p (k n) -> p k n", k=4)
                    else:
                        dst = lb[:, i, x * 512:(x + 1) * 512]
                    last = a(dst, src, ACT.Copy, scale=WS)
                if k == KC:
                    last = a(ag[:, i, :, ER:AGW], pW[1][0][:, 0:KC * NE].rearrange("p (k n) -> p k n", k=KC), ACT.Copy, scale=WS)
                last.then_inc((w_high, w_low)[i], 1)
            for k in range(EARLY):
                split(k, 0)
                split(k, 1)
            for k in range(BESIDE):
                split(EARLY + k, 0)
                copy_out(k, k % 2)
                split(EARLY + k, 1)
            copy_out(BESIDE, 1)
            with act.Fori((BESIDE + 1) // 2, NCH // 2) as half:
                copy_out(half * 2, 0)
                copy_out(half * 2 + 1, 1)

        @block.vector
        def _(dve):
            count = [0]

            def step(ins):
                count[0] += 1
                ins.then_inc(link, 1)
                dve.wait_ge(link, count[0])
            v = nc.vector
            v.memset(halfpi[:], PI / 2)
            dve.wait_ge(params_t, 1)
            v.tensor_copy(lp[:], bank[7][:, 0:2 * POS].rearrange("p (k h) -> p k h", k=2)).then_inc(params_copied, 1)
            dve.wait_ge(params_copied, 1)
            dve.wait_ge(consts_in, 32)
            mb = mult[:].unsqueeze(1).broadcast_to([P, POS, NM])
            v.tensor_tensor(dec[:], lp[:, 0, :].unsqueeze(2).broadcast_to([P, POS, NM]), mb, ALU.mult).then_inc(dec_arg, 1)
            step(v.tensor_tensor(ang[:], lp[:, 1, :].unsqueeze(2).broadcast_to([P, POS, NM]), mb, ALU.mult))
            step(v.tensor_scalar(rnd[:], ang[:], 1.0 / (2 * PI), MAGIC, ALU.mult, ALU.add))
            step(v.tensor_scalar(rnd[:], rnd[:], MAGIC, None, ALU.subtract))
            fl = lambda t: t[:].rearrange("p h m -> p (h m)")
            for c in (C1, C2):
                step(v.scalar_tensor_tensor(fl(ang), fl(rnd), -c, fl(ang), ALU.mult, ALU.add))
            v.tensor_scalar(ang[:], ang[:], PI, -PI, ALU.min, ALU.max).then_inc(angles, 1)
            for i in range(4):
                dve.wait_ge(c_t, i + 1)
                src = bank[2 * i][:].rearrange("p (c h) -> p h c", h=POS)
                v.tensor_copy(X1[:, :, 8 * i:8 * i + 8], src).then_inc(c_copied1, 1)
            dve.wait_ge(trig, 1)
            dve.wait_ge(dec_done, 1)
            v.tensor_tensor(sinr[:], sinr[:], dec[:], ALU.mult)
            step(v.tensor_tensor(cosr[:], cosr[:], dec[:], ALU.mult))
            la, w = lp[:, 0, :], ang[:, :, MONE]
            ar, den, den2, n1, n2, n3, n4, fr, fi = (sm[:, i, :] for i in range(9))
            ai = sinr[:, :, MONE]
            v.tensor_scalar(ar, cosr[:, :, MONE], 1.0, None, ALU.subtract)
            v.tensor_tensor(den, la, la, ALU.mult)
            step(v.tensor_tensor(den2, w, w, ALU.mult))
            v.tensor_tensor(n1, ar, la, ALU.mult)
            v.tensor_tensor(n2, ai, w, ALU.mult)
            v.tensor_tensor(n3, ai, la, ALU.mult)
            v.tensor_tensor(n4, ar, w, ALU.mult)
            step(v.tensor_tensor(den, den, den2, ALU.add))
            step(v.reciprocal(den, den))
            v.tensor_tensor(n1, n1, n2, ALU.add)
            step(v.tensor_tensor(n3, n3, n4, ALU.subtract))
            v.scalar_tensor_tensor(fr, n1, 2.0, den, ALU.mult, ALU.mult)
            step(v.scalar_tensor_tensor(fi, n3, 2.0, den, ALU.mult, ALU.mult))
            frb, fib = (t.unsqueeze(2).broadcast_to([P, POS, NA_]) for t in (fr, fi))
            ca, sa = cosr[:, :, A0:A0 + NA_], sinr[:, :, A0:A0 + NA_]
            for i, (x, y) in enumerate(((frb, ca), (fib, sa), (frb, sa), (fib, ca))):
                last = v.tensor_tensor(e1[:, i], x, y, ALU.mult)
            step(last)
            v.tensor_tensor(e1[:, 0], e1[:, 0], e1[:, 1], ALU.subtract)
            step(v.tensor_tensor(e1[:, 2], e1[:, 2], e1[:, 3], ALU.add))
            lo, hi = slice(0, 64), slice(64, 128)
            v.tensor_copy(TF1[lo], e1[lo, 0])
            v.tensor_scalar(TF1[hi], e1[hi, 2], -1.0, None, ALU.mult)
            v.tensor_scalar(TF2[lo], e1[lo, 2], -1.0, None, ALU.mult)
            v.tensor_scalar(TF2[hi], e1[hi, 0], -1.0, None, ALU.mult)
            cb, sb_ = cosr[:, :, B10:B10 + 16], sinr[:, :, B10:B10 + 16]
            v.tensor_copy(U[lo], cb[lo])
            v.tensor_copy(U[hi], sb_[hi])
            v.tensor_scalar(V[lo], sb_[lo], -1.0, None, ALU.mult)
            v.tensor_copy(V[hi], cb[hi]).then_inc(tables, 1)
            dve.wait_ge(tables, 1)
            dve.wait_ge(c_copied2, 4)
            dve.wait_ge(c_copied1, 4)

            def build(k, par):
                from_one(dve, h_done, 2 * (k - 1))
                hs = ds(k * HC, HC)
                c = lambda t: t[:, hs, :].unsqueeze(2).broadcast_to([P, HC, NA_, BATCH])
                f = lambda t: t[:, hs, :].unsqueeze(3).broadcast_to([P, HC, NA_, BATCH])
                v.tensor_tensor(Ga[:, par], c(X1), f(TF1), ALU.mult)
                v.tensor_tensor(Gb[:, par], c(X2), f(TF2), ALU.mult).then_inc(g_terms, 1)
                o = lambda t: t[:, hs, :].unsqueeze(3).broadcast_to([P, HC, 16, 16])
                i = lambda t: t[:, hs, B20:B20 + 16].unsqueeze(2).broadcast_to([P, HC, 16, 16])
                if isinstance(k, int):
                    v.tensor_tensor(E2b[:, par], o(V), i(sinr), ALU.mult)
                v.tensor_tensor(E2a[:, par], o(U), i(cosr), ALU.mult).then_inc(e_ready, 1)
                dve.wait_ge(g_terms, k + 1)
                v.tensor_tensor(Ga[:, par], Ga[:, par], Gb[:, par], ALU.add).then_inc(g_ready, 1)

            build(0, 0)
            build(1, 1)
            with dve.Fori(1, NCH // 2) as half:
                build(half * 2, 0)
                build(half * 2 + 1, 1)


def norm_phase(nc, xh, xl, Wg, w0, w0_in, w_ready, h_dram, k_ident, k_minus):
    with ExitStack() as ctx:
        sb = lambda name, shape, dt=F32: ctx.enter_context(nc.sbuf_tensor(name, shape, dt))
        sem = lambda name: ctx.enter_context(nc.semaphore("n_" + name))
        NB = 4
        ident, minus, eps, carry = sb("n_ident", [P, P]), sb("n_minus", [P, 2, P], F16), sb("n_eps", [P, 1]), sb("n_carry", [P, 1])
        ht, xn = sb("n_ht", [P, NB, HID]), sb("n_xn", [P, NB, HID])
        st, mv, sd, rs = sb("n_st", [P, 2, 2, 6]), sb("n_mv", [P, 2, 2]), sb("n_sd", [P, 2, 1]), sb("n_rs", [P, 2, 1])
        pX = [[ctx.enter_context(nc.psum_tensor(f"n_pX{i}{j}", [P, 4, P], F32)) for j in range(2)] for i in range(NB)]
        consts_in, h_in = sem("consts_in"), [sem(f"h_in{i}") for i in range(NB)]
        stats, var_ready, sd_ready, rs_ready, xn_ready, x_t, hi_done, lo_t, lo_done, lo2_done, w_high, w_scaled = (sem(x) for x in
            ("stats", "var_ready", "sd_ready", "rs_ready", "xn_ready", "x_t", "hi_done", "lo_t", "lo_done", "lo2_done", "w_high", "w_scaled"))
        block = ctx.enter_context(nc.Block())

        def steps(eng, order, fns):
            def step(t, i):
                for name, lag in order:
                    if not isinstance(t, int) or 0 <= t - lag < TILES:
                        fns[name](t - lag, (i - lag) % NB)
            for t in range(NB):
                step(t, t)
            with eng.Fori(1, TILES // NB) as quad:
                for i in range(NB):
                    step(quad * NB + i, i)
            step(TILES, 0)
            step(TILES + 1, 1)
            step(TILES + 2, 2)

        @block.gpsimd
        def _(pool):
            for c in range(0, KC, 2):
                pool.wait_ge(w_high, c // 2 + 1)
                hi, lo = (Wg[:, 1, x, c:c + 2, :].rearrange("p k n -> p (k n)") for x in range(2))
                w = w0[:, c:c + 2, :].rearrange("p k n -> p (k n)")
                nc.gpsimd.tensor_scalar(w, w, WS, None, ALU.mult).then_inc(w_scaled, 1)
                pool.wait_ge(w_scaled, c // 2 + 1)
                nc.gpsimd.tensor_tensor(lo, w, hi, ALU.subtract).then_inc(w_ready, 2)

        @block.sync
        def _(sp):
            hv = h_dram.rearrange("(t p) n -> t p n", p=P)
            sp.dma_start(ident[:], k_ident).then_inc(consts_in, 16)
            sp.dma_start(minus[:].rearrange("p x n -> p (x n)"), k_minus).then_inc(consts_in, 16)

            def load(t, i):
                if not isinstance(t, int) or t >= NB:
                    sp.wait_ge(xn_ready, t - NB + 1)
                sp.dma_start(ht[:, i, :], hv[ds(t, 1)].rearrange("o p n -> (o p) n")).then_inc(h_in[i], 16)
            for t in range(NB):
                load(t, t)
            with sp.Fori(1, TILES // NB) as quad:
                for i in range(NB):
                    load(quad * NB + i, i)

        @block.tensor
        def _(pe):
            def transposes(t, i):
                pe.wait_ge(xn_ready, t + 1)
                if not isinstance(t, int) or t >= NB:
                    pe.wait_ge(lo_done, t - NB + 1)
                    pe.wait_ge(lo2_done, t - NB + 1)
                for j in range(KC):
                    last = nc.tensor.matmul(pX[i][j // 4][:, j % 4, :], xn[:, i, j * P:(j + 1) * P], ident[:],
                                            start=(j % 4 == 0), stop=(j >= 4), is_transpose=True, skip_group_check=True)
                last.then_inc(x_t, 1)

            def take_off(t, i):
                pe.wait_ge(hi_done, t + 1)
                for c in range(4):
                    last = nc.tensor.matmul(pX[i][0][:, c, :], minus[:, 0, :], xh[:, c, ds(t * P, P)],
                                            start=False, stop=(c == 3), skip_group_check=True)
                last.then_inc(lo_t, 1)
            pe.wait_ge(consts_in, 32)
            steps(pe, [("t", 1), ("o", 2)], {"t": transposes, "o": take_off})

        @block.scalar
        def _(act):
            a = nc.scalar.activation

            def root(t, i):
                act.wait_ge(var_ready, t + 1)
                a(sd[:, i % 2, :], mv[:, i % 2, 1:2], ACT.Sqrt, bias=eps[:]).then_inc(sd_ready, 1)

            def high(t, i):
                act.wait_ge(x_t, t + 1)
                for j in range(2):
                    last = a(xh[:, 4 * j:4 * j + 4, ds(t * P, P)], pX[i][j][:], ACT.Copy)
                last.then_inc(hi_done, 1)

            def low(t, i):
                act.wait_ge(lo_t, t + 1)
                a(xl[:, 0:4, ds(t * P, P)], pX[i][0][:], ACT.Copy).then_inc(lo_done, 1)
            act.wait_ge(w0_in, 48)
            for c in range(0, KC, 2):
                a(Wg[:, 1, 0, c:c + 2, :], w0[:, c:c + 2, :], ACT.Copy, scale=WS).then_inc(w_high, 1)
            steps(act, [("r", 0), ("h", 1), ("l", 2)], {"r": root, "h": high, "l": low})

        @block.vector
        def _(dve):
            v = nc.vector
            v.memset(eps[:], EPS)

            def moments(t, i):
                dve.wait_ge(h_in[i], (t - i) * (16 // NB) + 16)
                from_one(dve, sd_ready, t - 1)
                for j in range(2):
                    last = v.bn_stats(st[:, i % 2, j, :], ht[:, i, j * 512:(j + 1) * 512])
                last.then_inc(stats, 1)
                dve.wait_ge(stats, t + 1)
                v.memset(carry[:], 0.0)
                v.bn_aggr(mv[:, i % 2, :], st[:, i % 2]).then_inc(var_ready, 1)

            def normalise(t, i):
                dve.wait_ge(sd_ready, t + 1)
                v.reciprocal(rs[:, i % 2, :], sd[:, i % 2, :]).then_inc(rs_ready, 1)
                dve.wait_ge(rs_ready, t + 1)
                dve.wait_ge(var_ready, t + 1)
                if not isinstance(t, int) or t >= NB:
                    dve.wait_ge(x_t, t - NB + 1)
                v.tensor_scalar(xn[:, i, :], ht[:, i, :], mv[:, i % 2, 0:1], rs[:, i % 2, :], ALU.subtract,
                                ALU.mult).then_inc(xn_ready, 1)

            def low(t, i):
                dve.wait_ge(hi_done, t + 1)
                v.tensor_tensor(xl[:, 4:8, ds(t * P, P)], pX[i][1][:], xh[:, 4:8, ds(t * P, P)], ALU.subtract).then_inc(lo2_done, 1)
            steps(dve, [("l", 3), ("m", 0), ("n", 1)], {"m": moments, "n": normalise, "l": low})


def attention_phase(nc, xh, xl, Wg, wst, w_ready, WoS, oT, o_in, Wq, Wk, Wv, Wo, k_ident, k_rope, k_masks, k_cum, ot_dram, wo_dram):
    with ExitStack() as ctx:
        sb = lambda name, shape, dt=F32: ctx.enter_context(nc.sbuf_tensor(name, shape, dt))
        pb = lambda name, shape, dt=F32: ctx.enter_context(nc.psum_tensor(name, shape, dt))
        sem = lambda name: ctx.enter_context(nc.semaphore(name))
        H2 = GRP // 2
        ident, rope = sb("ident", [P, P]), sb("rope", [P, 6, DH // 2])
        masks, cum = sb("masks", [P, 2, POS]), sb("cum", [P, P])
        ost = sb("ost", [P, HID])
        oh, ol = sb("oh", [P, HID], F16), sb("ol", [P, HID], F16)
        KV = sb("KV", [P, 2, KVW])
        K, V = KV[:, :, 0:DH], KV[:, :, DH:KVW]
        Vs = sb("Vs", [P, 2, 4, DH], F16)
        kabs, kexp, kln, gate = (sb(n, [P, 2, DH]) for n in ("kabs", "kexp", "kln", "gate"))
        eG, eGn = sb("eG", [P, 2, DH]), sb("eGn", [P, 2, DH])
        qmx, qnb, qsum, qrs = (sb(n, [P, 2, GRP]) for n in ("qmx", "qnb", "qsum", "qrs"))
        kmx, knb, ksum, krs = (sb(n, [P, 2, 1]) for n in ("kmx", "knb", "ksum", "krs"))
        smx, snb, ssum, srs = (sb(n, [P, 2, 4]) for n in ("smx", "snb", "ssum", "srs"))
        E, Ek = sb("E", [P, 2, GRP, DH]), sb("Ek", [P, 2, DH])
        t1, t2 = sb("t1", [P, GRP, 2, DH // 2]), sb("t2", [P, GRP, 2, DH // 2])
        kt1, kt2 = sb("kt1", [P, 2, DH // 2]), sb("kt2", [P, 2, DH // 2])
        QR, QD = sb("QR", [P, 2, GRP, DH]), sb("QD", [P, 2, GRP, DH])
        KR, KD = sb("KR", [P, 2, DH]), sb("KD", [P, 2, DH])
        QT, ET = sb("QT", [P, 2, 2, GRP, POS], F16), sb("ET", [P, 2, GRP, POS])
        KRT, KDT = sb("KRT", [P, 2, P], F16), sb("KDT", [P, P])
        S2, L, Es, PR = (sb(n, [P, 2, 4, POS]) for n in ("S2", "L", "Es", "PR"))
        PT = sb("PT", [P, 2, 2, H2 * P], F16)
        OT = sb("OT", [P, 2, GRP, 2, POS], BF16)

        QP = [pb(f"QP{i}", [P, QW]) for i in range(2)]
        KVP = pb("KVP", [P, 512])
        TQ, TE = pb("TQ", [P, GRP, P]), pb("TE", [P, GRP, P])
        KG = pb("KG", [P, 4, P])
        SC = pb("SC", [P, 2, 4, POS])
        OP = pb("OP", [P, 2, GRP, POS])
        PTP = KVP[:, KVW:512]

        consts_in, w_high, v_high, v_low, pt_high, o_half = (sem(n) for n in ("consts_in", "w_high", "v_high", "v_low", "pt_high", "o_half"))
        w_in = [sem(f"w_in{i}") for i in range(2)]
        wo_in, wo_high, wo_ready, wo_out, wo_kept = (sem(n) for n in ("wo_in", "wo_high", "wo_ready", "wo_out", "wo_kept"))
        rows = lambda W: W.rearrange("(c p) n -> c p n", p=P)
        kv_done, kv_copied, q_done = sem("kv_done"), sem("kv_copied"), sem("q_done")
        qmax_raw, qmax_ready, q_read, qexp_done, q_terms, q_roped, qrs_ready, q_decayed = (sem(n) for n in
            ("qmax_raw", "qmax_ready", "q_read", "qexp_done", "q_terms", "q_roped", "qrs_ready", "q_decayed"))
        kmax_raw, kmax_ready, kexp_done, k_terms, k_roped, krs_ready, k_decayed = (sem(n) for n in
            ("kmax_raw", "kmax_ready", "kexp_done", "k_terms", "k_roped", "krs_ready", "k_decayed"))
        kabs_done, knegexp_done, kln_done, gate_ready, G_done, eG_done = (sem(n) for n in
            ("kabs_done", "knegexp_done", "kln_done", "gate_ready", "G_done", "eG_done"))
        t_done, kt_done, qt_copied, kt_high, kt_copied, qt_low = (sem(n) for n in
            ("t_done", "kt_done", "qt_copied", "kt_high", "kt_copied", "qt_low"))
        sc_done, s_read, smax_raw, smax_ready, sexp_done, srs_ready, p_ready = (sem(n) for n in
            ("sc_done", "s_read", "smax_raw", "smax_ready", "sexp_done", "srs_ready", "p_ready"))
        pt_done, pt_copied, o_done, o_copied, o_out0 = (sem(n) for n in ("pt_done", "pt_copied", "o_done", "o_copied", "o_out0"))
        o_out = [o_out0, sem("o_out1")]
        block = ctx.enter_context(nc.Block())
        LASTU = (KVH - 1) * TILES // 4

        def steps(eng, order, weights, fns):
            def step(n, i, piece=None):
                for name, lag in order:
                    if name == "w":
                        if piece:
                            weights(*piece)
                    elif not isinstance(n, int) or 0 <= n - lag < STEPS:
                        fns[name](n - lag, (i - lag) % 4)

            def quads(quad, more):
                for i in range(4):
                    step(quad * 4 + i, i, (quad, i, more))
            quads(0, True)
            with eng.Fori(1, LASTU) as quad:
                quads(quad, True)
            with eng.Fori(LASTU, STEPS // 4) as quad:
                quads(quad, False)
            step(STEPS, 0)
            step(STEPS + 1, 1)
            step(STEPS + 2, 2)

        @block.sync
        def _(sp):
            sp.dma_start(ident[:], k_ident).then_inc(consts_in, 16)
            sp.dma_start(rope[:].rearrange("p a b -> p (a b)"), k_rope).then_inc(consts_in, 16)
            sp.dma_start(masks[:].rearrange("p a b -> p (a b)"), k_masks).then_inc(consts_in, 16)
            sp.dma_start(cum[:], k_cum).then_inc(consts_in, 16)

            def store(n, par):
                sp.wait_ge(o_copied, n + 1)
                g, t = n // TILES, n % TILES
                dst = ot_dram[ds(t, 1), :, ds(g, 1), :].rearrange("o d u m -> (o d) (u m)")
                sp.dma_start(dst, OT[:, par].rearrange("p h b t -> p (h b t)")).then_inc(o_out[par], 16)
            last = STEPS // 2 - 4
            with sp.Fori(0, last) as half:
                for i in range(2):
                    store(half * 2 + i, i)
            for i in range(2):
                sp.wait_ge(o_out[i], 16 * last)
            for i in range(2):
                load_o(sp, oT, o_in, ot_dram, i, i)
            with sp.Fori(last, STEPS // 2) as half:
                for i in range(2):
                    store(half * 2 + i, i)
            for s in o_out:
                sp.wait_ge(s, 16 * STEPS // 2)

        @block.gpsimd
        def _(pool):
            def load_chunk(g, c, slot):
                for W, at, n in ((Wq, 0, QW), (Wk, QW, DH), (Wv, QW + DH, DH)):
                    src = rows(W)[ds(c, 1), :, ds(g * n, n)].rearrange("o p n -> (o p) n")
                    pool.dma_start(wst[:, slot, at:at + n], src).then_inc(w_in[slot], 16)

            def unit(u, more):
                if more:
                    for i in range(2):
                        pool.wait_ge(w_ready, KC + 2 * u - 1 + i)
                        load_chunk(u // 4 + 1, (u % 4) * 2 + i, i)
                from_one(pool, wo_ready, u)
                pool.dma_start(ost[:], rows(Wo)[ds(u, 1)].rearrange("o p n -> (o p) n")).then_inc(wo_in, 16)
                pool.wait_ge(wo_ready, u + 1)
                for x, part in enumerate((oh, ol)):
                    pool.dma_start(wo_dram[x, :, ds(u, 1), :].rearrange("p o n -> p (o n)"), part[:]).then_inc(wo_out, 16)
            unit(0, True)
            with pool.Fori(1, LASTU) as u:
                unit(u, True)
            pool.wait_ge(wo_out, 32 * LASTU)
            pool.wait_ge(q_done, (KVH - 1) * TILES)
            for part in range(KEPT):
                for x in range(2):
                    pool.dma_start(WoS[part][:, x], wo_dram[x, :, part * PART:(part + 1) * PART, :]).then_inc(wo_kept, 16)
            with pool.Fori(LASTU, HEADS) as u:
                unit(u, False)
            pool.wait_ge(wo_out, 32 * HEADS)
            pool.wait_ge(wo_kept, 32 * KEPT)

        @block.tensor
        def _(pe):
            mm = nc.tensor.matmul

            def project(out, n, cols, chunks):
                g = n // TILES
                tok = ds((n % TILES) * P, P)
                par = (g + 1) % 2
                for c in chunks:
                    wv = [Wg[:, ds(par, 1), i, c, cols].rearrange("p o n -> p (o n)") for i in range(2)]
                    mm(out, xh[:, c, tok], wv[0], start=(c == 0), stop=False, skip_group_check=True)
                    mm(out, xh[:, c, tok], wv[1], start=False, stop=False, skip_group_check=True)
                    last = mm(out, xl[:, c, tok], wv[0], start=False, stop=(c == KC - 1), skip_group_check=True)
                return last

            def kv(n, s):
                pe.wait_ge(w_ready, (n // TILES + 1) * KC)
                from_one(pe, kv_copied, n)
                project(KVP[:, 0:KVW], n, slice(QW, GW), range(KC)).then_inc(kv_done, 1)

            def transposes(n, s):
                p = s % 2
                pe.wait_ge(q_roped, n + 1)
                pe.wait_ge(q_decayed, n + 1)
                pe.wait_ge(k_roped, n + 1)
                pe.wait_ge(k_decayed, n + 1)
                from_one(pe, qt_copied, 2 * n)
                from_one(pe, kt_copied, n)
                from_one(pe, qt_low, n)
                nc.tensor.transpose(KG[:, 1, :], KR[:, p, :], ident[:])
                nc.tensor.transpose(KG[:, 2, :], KD[:, p, :], ident[:]).then_inc(kt_done, 1)
                for h in range(GRP):
                    nc.tensor.transpose(TQ[:, h, :], QR[:, p, h, :], ident[:])
                for h in range(GRP):
                    last = nc.tensor.transpose(TE[:, h, :], QD[:, p, h, :], ident[:])
                last.then_inc(t_done, 1)

            def q_first(n, s):
                if not isinstance(n, int) or n >= 2:
                    pe.wait_ge(q_read, n - 1)
                    pe.wait_ge(qexp_done, n - 1)
                project(QP[s % 2][:], n, slice(0, QW), range(KC // 2))

            def q_fifth(n, s):
                project(QP[s % 2][:], n, slice(0, QW), [KC // 2])

            def q_sixth(n, s):
                project(QP[s % 2][:], n, slice(0, QW), [KC // 2 + 1])

            def q_last(n, s):
                project(QP[s % 2][:], n, slice(0, QW), range(KC - 2, KC)).then_inc(q_done, 1)

            def cumulate(n, s):
                pe.wait_ge(gate_ready, n + 1)
                from_one(pe, eG_done, n)
                from_one(pe, kt_copied, n)
                mm(KG[:, 0, :], cum[:], gate[:, s % 2, :], start=True, stop=True, skip_group_check=True).then_inc(G_done, 1)

            def scores(n, s):
                pe.wait_ge(qt_copied, 2 * (n + 1))
                pe.wait_ge(qt_low, n + 1)
                pe.wait_ge(kt_copied, n + 1)
                from_one(pe, s_read, n)
                for hp in range(H2):
                    for b in range(2):
                        keys = slice(b * POS, (b + 1) * POS)
                        rows = lambda t: t[:, b, 2 * hp:2 * hp + 2, :].rearrange("p h t -> p (h t)")
                        for i, (x, y) in enumerate(((0, 0), (0, 1), (1, 0))):
                            mm(SC[:, 0, 2 * hp + b, :], rows(QT[:, x]), KRT[:, y, keys], start=(i == 0), stop=(i == 2),
                               skip_group_check=True)
                        last = mm(SC[:, 1, 2 * hp + b, :], rows(ET), KDT[:, keys], start=True, stop=True, skip_group_check=True)
                last.then_inc(sc_done, 1)

            def p_transpose(n, s):
                pe.wait_ge(p_ready, n + 1)
                pe.wait_ge(kv_copied, n + 3 if not isinstance(n, int) else min(n + 3, STEPS))
                from_one(pe, pt_copied, n)
                for hp in range(H2):
                    last = nc.tensor.transpose(PTP[:, hp * P:(hp + 1) * P], PR[:, s % 2, 2 * hp:2 * hp + 2, :].rearrange("p b t -> p (b t)"), ident[:])
                last.then_inc(pt_done, 1)

            def values(n, s, b, done):
                keys = slice(b * POS, (b + 1) * POS)
                for i, (x, y) in enumerate(((0, 0), (0, 1), (1, 0))):
                    last = mm(OP[:, b].rearrange("p h t -> p (h t)"), Vs[keys, x, s, :], PT[keys, s % 2, y, :],
                              start=(i == 0), stop=(i == 2), skip_group_check=True)
                last.then_inc(done, 1)

            def v_first(n, s):
                pe.wait_ge(pt_copied, n + 1)
                pe.wait_ge(v_low, n + 1)
                from_one(pe, o_copied, n)
                values(n, s, 0, o_half)

            def v_second(n, s):
                pe.wait_ge(o_half, n + 1)
                values(n, s, 1, o_done)

            pe.wait_ge(consts_in, 64)
            steps(pe, [("kv", 0), ("v1", 3), ("qa", 0), ("t", 1), ("q5", 0), ("G", 0), ("q6", 0), ("pt", 2), ("qc", 0), ("s", 1), ("v0", 2)], None,
                  {"kv": kv, "qa": q_first, "G": cumulate, "q5": q_fifth, "q6": q_sixth, "qc": q_last, "t": transposes, "s": scores,
                   "pt": p_transpose, "v0": v_first, "v1": v_second})

        @block.scalar
        def _(act):
            a = nc.scalar.activation

            def q_exp(n, s):
                p = s % 2
                act.wait_ge(q_done, n + 1)
                act.wait_ge(qmax_ready, n + 1)
                from_one(act, q_decayed, n - 1)
                for h in range(GRP):
                    last = a(E[:, p, h, :], QP[p][:, h * DH:(h + 1) * DH], ACT.Exp, bias=qnb[:, p, h:h + 1], scale=1.0 / WS,
                             accum_out=qsum[:, p, h:h + 1])
                last.then_inc(qexp_done, 1)

            def s_exp(n, s):
                p = s % 2
                act.wait_ge(smax_ready, n + 1)
                from_one(act, p_ready, n - 1)
                for j in range(4):
                    last = a(Es[:, p, j, :], S2[:, p, j, :], ACT.Exp, bias=snb[:, p, j:j + 1], scale=SCORE, accum_out=ssum[:, p, j:j + 1])
                last.then_inc(sexp_done, 1)

            def kv_copy(n, s):
                p = s % 2
                act.wait_ge(kv_done, n + 1)
                if not isinstance(n, int) or n >= 2:
                    act.wait_ge(k_roped, n - 1)
                    act.wait_ge(gate_ready, n - 1)
                    act.wait_ge(v_low, n - 1)
                a(KV[:, p, :], KVP[:, 0:KVW], ACT.Copy, scale=1.0 / WS).then_inc(kv_copied, 1)

            def gates(n, s):
                p = s % 2
                act.wait_ge(kv_copied, n + 1)
                a(kabs[:, p, :], K[:, p, :], ACT.Abs).then_inc(kabs_done, 1)
                if not isinstance(n, int) or n >= 4:
                    act.wait_ge(o_done, n - 3)
                a(Vs[:, 0, s, :], V[:, p, :], ACT.Copy, scale=VS).then_inc(v_high, 1)
                act.wait_ge(kabs_done, n + 1)
                a(kexp[:, p, :], kabs[:, p, :], ACT.Exp, scale=-1.0).then_inc(knegexp_done, 1)
                act.wait_ge(knegexp_done, n + 1)
                a(kln[:, p, :], kexp[:, p, :], ACT.Ln, bias=1.0).then_inc(kln_done, 1)
                act.wait_ge(kmax_ready, n + 1)
                from_one(act, k_decayed, n - 1)
                a(Ek[:, p, :], K[:, p, :], ACT.Exp, bias=knb[:, p, :], accum_out=ksum[:, p, :]).then_inc(kexp_done, 1)

            def t_copy(n, s):
                act.wait_ge(t_done, n + 1)
                from_one(act, sc_done, n)
                for src, dst in ((TQ, QT[:, 0]), (TE, ET[:])):
                    a(dst.rearrange("p b h t -> p h b t"), src[:].rearrange("p h (b t) -> p h b t", b=2), ACT.Copy).then_inc(qt_copied, 1)

            def decays(n, s):
                p = s % 2
                act.wait_ge(G_done, n + 1)
                if not isinstance(n, int) or n >= 2:
                    act.wait_ge(q_decayed, n - 1)
                    act.wait_ge(k_decayed, n - 1)
                a(eG[:, p, :], KG[:, 0, :], ACT.Exp)
                a(eGn[:, p, :], KG[:, 0, :], ACT.Exp, scale=-1.0).then_inc(eG_done, 1)

            def o_copy(n, s):
                act.wait_ge(o_done, n + 1)
                if not isinstance(n, int) or n >= 2:
                    act.wait_ge(o_out[s % 2], turns(n - 2, s % 2, 16))
                a(OT[:, s % 2].rearrange("p h b t -> p b h t"), OP[:], ACT.Copy, scale=0.5 / (VS * PS)).then_inc(o_copied, 1)

            def pt_copy(n, s):
                act.wait_ge(pt_done, n + 1)
                from_one(act, o_done, n - 1)
                a(PT[:, s % 2, 0, :], PTP, ACT.Copy, scale=PS).then_inc(pt_high, 1)

            def w_piece(u, i, more):
                if i < 2 and more:
                    act.wait_ge(w_in[i], 3 * 16 * (u + 1))
                    g, c = u // 4 + 1, (u % 4) * 2 + i
                    a(Wg[:, ds((g + 1) % 2, 1), 0, ds(c, 1), :].rearrange("p a b n -> p (a b n)"), wst[:, i, :], ACT.Copy,
                      scale=WS).then_inc(w_high, 1)
                if i == 2:
                    act.wait_ge(wo_in, 16 * (u + 1))
                    from_one(act, wo_out, 32 * u)
                    a(oh[:], ost[:], ACT.Copy, scale=WS).then_inc(wo_high, 1)

            act.preload_act_table_set("natural_log_exp_and_others")
            steps(act, [("qe", 1), ("se", 2), ("kvc", 0), ("g", 0), ("o", 3), ("tc", 1), ("d", 0), ("ph", 2), ("w", 0)], w_piece,
                  {"ph": pt_copy, "kvc": kv_copy, "g": gates, "d": decays, "qe": q_exp, "tc": t_copy, "se": s_exp, "o": o_copy})

        @block.vector
        def _(dve):
            v = nc.vector

            def rope_tab(i, dims):
                t = rope[:, i, :]
                for _ in range(len(dims) - 2):
                    t = t.unsqueeze(1)
                return t.broadcast_to(dims)

            def q_max(n, s):
                p = s % 2
                dve.wait_ge(q_done, n + 1)
                from_one(dve, qexp_done, n - 1)
                v.tensor_reduce(qmx[:, p, :], QP[p][:].rearrange("p (h d) -> p h d", h=GRP), X, ALU.max).then_inc(qmax_raw, 1)
                dve.wait_ge(qmax_raw, n + 1)
                v.tensor_scalar(qnb[:, p, :], qmx[:, p, :], -1.0 / WS, None, ALU.mult).then_inc(qmax_ready, 1)

            def q_rope(n, s):
                p = s % 2
                q4 = QP[p][:].rearrange("p (h x d) -> p h x d", h=GRP, x=2)
                dve.wait_ge(qexp_done, n + 1)
                from_one(dve, q_roped, n)
                v.tensor_tensor(t1[:], q4, rope_tab(3, [P, GRP, 2, DH // 2]), ALU.mult)
                v.tensor_tensor(t2[:, :, 0, :], q4[:, :, 1, :], rope_tab(5, [P, GRP, DH // 2]), ALU.mult)
                v.tensor_tensor(t2[:, :, 1, :], q4[:, :, 0, :], rope_tab(4, [P, GRP, DH // 2]), ALU.mult).then_inc(q_read, 1)
                dve.wait_ge(q_read, n + 1)
                from_one(dve, t_done, n - 1)
                v.tensor_tensor(QR[:, p].rearrange("p h d -> p (h d)"), t1[:].rearrange("p h x d -> p (h x d)"),
                                t2[:].rearrange("p h x d -> p (h x d)"), ALU.add).then_inc(q_roped, 1)

            def q_decay(n, s):
                p = s % 2
                dve.wait_ge(qexp_done, n + 1)
                dve.wait_ge(eG_done, n + 1)
                v.reciprocal(qrs[:, p, :], qsum[:, p, :]).then_inc(qrs_ready, 1)
                dve.wait_ge(qrs_ready, n + 1)
                for h in range(GRP):
                    last = v.scalar_tensor_tensor(QD[:, p, h, :], E[:, p, h, :], qrs[:, p, h:h + 1], eG[:, p, :], ALU.mult, ALU.mult)
                last.then_inc(q_decayed, 1)

            def s_soft(n, s):
                p = s % 2
                dve.wait_ge(sc_done, n + 1)
                from_one(dve, sexp_done, n - 1)
                mk = lambda i: masks[:, i, :].unsqueeze(1).broadcast_to([P, 4, POS])
                v.tensor_tensor(S2[:, p], SC[:, 0], mk(0), ALU.add)
                v.scalar_tensor_tensor(L[:, p], SC[:, 1], BIG, mk(1), ALU.min, ALU.mult).then_inc(s_read, 1)
                dve.wait_ge(s_read, n + 1)
                v.tensor_reduce(smx[:, p, :], S2[:, p], X, ALU.max).then_inc(smax_raw, 1)
                dve.wait_ge(smax_raw, n + 1)
                v.tensor_scalar(snb[:, p, :], smx[:, p, :], -SCORE, None, ALU.mult).then_inc(smax_ready, 1)

            def s_prob(n, s):
                p = s % 2
                dve.wait_ge(sexp_done, n + 1)
                v.reciprocal(srs[:, p, :], ssum[:, p, :]).then_inc(srs_ready, 1)
                dve.wait_ge(srs_ready, n + 1)
                from_one(dve, pt_done, n - 1)
                for j in range(4):
                    last = v.scalar_tensor_tensor(PR[:, p, j, :], Es[:, p, j, :], srs[:, p, j:j + 1], L[:, p, j, :], ALU.mult, ALU.add)
                last.then_inc(p_ready, 1)

            def k_rope(n, s):
                p = s % 2
                dve.wait_ge(kv_copied, n + 1)
                from_one(dve, kexp_done, n - 1)
                v.tensor_reduce(kmx[:, p, :], K[:, p, :], X, ALU.max).then_inc(kmax_raw, 1)
                k3 = K[:, p, :].rearrange("p (x d) -> p x d", x=2)
                from_one(dve, k_roped, n)
                v.tensor_tensor(kt1[:], k3, rope_tab(0, [P, 2, DH // 2]), ALU.mult)
                dve.wait_ge(kmax_raw, n + 1)
                v.tensor_scalar(knb[:, p, :], kmx[:, p, :], -1.0, None, ALU.mult).then_inc(kmax_ready, 1)
                v.tensor_tensor(kt2[:, 0, :], k3[:, 1, :], rope[:, 2, :], ALU.mult)
                v.tensor_tensor(kt2[:, 1, :], k3[:, 0, :], rope[:, 1, :], ALU.mult).then_inc(k_terms, 1)
                dve.wait_ge(k_terms, n + 1)
                from_one(dve, t_done, n - 1)
                v.tensor_tensor(KR[:, p, :], kt1[:].rearrange("p x d -> p (x d)"), kt2[:].rearrange("p x d -> p (x d)"),
                                ALU.add).then_inc(k_roped, 1)
                dve.wait_ge(v_high, n + 1)
                v.scalar_tensor_tensor(Vs[:, 1, s, :], V[:, p, :], VS, Vs[:, 0, s, :], ALU.mult, ALU.subtract).then_inc(v_low, 1)
                dve.wait_ge(kln_done, n + 1)
                from_one(dve, G_done, n - 1)
                v.scalar_tensor_tensor(gate[:, p, :], K[:, p, :], 0.0, kln[:, p, :], ALU.min, ALU.subtract).then_inc(gate_ready, 1)

            def k_tcopy(n, s):
                dve.wait_ge(kt_done, n + 1)
                from_one(dve, sc_done, n)
                v.tensor_copy(KRT[:, 0, :], KG[:, 1, :]).then_inc(kt_high, 1)
                v.tensor_copy(KDT[:], KG[:, 2, :])
                dve.wait_ge(kt_high, n + 1)
                v.tensor_tensor(KRT[:, 1, :], KG[:, 1, :], KRT[:, 0, :], ALU.subtract).then_inc(kt_copied, 1)

            def q_tlow(n, s):
                dve.wait_ge(qt_copied, 2 * n + 1)
                v.tensor_tensor(QT[:, 1].rearrange("p b h t -> p h b t"), TQ[:].rearrange("p h (b t) -> p h b t", b=2),
                                QT[:, 0].rearrange("p b h t -> p h b t"), ALU.subtract).then_inc(qt_low, 1)

            def k_decay(n, s):
                p = s % 2
                dve.wait_ge(kexp_done, n + 1)
                dve.wait_ge(eG_done, n + 1)
                v.reciprocal(krs[:, p, :], ksum[:, p, :]).then_inc(krs_ready, 1)
                dve.wait_ge(krs_ready, n + 1)
                from_one(dve, t_done, n - 1)
                v.scalar_tensor_tensor(KD[:, p, :], Ek[:, p, :], krs[:, p, :], eGn[:, p, :], ALU.mult, ALU.mult).then_inc(k_decayed, 1)

            def pt_copy(n, s):
                dve.wait_ge(pt_high, n + 1)
                v.scalar_tensor_tensor(PT[:, s % 2, 1, :], PTP, PS, PT[:, s % 2, 0, :], ALU.mult, ALU.subtract).then_inc(pt_copied, 1)

            def w_piece(u, i, more):
                if 1 <= i < 3 and more:
                    dve.wait_ge(w_high, 2 * u + i)
                    g, c = u // 4 + 1, (u % 4) * 2 + i - 1
                    hi, lo = (Wg[:, ds((g + 1) % 2, 1), x, ds(c, 1), :].rearrange("p a b n -> p (a b n)") for x in range(2))
                    v.scalar_tensor_tensor(lo, wst[:, i - 1, :], WS, hi, ALU.mult, ALU.subtract).then_inc(w_ready, 1)
                if i == 3:
                    dve.wait_ge(wo_high, u + 1)
                    v.scalar_tensor_tensor(ol[:], ost[:], WS, oh[:], ALU.mult, ALU.subtract).then_inc(wo_ready, 1)

            dve.wait_ge(consts_in, 64)
            steps(dve, [("qm", 1), ("ss", 2), ("qr", 1), ("qd", 1), ("kr", 0), ("ktc", 1), ("sp", 2), ("qtl", 1), ("kd", 0), ("ptc", 2), ("w", 0)], w_piece,
                  {"kr": k_rope, "kd": k_decay, "qm": q_max, "qr": q_rope, "qd": q_decay, "ktc": k_tcopy, "qtl": q_tlow, "ss": s_soft,
                   "sp": s_prob, "ptc": pt_copy})


def load_o(eng, oT, o_in, ot_dram, t, par):
    ov = ot_dram.rearrange("t d g m -> t d (g m)").rearrange("t d (x m) -> t d x m", x=2)
    for x in range(2):
        eng.dma_start(oT[:, 2 * par + x].rearrange("p h n -> p (h n)"),
                      ov[ds(t, 1), :, x, :].rearrange("o d m -> (o d) m")).then_inc(o_in[2 * par + x], 16)


def output_phase(nc, WoS, oT, o_in, h_dram, ot_dram, wo_dram, bt_dram, ag_dram, lb_dram, base_b, k_ident, k_before, out):
    with ExitStack() as ctx:
        sb = lambda name, shape, dt=F32: ctx.enter_context(nc.sbuf_tensor(name, shape, dt))
        pb = lambda name, shape, dt=F32: ctx.enter_context(nc.psum_tensor(name, shape, dt))
        sem = lambda name: ctx.enter_context(nc.semaphore(name))
        HALF = HID // 2
        ident, before, eps = sb("o_ident", [P, P]), sb("o_before", [P, NE, NE]), sb("o_eps", [P, 1])
        carry = sb("o_carry", [P, 1])
        BT = sb("o_BT", [P, 2, KC, HID], F16)
        AG = sb("o_AG", [P, 2, KC, AGW], F16)
        LB = sb("o_LB", [P, 2, HID], F16)
        bias = sb("o_bias", [P, HID])
        ht = sb("o_ht", [P, 2, HID])
        xn = sb("o_xn", [P, HID])
        x2h, x2l = sb("o_x2h", [P, KC, P], F16), sb("o_x2l", [P, KC, P], F16)
        st, mv, sd, rs = sb("o_st", [P, 2, 6]), sb("o_mv", [P, 2]), sb("o_sd", [P, 1]), sb("o_rs", [P, 1])
        lg, top, ntop = sb("o_lg", [P, NE]), sb("o_top", [P, 1]), sb("o_ntop", [P, 1])
        gt_, eq_ = sb("o_gt", [P, NE, NE]), sb("o_eq", [P, NE, NE])
        rank, sel, ew, wsum, wr, wf = (sb("o_" + x, [P, n]) for x, n in (("rank", NE), ("sel", NE), ("ew", NE), ("wsum", 1), ("wr", 1), ("wf", NE)))
        lw = sb("o_lw", [P, NE, RANK])
        lwh, lwl = sb("o_lwh", [P, P], F16), sb("o_lwl", [P, P], F16)
        Y = [pb(f"o_Y{i}", [P, HALF]) for i in range(2)]
        XT = [pb(f"o_XT{i}", [P, 4, P]) for i in range(2)]
        F = [pb(f"o_F{i}", [P, HALF]) for i in range(2)]
        LG, LWT = pb("o_LG", [P, 512]), pb("o_LWT", [P, 512])

        consts_in, ffn_in = sem("o_consts_in"), sem("o_ffn_in")
        h_in, out_done = ([sem(f"o_{x}{i}") for i in range(2)] for x in ("h_in", "out_done"))
        wo_in = [sem(f"o_wo_in{i}") for i in range(KEPT, PARTS)]
        o_used, h2_ready, stats, var_ready, sd_ready, rs_ready, xn_ready, x_t, x_hi, x_lo = (sem("o_" + x) for x in
            ("o_used", "h2_ready", "stats", "var_ready", "sd_ready", "rs_ready", "xn_ready", "x_t", "x_hi", "x_lo"))
        lg_done, link, ew_ready, lw_ready, lw_t, lw_hi, lw_lo, f_done, hb_ready, fin_ready, top_ready = (sem("o_" + x) for x in
            ("lg_done", "link", "ew_ready", "lw_ready", "lw_t", "lw_hi", "lw_lo", "f_done", "hb_ready", "fin_ready", "top_ready"))
        link2 = sem("o_link2")
        block = ctx.enter_context(nc.Block())

        def steps(order, fns):
            def step(t, par):
                for name, lag in order:
                    if not isinstance(t, int) or 0 <= t - lag < TILES:
                        fns[name](t - lag, (par + lag) % 2)
            return step

        def run(eng, order, fns):
            step = steps(order, fns)
            for name, lag in order:
                if name not in ("ya", "yb", "r"):
                    fns[name](1 - lag, (1 + lag) % 2)
            with eng.Fori(1, TILES // 2) as half:
                step(half * 2, 0)
                step(half * 2 + 1, 1)
            step(TILES, 0)

        @block.sync
        def _(sp):
            hv = h_dram.rearrange("(t p) n -> t p n", p=P)

            def load(t, par):
                if not isinstance(t, int) or t >= 2:
                    sp.wait_ge(o_used, t - 1)
                    load_o(sp, oT, o_in, ot_dram, t, par)
                if not isinstance(t, int) or t >= 2:
                    sp.wait_ge(out_done[par], turns(t - 2, par, 16))
                sp.dma_start(ht[:, par, :], hv[ds(t, 1)].rearrange("o p n -> (o p) n")).then_inc(h_in[par], 16)
            load(0, 0)
            load(1, 1)
            for part in range(KEPT, PARTS):
                for x in range(2):
                    sp.dma_start(WoS[part][:, x], wo_dram[x, :, part * PART:(part + 1) * PART, :]).then_inc(wo_in[part - KEPT], 16)
            for x in range(2):
                sp.dma_start(BT[:, x], bt_dram[x]).then_inc(ffn_in, 16)
            sp.dma_start(AG[:].rearrange("p x k n -> p x (k n)"), ag_dram.rearrange("x p k n -> p x (k n)")).then_inc(ffn_in, 16)
            sp.dma_start(LB[:], lb_dram.rearrange("x p n -> p x n")).then_inc(ffn_in, 16)
            with sp.Fori(1, TILES // 2) as half:
                load(half * 2, 0)
                load(half * 2 + 1, 1)

        @block.tensor
        def _(pe):
            mm = nc.tensor.matmul

            def products(out, par, k):
                for i in range(2):
                    for y in range(2):
                        last = mm(out[y][:], oT[:, 2 * par + k // (HEADS // 2), k % (HEADS // 2), :],
                                  WoS[k // PART][:, i, k % PART, y * HALF:(y + 1) * HALF],
                                  start=(k == 0 and i == 0), stop=(k == HEADS - 1 and i == 1))
                return last

            def project(t, par, x):
                pe.wait_ge(o_in[2 * par + x], turns(t, par, 16))
                if x == 0:
                    pe.wait_ge(h2_ready, t)
                for h in range(HEADS // 2):
                    last = products(Y, par, x * HEADS // 2 + h)
                if x == 1:
                    last.then_inc(o_used, 1)

            def x_transpose(t, par):
                pe.wait_ge(xn_ready, t + 1)
                from_one(pe, x_lo, t)
                for c in range(KC):
                    last = nc.tensor.transpose(XT[c // 4][:, c % 4, :], xn[:, c * P:(c + 1) * P], ident[:])
                last.then_inc(x_t, 1)

            def gates(t, par):
                if isinstance(t, int) and t == 0:
                    pe.wait_ge(ffn_in, 16 * 4)
                pe.wait_ge(x_lo, t + 1)
                from_one(pe, lw_ready, t)
                for c in range(KC):
                    mm(LG[:, 0:AGW], x2h[:, c, :], AG[:, 0, c, :], start=(c == 0), stop=False)
                    mm(LG[:, 0:AGW], x2h[:, c, :], AG[:, 1, c, :], start=False, stop=False)
                    last = mm(LG[:, 0:AGW], x2l[:, c, :], AG[:, 0, c, :], start=False, stop=(c == KC - 1))
                last.then_inc(lg_done, 1)

            def base(t, par):
                from_one(pe, fin_ready, t)
                if isinstance(t, int) and t == 0:
                    pe.wait_ge(h2_ready, 2)
                for y in range(2):
                    cols = slice(y * HALF, (y + 1) * HALF)
                    for c in range(KC):
                        mm(F[y][:], x2h[:, c, :], BT[:, 0, c, cols], start=(c == 0), stop=False)
                        mm(F[y][:], x2h[:, c, :], BT[:, 1, c, cols], start=False, stop=False)
                        mm(F[y][:], x2l[:, c, :], BT[:, 0, c, cols], start=False, stop=False)
                    if y == 0:
                        pe.wait_ge(lw_ready, t + 1)
                        from_one(pe, lw_lo, t)
                        nc.tensor.transpose(LWT[:, 0:P], lw[:].rearrange("p e r -> p (e r)"), ident[:]).then_inc(lw_t, 1)
                pe.wait_ge(lw_lo, t + 1)
                for y in range(2):
                    cols = slice(y * HALF, (y + 1) * HALF)
                    mm(F[y][:], lwh[:], LB[:, 0, cols], start=False, stop=False)
                    mm(F[y][:], lwh[:], LB[:, 1, cols], start=False, stop=False)
                    last = mm(F[y][:], lwl[:], LB[:, 0, cols], start=False, stop=True)
                last.then_inc(f_done, 1)

            for i in range(4):
                pe.wait_ge(o_in[i], 16)
            for part in range(PARTS):
                if part >= KEPT:
                    pe.wait_ge(wo_in[part - KEPT], 32)
                for par, to in enumerate((Y, F)):
                    for k in range(part * PART, (part + 1) * PART):
                        last = products(to, par, k)
                    if part == PARTS - 1:
                        last.then_inc(o_used, 1)
            pe.wait_ge(consts_in, 48)
            run(pe, [("ya", 0), ("xt", 1), ("yb", 0), ("g", 1), ("f", 1)],
                {"ya": lambda t, p: project(t, p, 0), "yb": lambda t, p: project(t, p, 1), "xt": x_transpose, "g": gates, "f": base})

        @block.scalar
        def _(act):
            act.dma_start(ident[:], k_ident).then_inc(consts_in, 16)
            act.dma_start(before[:].rearrange("p a b -> p (a b)"), k_before).then_inc(consts_in, 16)
            act.dma_start(bias[:], base_b.rearrange("(a n) -> a n", a=1).broadcast_to([P, HID])).then_inc(consts_in, 16)
            a = nc.scalar.activation

            def root(t, par):
                act.wait_ge(var_ready, t + 1)
                a(sd[:], mv[:, 1:2], ACT.Sqrt, bias=eps[:]).then_inc(sd_ready, 1)

            def high(t, par):
                act.wait_ge(x_t, t + 1)
                from_one(act, f_done, t)
                for i in range(2):
                    last = a(x2h[:, 4 * i:4 * i + 4, :], XT[i][:], ACT.Copy)
                last.then_inc(x_hi, 1)

            def weigh(t, par):
                act.wait_ge(top_ready, t + 1)
                a(ew[:], lg[:], ACT.Exp, bias=ntop[:]).then_inc(ew_ready, 1)

            def lw_high(t, par):
                act.wait_ge(lw_t, t + 1)
                from_one(act, f_done, t)
                a(lwh[:], LWT[:, 0:P], ACT.Copy).then_inc(lw_hi, 1)

            def store(t, par):
                act.wait_ge(fin_ready, t + 1)
                act.dma_start(out.rearrange("(t p) n -> t p n", p=P)[ds(t, 1)].rearrange("o p n -> (o p) n"),
                              ht[:, par, :]).then_inc(out_done[par], 16)
            root(0, 0)
            root(1, 1)
            run(act, [("h", 1), ("r", 0), ("w", 1), ("l", 1), ("s", 1)],
                {"r": root, "h": high, "w": weigh, "l": lw_high, "s": store})
            for s in out_done:
                act.wait_ge(s, 16 * TILES // 2)

        @block.vector
        def _(dve):
            v = nc.vector
            NL = 6

            def residual(t, par, Y=Y):
                dve.wait_ge(o_used, t + 1)
                dve.wait_ge(h_in[par], turns(t, par, 16))
                for y in range(2):
                    hs = ht[:, par, y * HALF:(y + 1) * HALF]
                    last = v.scalar_tensor_tensor(hs, Y[y][:], 1.0 / WS, hs, ALU.mult, ALU.add)
                last.then_inc(h2_ready, 1)
                dve.wait_ge(h2_ready, t + 1)
                for y in range(2):
                    last = v.bn_stats(st[:, y, :], ht[:, par, y * HALF:(y + 1) * HALF])
                last.then_inc(stats, 1)
                dve.wait_ge(stats, t + 1)
                v.memset(carry[:], 0.0)
                v.bn_aggr(mv[:], st[:]).then_inc(var_ready, 1)

            def normalise(t, par):
                dve.wait_ge(sd_ready, t + 1)
                v.reciprocal(rs[:], sd[:]).then_inc(rs_ready, 1)
                dve.wait_ge(rs_ready, t + 1)
                dve.wait_ge(var_ready, t + 1)
                from_one(dve, x_t, t)
                v.tensor_scalar(xn[:], ht[:, par, :], mv[:, 0:1], rs[:], ALU.subtract, ALU.mult).then_inc(xn_ready, 1)
                dve.wait_ge(xn_ready, t + 1)
                v.tensor_tensor(ht[:, par, :], ht[:, par, :], bias[:], ALU.add).then_inc(hb_ready, 1)

            def low(t, par):
                dve.wait_ge(x_hi, t + 1)
                for i in range(2):
                    last = v.tensor_tensor(x2l[:, 4 * i:4 * i + 4, :], XT[i][:], x2h[:, 4 * i:4 * i + 4, :], ALU.subtract)
                last.then_inc(x_lo, 1)

            def gating(t, par):
                dve.wait_ge(lg_done, t + 1)
                b = NL * t

                def step(i, ins):
                    ins.then_inc(link, 1)
                    dve.wait_ge(link, b + i)
                step(1, v.tensor_scalar(lg[:], LG[:, ER:AGW], 1.0 / WS, None, ALU.mult))
                v.tensor_reduce(top[:], lg[:], X, ALU.max)
                me = lg[:].unsqueeze(2).broadcast_to([P, NE, NE])
                other = lg[:].unsqueeze(1).broadcast_to([P, NE, NE])
                v.tensor_tensor(gt_[:], other, me, ALU.is_gt)
                step(2, v.tensor_tensor(eq_[:], other, me, ALU.is_equal))
                v.tensor_scalar(ntop[:], top[:], -1.0, None, ALU.mult).then_inc(top_ready, 1)
                step(3, v.tensor_tensor(eq_[:], eq_[:], before[:], ALU.mult))
                step(4, v.tensor_tensor(gt_[:], gt_[:], eq_[:], ALU.add))
                step(5, v.tensor_reduce(rank[:], gt_[:], X, ALU.add))
                step(6, v.tensor_scalar(sel[:], rank[:], 1.5, None, ALU.is_lt))

            def weights(t, par):
                dve.wait_ge(ew_ready, t + 1)
                b = 4 * t

                def step(i, ins):
                    ins.then_inc(link2, 1)
                    dve.wait_ge(link2, b + i)
                step(1, v.tensor_tensor(ew[:], ew[:], sel[:], ALU.mult))
                step(2, v.tensor_reduce(wsum[:], ew[:], X, ALU.add))
                step(3, v.reciprocal(wr[:], wsum[:]))
                step(4, v.tensor_scalar(wf[:], ew[:], wr[:], LORA_SCALE / WS, ALU.mult, ALU.mult))
                from_one(dve, lw_t, t)
                v.tensor_tensor(lw[:], LG[:, 0:ER].rearrange("p (e r) -> p e r", e=NE), wf[:].unsqueeze(2).broadcast_to([P, NE, RANK]),
                                ALU.mult).then_inc(lw_ready, 1)

            def lw_low(t, par):
                dve.wait_ge(lw_hi, t + 1)
                v.tensor_tensor(lwl[:], LWT[:, 0:P], lwh[:], ALU.subtract).then_inc(lw_lo, 1)

            def finish(t, par):
                dve.wait_ge(f_done, t + 1)
                dve.wait_ge(hb_ready, t + 1)
                for y in range(2):
                    hs = ht[:, par, y * HALF:(y + 1) * HALF]
                    last = v.scalar_tensor_tensor(hs, F[y][:], 1.0 / WS, hs, ALU.mult, ALU.add)
                last.then_inc(fin_ready, 1)

            v.memset(eps[:], EPS)
            dve.wait_ge(consts_in, 48)
            residual(0, 0)
            normalise(0, 0)
            residual(1, 1, F)
            run(dve, [("lo", 1), ("r", 0), ("g", 1), ("w", 1), ("ll", 1), ("n", 0), ("f", 1)],
                {"r": residual, "n": normalise, "lo": low, "g": gating, "w": weights, "ll": lw_low, "f": finish})


def block_kernel(nc, x, abslog, phase, Wq, Wk, Wv, Wo, gate_w, base_w, base_b, lora_A, lora_B,
                 k_ident, k_minus, k_rope, k_masks, k_cum, k_mult, k_before, out):
    scratch = lambda name, shape, dt: nc.dram_tensor(name, shape, dt).ap()
    h_dram = scratch("h_dram", (TOK, HID), F32)
    ot_dram = scratch("ot_dram", (TILES, P, KVH, GRP * P), BF16)
    wo_dram = scratch("wo_dram", (2, P, HEADS, HID), F16)
    bt_dram = scratch("bt_dram", (2, P, KC, HID), F16)
    ag_dram = scratch("ag_dram", (2, P, KC, AGW), F16)
    lb_dram = scratch("lb_dram", (2, P, HID), F16)
    part, nx, ng = 2 * PART * HID, KC * TOK, 2 * KC * GW
    with nc.sbuf_tensor("arena", [P, PARTS * part], F16) as arena, nc.semaphore("w0_in") as w0_in, \
            nc.semaphore("w_ready") as w_ready:
        assert 2 * nx == 4 * part and 2 * ng == 3 * part and KEPT == 2
        halves = arena[:].rearrange("p (g n) -> p g n", g=2)
        Wg = halves[:, :, 0:ng].rearrange("p g (x k n) -> p g x k n", x=2, k=KC)
        xh, xl = (halves[:, i, 2 * part:4 * part].rearrange("p (k n) -> p k n", k=KC) for i in range(2))
        w0 = halves[:, 0, 0:ng].bitcast(F32).rearrange("p (k n) -> p k n", k=KC)
        wst = halves[:, 0, ng:ng + 4 * GW].bitcast(F32).rearrange("p (i n) -> p i n", i=2)
        WoS = [arena[:, i * part:(i + 1) * part].rearrange("p (x h n) -> p x h n", x=2, h=PART) for i in (4, 5, 0, 1, 2, 3, 6, 7)]
        tokens_phase(nc, x, abslog, phase, base_w, gate_w, lora_A, lora_B, k_ident, k_minus, k_mult, Wq, Wk, Wv,
                     arena[:, ng:].bitcast(F32), w0, w0_in, h_dram, bt_dram, ag_dram, lb_dram)
        norm_phase(nc, xh, xl, Wg, w0, w0_in, w_ready, h_dram, k_ident, k_minus)
        with ExitStack() as ctx:
            oT = ctx.enter_context(nc.sbuf_tensor("oT", [P, 4, HEADS // 2, P], BF16))
            o_in = [ctx.enter_context(nc.semaphore(f"o_in{i}")) for i in range(4)]
            attention_phase(nc, xh, xl, Wg, wst, w_ready, WoS, oT, o_in, Wq, Wk, Wv, Wo, k_ident, k_rope, k_masks, k_cum,
                            ot_dram, wo_dram)
            output_phase(nc, WoS, oT, o_in, h_dram, ot_dram, wo_dram, bt_dram, ag_dram, lb_dram, base_b, k_ident, k_before,
                         out.rearrange("b n d -> (b n) d"))


_INS = ['x', 'L0_tok_A_abslog', 'L0_tok_A_phase', 'L0_attn_Wq', 'L0_attn_Wk', 'L0_attn_Wv', 'L0_attn_Wo',
        'L0_ffn_gate_w', 'L0_ffn_base_w', 'L0_ffn_base_b', 'L0_ffn_lora_A', 'L0_ffn_lora_B']


def kernel(**inputs):
    import numpy as _np
    import concourse.bacc as _bacc
    from concourse import mybir as _mybir
    from concourse.bass_utils import run_bass_kernel_spmd as _run

    nc = _bacc.Bacc("TRN2", target_bir_lowering=False, num_devices=1)
    arrays, args = {}, []
    for name, a in [(n, inputs[n]) for n in _INS] + list(constants().items()):
        a = _np.ascontiguousarray(a)
        arrays[f"in_{name}_dram"] = a
        args.append(nc.dram_tensor(f"in_{name}_dram", a.shape, _mybir.dt.from_np(a.dtype), kind="ExternalInput").ap())
    args.append(nc.dram_tensor("out_0_dram", (BATCH, POS, HID), _mybir.dt.float32, kind="ExternalOutput").ap())
    block_kernel(nc, *args)
    r = _run(nc, [arrays], core_ids=[0])
    return r.results[0]["out_0_dram"]
```
